# Optimizing a Trainium2 kernel written in Bass

```python
import numpy as np
import jax
import jax.numpy as jnp

def _softmax(x, axis=-1):
    return jax.nn.softmax(x, axis=axis)

def _gelu(x):
    return jax.nn.gelu(x, approximate=True)

def _silu(x):
    return jax.nn.silu(x)

def _sigmoid(x):
    return jax.nn.sigmoid(x)

def _layernorm(x, axis=-1, eps=1e-05):
    m = jnp.mean(x, axis=axis, keepdims=True)
    v = jnp.var(x, axis=axis, keepdims=True)
    return (x - m) / jnp.sqrt(v + eps)

def _scatter_add(tgt, idx, src, axis=0):
    return tgt.at[idx].add(src)

def _segment_sum(src, seg, n):
    return jax.ops.segment_sum(src, seg, n)
kernel_name = 'mk_seq_postln_d1_jaxref_r8_63c4c4'

def setup_inputs(seed: int=0):
    np.random.seed(seed)
    _w = jnp.asarray

    def _L0_attn_setup():
        import jax, jax.numpy as jnp
        import numpy as np
        N_EMBD = 128
        N_HEAD = 16
        HEAD_DIM = N_EMBD // N_HEAD
        KV_RANK = 32
        Q_RANK = 64
        ROPE_DIM = 32
        B, T = (2, 256)
        EPS = 1e-06

        def _rope_tables(T, dim):
            inv_freq = 1.0 / 10000.0 ** (np.arange(0, dim, 2, dtype=np.float32) / dim)
            t = np.arange(T, dtype=np.float32)
            freqs = np.outer(t, inv_freq)
            emb = np.concatenate([freqs, freqs], -1)
            return (jnp.asarray(np.cos(emb)), jnp.asarray(np.sin(emb)))

        def _apply_rope(x, cos, sin):
            d2 = x.shape[-1] // 2
            x1, x2 = (x[..., :d2], x[..., d2:])
            rot = jnp.concatenate([-x2, x1], axis=-1)
            return x * cos[None, None, :, :] + rot * sin[None, None, :, :]
        key = jax.random.key(seed)
        ks = jax.random.split(key, 10)

        def w(k, fan_in, fan_out):
            return jax.random.normal(k, (fan_in, fan_out), dtype=jnp.float32) * fan_in ** (-0.5)
        return {'x': jax.random.normal(ks[0], (B, T, N_EMBD), dtype=jnp.float32), 'W_kv': w(ks[1], N_EMBD, KV_RANK), 'g_kv': jnp.ones((KV_RANK,), dtype=jnp.float32), 'W_kdec': w(ks[2], KV_RANK, N_HEAD * HEAD_DIM), 'W_vdec': w(ks[3], KV_RANK, N_HEAD * HEAD_DIM), 'W_q': w(ks[4], N_EMBD, Q_RANK), 'W_qdec': w(ks[5], Q_RANK, N_HEAD * HEAD_DIM), 'W_krope': w(ks[6], N_EMBD, N_HEAD * ROPE_DIM), 'W_qrope': w(ks[7], Q_RANK, N_HEAD * ROPE_DIM), 'W_o': w(ks[8], N_HEAD * HEAD_DIM, N_EMBD)}
    _L0_attn_in = _L0_attn_setup()

    def _L0_ffn_setup():
        import jax, jax.numpy as jnp
        import numpy as np
        EMBED_DIM = 128
        HIDDEN_DIM = 512
        NUM_EXPERTS = 8
        TOP_K = 2
        key = jax.random.key(seed)
        k_x, k_g, k_w1, k_w2 = jax.random.split(key, 4)
        x = jax.random.normal(k_x, (2, 64, EMBED_DIM), dtype=jnp.float32)
        gate_w = jax.random.normal(k_g, (NUM_EXPERTS, EMBED_DIM), dtype=jnp.float32) * (1.0 / np.sqrt(EMBED_DIM))
        w1 = jax.random.normal(k_w1, (NUM_EXPERTS, EMBED_DIM, HIDDEN_DIM), dtype=jnp.float32) * np.sqrt(2.0 / EMBED_DIM)
        b1 = jnp.zeros((NUM_EXPERTS, HIDDEN_DIM), dtype=jnp.float32)
        w2 = jax.random.normal(k_w2, (NUM_EXPERTS, HIDDEN_DIM, EMBED_DIM), dtype=jnp.float32) * np.sqrt(2.0 / HIDDEN_DIM)
        b2 = jnp.zeros((NUM_EXPERTS, EMBED_DIM), dtype=jnp.float32)
        return {'x': x, 'gate_w': gate_w, 'w1': w1, 'b1': b1, 'w2': w2, 'b2': b2}
    _L0_ffn_in = _L0_ffn_setup()
    _d = {'L0_attn_x': _L0_attn_in['x'], 'L0_attn_W_kv': _L0_attn_in['W_kv'], 'L0_attn_g_kv': _L0_attn_in['g_kv'], 'L0_attn_W_kdec': _L0_attn_in['W_kdec'], 'L0_attn_W_vdec': _L0_attn_in['W_vdec'], 'L0_attn_W_q': _L0_attn_in['W_q'], 'L0_attn_W_qdec': _L0_attn_in['W_qdec'], 'L0_attn_W_krope': _L0_attn_in['W_krope'], 'L0_attn_W_qrope': _L0_attn_in['W_qrope'], 'L0_attn_W_o': _L0_attn_in['W_o'], 'L0_ffn_gate_w': _L0_ffn_in['gate_w'], 'L0_ffn_w1': _L0_ffn_in['w1'], 'L0_ffn_b1': _L0_ffn_in['b1'], 'L0_ffn_w2': _L0_ffn_in['w2'], 'L0_ffn_b2': _L0_ffn_in['b2']}
    _x0 = _d['L0_attn_x']
    _d['L0_attn_x'] = jax.random.normal(jax.random.fold_in(jax.random.key(seed), 1), (32, 256, 128), dtype=_x0.dtype)
    del _x0
    return _d

def reference(L0_attn_x, L0_attn_W_kv, L0_attn_g_kv, L0_attn_W_kdec, L0_attn_W_vdec, L0_attn_W_q, L0_attn_W_qdec, L0_attn_W_krope, L0_attn_W_qrope, L0_attn_W_o, L0_ffn_gate_w, L0_ffn_w1, L0_ffn_b1, L0_ffn_w2, L0_ffn_b2):

    def _L0_attn_ref(x, W_kv, g_kv, W_kdec, W_vdec, W_q, W_qdec, W_krope, W_qrope, W_o):
        import jax, jax.numpy as jnp
        import numpy as np
        N_EMBD = 128
        N_HEAD = 16
        HEAD_DIM = N_EMBD // N_HEAD
        KV_RANK = 32
        Q_RANK = 64
        ROPE_DIM = 32
        B, T = (2, 256)
        EPS = 1e-06

        def _rope_tables(T, dim):
            inv_freq = 1.0 / 10000.0 ** (np.arange(0, dim, 2, dtype=np.float32) / dim)
            t = np.arange(T, dtype=np.float32)
            freqs = np.outer(t, inv_freq)
            emb = np.concatenate([freqs, freqs], -1)
            return (jnp.asarray(np.cos(emb)), jnp.asarray(np.sin(emb)))

        def _apply_rope(x, cos, sin):
            d2 = x.shape[-1] // 2
            x1, x2 = (x[..., :d2], x[..., d2:])
            rot = jnp.concatenate([-x2, x1], axis=-1)
            return x * cos[None, None, :, :] + rot * sin[None, None, :, :]
        Bx, Tx, C = x.shape
        kv_c = x @ W_kv
        kv_c = kv_c * jax.lax.rsqrt(jnp.mean(kv_c * kv_c, axis=-1, keepdims=True) + EPS) * g_kv
        q_c = x @ W_q

        def heads(y, d):
            return y.reshape(Bx, Tx, N_HEAD, d).transpose(0, 2, 1, 3)
        k_content = heads(kv_c @ W_kdec, HEAD_DIM)
        v = heads(kv_c @ W_vdec, HEAD_DIM)
        q_content = heads(q_c @ W_qdec, HEAD_DIM)
        k_rope = heads(x @ W_krope, ROPE_DIM)
        q_rope = heads(q_c @ W_qrope, ROPE_DIM)
        cos, sin = _rope_tables(Tx, ROPE_DIM)
        q_rope = _apply_rope(q_rope, cos, sin)
        k_rope = _apply_rope(k_rope, cos, sin)
        q = jnp.concatenate([q_content, q_rope], axis=-1)
        k = jnp.concatenate([k_content, k_rope], axis=-1)
        scale = 1.0 / jnp.sqrt(jnp.float32(q.shape[-1]))
        scores = jnp.einsum('bhqd,bhkd->bhqk', q, k) * scale
        causal = jnp.tril(jnp.ones((Tx, Tx), dtype=bool))
        scores = jnp.where(causal[None, None], scores, jnp.float32(-jnp.inf))
        attn = jax.nn.softmax(scores, axis=-1)
        out = jnp.einsum('bhqk,bhkd->bhqd', attn, v)
        out = out.transpose(0, 2, 1, 3).reshape(Bx, Tx, N_HEAD * HEAD_DIM)
        return out @ W_o

    def _L0_ffn_ref(x, gate_w, w1, b1, w2, b2):
        import jax, jax.numpy as jnp
        import numpy as np
        EMBED_DIM = 128
        HIDDEN_DIM = 512
        NUM_EXPERTS = 8
        TOP_K = 2
        orig_shape = x.shape
        xt = x.reshape(-1, EMBED_DIM)
        logits = xt @ gate_w.T
        probs = jax.nn.softmax(logits, axis=-1)
        top_w, top_i = jax.lax.top_k(probs, TOP_K)
        top_w = top_w / (top_w.sum(axis=-1, keepdims=True) + 1e-09)
        h = jnp.einsum('td,ndh->tnh', xt, w1) + b1
        h = jax.nn.gelu(h, approximate=False)
        out_all = jnp.einsum('tnh,nhd->tnd', h, w2) + b2
        sel = jnp.take_along_axis(out_all, top_i[:, :, None], axis=1)
        out = (sel * top_w[:, :, None]).sum(axis=1)
        return out.reshape(orig_shape)
    x = L0_attn_x
    x = _layernorm(x + _L0_attn_ref(x, L0_attn_W_kv, L0_attn_g_kv, L0_attn_W_kdec, L0_attn_W_vdec, L0_attn_W_q, L0_attn_W_qdec, L0_attn_W_krope, L0_attn_W_qrope, L0_attn_W_o), axis=-1)
    x = _layernorm(x + _L0_ffn_ref(x, L0_ffn_gate_w, L0_ffn_w1, L0_ffn_b1, L0_ffn_w2, L0_ffn_b2), axis=-1)
    return x

_drawn_inputs = setup_inputs


def setup_inputs(seed=0):
    import zlib

    import numpy as np

    out = dict(_drawn_inputs(seed))
    spreads = {'L0_attn_g_kv': (1.0, 0.2), 'L0_ffn_b1': (0.0, 0.1), 'L0_ffn_b2': (0.0, 0.1)}
    factors = {}
    for name, (base, spread) in spreads.items():
        noise = np.random.default_rng([zlib.crc32(name.encode()), seed]).standard_normal(out[name].shape)
        drawn = base * np.exp(spread * noise) if base else spread * noise
        out[name] = jnp.asarray(drawn.astype(out[name].dtype))
    for name, factor in factors.items():
        out[name] = (out[name] * factor).astype(out[name].dtype)
    return out
```

```python
import numpy as np
from contextlib import ExitStack

import concourse.bass as bass
from concourse import mybir

ALU = mybir.AluOpType
ACT = mybir.ActivationFunctionType
AX = mybir.AxisListType
F32 = mybir.dt.float32
F16 = mybir.dt.float16
BF16 = mybir.dt.bfloat16
I32 = mybir.dt.int32

P = 128
C = 128
T = 256
RB = T // P
H = 16
DC = 8
DR = 32
QR = 64
KR = 32
NG = 4
SROWS = 3 * (DR + DC)
MROW = SROWS
MSCALE = 32768.0
RING = 3
UNITS = 12
STACK = 8 * 16
NLOADS = 23
NCONSTS = 12


E = 8
HID = 512
HC = HID // P
ROWS = RB * P
ROWLEN = C + 4
GT = 4
XRING = 6


def route_tiles(n):
    return 2 * n // ROWS + E


def room(n):
    return n + ROWS


class Batch:

    def __init__(self, idx, turn, slot, par):
        self.idx, self.turn, self.slot, self.par = idx, turn, slot, par


def wait(eng, sem, value):
    if isinstance(value, int) and value <= 0:
        return
    eng.wait_ge(sem, value)


def counts(eng, *values):
    return [v if isinstance(v, int) else eng.to_reg(v) for v in values]


def run_steps(eng, nb, step, back=-2, ahead=4, ring=RING):
    def fixed(t):
        def at(d):
            b = t + d
            return Batch(b, b // ring, b % ring, b % 2) if 0 <= b < nb else None
        return at

    first = ring - back
    turns = (nb - ahead - first) // ring
    for t in range(-ahead, first):
        step(fixed(t))
    if turns > 0:
        with eng.Fori(0, turns) as i:
            for q in range(ring):
                def at(d):
                    k = first + q + d
                    return Batch(i * ring + k, i + k // ring, k % ring, k % 2)
                step(at)
    for t in range(first + max(turns, 0) * ring, nb - back):
        step(fixed(t))


def attention(nc, logits, x, W_kv, g_kv, W_kdec, W_vdec, W_q, W_qdec, W_krope, W_qrope, W_o, gate_wT, cos_t, sin_t, x1_dram, scratch):
    NB = x.shape[0]
    SCALE = float(DC + DR) ** -0.5

    with ExitStack() as ctx:
        def sb(name, shape, dt):
            return ctx.enter_context(nc.sbuf_tensor(name, shape, dt))

        def psum(name, shape, dt):
            return ctx.enter_context(nc.psum_tensor(name, shape, dt))

        def sem(name):
            return ctx.enter_context(nc.semaphore(name))

        def ring_sems(name):
            return [sem(f"{name}{i}") for i in range(RING)]

        ps_max = psum("ps_max", [P, 2, 512], F32)
        ps_exp = psum("ps_exp", [P, 2, 512], F32)
        ps_rope = psum("ps_rope", [P, 2, 512], F32)
        ps_proj = psum("ps_proj", [P, 512], F32)
        ps_out = psum("ps_out", [P, 512], F32)

        ident = sb("ident", [P, P], F32)
        ident16 = sb("ident16", [P, P], F16)
        identb = sb("identb", [P, P], BF16)
        causal = sb("causal", [P, 4, P], BF16)
        cos_sb = sb("cos_sb", [P, T], F32)
        sin_sb = sb("sin_sb", [P, T], F32)
        neghalf = sb("neghalf", [P, 2], F32)
        raw = sb("raw", [P, 2, 512], F32)
        raws = sb("raws", [P, 4, P], F32)
        gk = sb("gk", [P, 1], F32)
        w_qkv = sb("w_qkv", [P, 2, QR + KR], F16)
        w_rope = sb("w_rope", [P, 2, 2, 2, NG, P], F16)
        w_qc = sb("w_qc", [P, 2, P], F16)
        w_kv_split = sb("w_kv_split", [P, 2, 2, P], F16)
        w_kv_stack = sb("w_kv_stack", [P, 2, P], F16)
        wo = sb("wo", [P, C], F32)
        gate_t = sb("gate_t", [C, 8], F32)

        x_in = sb("x_in", [P, RING, RB, C], F32)
        x_res = sb("x_res", [P, RING, RB, C], F32)
        x_split = sb("x_split", [P, 2, RB * C], F16)
        xT = sb("xT", [C, RING, 2, T], F16)
        ssq = sb("ssq", [P, RING, RB], F32)
        sq_junk = sb("sq_junk", [P, RB, KR], F32)
        ms = sb("ms", [P, RB], F32)
        rstd_kv = sb("rstd_kv", [P, RB], F32)
        qkv = sb("qkv", [P, RB, QR + KR], F32)
        kvn = sb("kvn", [P, RB, KR], F32)
        qkv_split = sb("qkv_split", [P, RB, 4, QR], F16)
        qkvT = sb("qkvT", [P, RING, 2, T], F16)
        rope_cos = sb("rope_cos", [P, 2, 512], F32)
        rope_sin = sb("rope_sin", [P, 2, 512], F32)
        rope_sum = sb("rope_sum", [P, 2, 512], F32)
        parts = sb("parts", [P, 2, 2, NG + 1, T], F16)
        k_stack = sb("k_stack", [P, RING, H, T], F16)
        q_stack = sb("q_stack", [P, RING, H, T], F16)
        v_aug = sb("v_aug", [P, RING, RB, H, 32], F32)
        row_max = sb("row_max", [P, RB, H], F32)
        neg_max = sb("neg_max", [P, RB, H], F16)
        neg_maxT = sb("neg_maxT", [H, RING, T], F16)
        p0 = sb("p0", [P, H, T], F32)
        p1 = sb("p1", [P, H, P], F32)
        oT = sb("oT", [P, NG, T], F32)
        rden = sb("rden", [P, H], F32)
        on = sb("on", [P, RB, H, DC], F32)
        onT = sb("onT", [P, T], F32)
        resid = sb("resid", [P, RB, C], F32)
        stats = sb("stats", [P, RB, 6], F32)
        mean_var = sb("mean_var", [P, RB, 2], F32)
        rstd1 = sb("rstd1", [P, RB], F32)
        var_eps = sb("var_eps", [P, RB], F32)
        x1 = sb("x1", [P, RING, RB, C], F32)
        x1T = sb("x1T", [C, T], F32)

        const_in = sem("const_in")
        consts_made = sem("consts_made")
        weights_made = sem("weights_made")
        dve_step = sem("dve_step")
        x_loaded = ring_sems("x_loaded")
        res_loaded = ring_sems("res_loaded")
        x_hi_made = sem("x_hi_made")
        x_lo_made = sem("x_lo_made")
        xT_ready = sem("xT_ready")
        xT_copied = sem("xT_copied")
        qkv_ready = sem("qkv_ready")
        qkv_read = sem("qkv_read")
        ms_made = sem("ms_made")
        rstd_kv_made = sem("rstd_kv_made")
        kvn_made = sem("kvn_made")
        kv_hi_made = sem("kv_hi_made")
        split_made = sem("split_made")
        splitT_ready = sem("splitT_ready")
        splitT_copied = sem("splitT_copied")
        content_ready = sem("content_ready")
        c_hi_made = sem("c_hi_made")
        c_lo_made = sem("c_lo_made")
        v_ready = sem("v_ready")
        v_copied = sem("v_copied")
        rope_a = sem("rope_a")
        rope_b = sem("rope_b")
        cos_done = sem("cos_done")
        sin_done = sem("sin_done")
        sum_done = sem("sum_done")
        r_hi_made = sem("r_hi_made")
        k_lo_made = sem("k_lo_made")
        q_lo_made = sem("q_lo_made")
        parked = ring_sems("parked")
        stacked = ring_sems("stacked")
        max_in = sem("max_in")
        max_done = sem("max_done")
        neg_max_made = sem("neg_max_made")
        neg_maxT_ready = sem("neg_maxT_ready")
        neg_maxT_copied = sem("neg_maxT_copied")
        max_row_in = ring_sems("max_row_in")
        exp_in = sem("exp_in")
        exp_done = sem("exp_done")
        masked = sem("masked")
        pv_done = sem("pv_done")
        oT_copied = sem("oT_copied")
        o_ready = sem("o_ready")
        rden_made = sem("rden_made")
        norm_done = sem("norm_done")
        onT_ready = sem("onT_ready")
        onT_copied = sem("onT_copied")
        attn_ready = sem("attn_ready")
        resid_made = sem("resid_made")
        stats_made = sem("stats_made")
        var_made = sem("var_made")
        eps_added = sem("eps_added")
        rstd1_made = sem("rstd1_made")
        x1_made = sem("x1_made")
        x1T_ready = sem("x1T_ready")
        x1T_copied = sem("x1T_copied")
        logits_ready = sem("logits_ready")
        logits_copied = sem("logits_copied")
        x1_stored = ring_sems("x1_stored")

        f16_proj = ps_proj[:, :].bitcast(F16)

        def rows(b):
            def of(a):
                if isinstance(b.idx, int):
                    return a[b.idx].rearrange("(r p) c -> p r c", p=P)
                return a[bass.ds(b.idx, 1), :, :].rearrange("a (r p) c -> p (a r) c", p=P)
            return of

        with nc.Block() as block:
            def wait_parked(eng, b):
                if isinstance(b.idx, int):
                    wait(eng, parked[(b.idx - 1) % RING], 32 * ((b.idx - 1) // RING + 1) if b.idx else 0)
                else:
                    eng.wait_ge(parked[(b.slot - 1) % RING], (b.turn + (1 if b.slot else 0)) * 32)

            @block.sync
            def _(sp):
                n = [0]

                def load(dst, src):
                    sp.dma_start(dst, src).then_inc(const_in, 16)
                    n[0] += 1
                load(raws[:, 0, 0:QR], W_q)
                load(raws[:, 0, QR:QR + KR], W_kv)
                load(cos_sb[:, :], cos_t)
                load(sin_sb[:, :], sin_t)
                load(raw[:, 0, :], W_krope)
                for k in range(2):
                    load(raw[64 * k:64 * k + 64, 1, :], W_qrope)
                    load(raws[64 * k:64 * k + 64, 1, :], W_qdec)
                for k in range(4):
                    load(raws[32 * k:32 * k + 32, 2, :], W_kdec)
                    load(raws[32 * k:32 * k + 32, 3, :], W_vdec)
                    load(gk[32 * k:32 * k + 32, :], g_kv.rearrange("(p a) -> p a", a=1))
                load(wo[:, :], W_o)
                load(gate_t[:, :], gate_wT)
                assert n[0] == NLOADS

                def park(b, side):
                    dst = scratch[b.slot, side].rearrange("m p n -> p m n")
                    sp.dma_start(dst, parts[:, side].rearrange("p m g t -> p m (g t)")).then_inc(parked[b.slot], 16)

                def stack(b, side, tile, at, part, count):
                    src = scratch[b.slot, side, part:part + count].rearrange("m p n -> (m p) n")
                    rope = src[:, 0:NG * T].rearrange("(i j) n -> i j n", j=4)
                    sp.dma_start(tile[DR * at:DR * (at + count), b.slot].rearrange("p (j g) t -> p j (g t)", j=4),
                                 rope).then_inc(stacked[b.slot], 16)
                    first = 3 * DR + DC * at
                    sp.dma_start(tile[first:first + DC * count, b.slot],
                                 src[:, NG * T:].rearrange("(d h) n -> d h n", h=H)).then_inc(stacked[b.slot], 16)

                def step(at):
                    if b := at(4):
                        wait(sp, x_lo_made, b.idx - RING + 1)
                        sp.dma_start(x_in[:, b.slot], rows(b)(x)).then_inc(x_loaded[b.slot], 16)
                    if b := at(0):
                        wait(sp, resid_made, b.idx - RING + 1)
                        sp.dma_start(x_res[:, b.slot], rows(b)(x)).then_inc(res_loaded[b.slot], 16)
                    if b := at(0):
                        wait(sp, neg_maxT_copied, b.idx + 1)
                        sp.dma_start(q_stack[MROW:MROW + 1, b.slot], neg_maxT[:, b.slot]).then_inc(max_row_in[b.slot], 16)
                    if b := at(-2):
                        wait(sp, x1_made, 2 * b.idx + 2)
                        sp.dma_start(rows(b)(x1_dram), x1[:, b.slot]).then_inc(x1_stored[b.slot], 16)
                    if b := at(2):
                        wait(sp, exp_in, UNITS * (b.idx - RING + 1))
                        wait(sp, consts_made, NCONSTS)
                        wait(sp, parked[b.slot], 32 * (b.turn + 1))
                        stack(b, 0, k_stack, 0, 0, 2)
                        stack(b, 1, q_stack, 0, 0, 1)
                        stack(b, 1, q_stack, 1, 0, 2)
                        stack(b, 0, k_stack, 2, 0, 1)
                    if b := at(3):
                        wait(sp, stacked[b.slot], STACK * b.turn)
                        wait(sp, r_hi_made, 4 * b.idx + 2)
                        wait(sp, k_lo_made, 2 * b.idx + 2)
                        wait(sp, c_lo_made, b.idx + 1)
                        park(b, 0)
                        wait(sp, r_hi_made, 4 * b.idx + 4)
                        wait(sp, q_lo_made, 2 * b.idx + 2)
                        park(b, 1)
                run_steps(sp, NB, step)
                for s in range(RING):
                    wait(sp, x1_stored[s], 16 * len(range(s, NB, RING)))

            @block.gpsimd
            def _(pool):
                g = nc.gpsimd
                n = [0]

                def made(ins):
                    ins.then_inc(consts_made, 1)
                    n[0] += 1
                made(g.memset(neghalf[:, :], -0.5))
                for m in (ident, ident16, identb):
                    made(g.memset(m[:, :], 0.0))
                made(g.memset(causal[:, :, :], 0.0))
                made(g.memset(v_aug[:, :, :, :, :], 0.0))
                pool.wait_ge(consts_made, n[0])
                made(g.memset(k_stack[96:128, :, :, :], MSCALE))
                pool.wait_ge(consts_made, n[0])
                for m in (ident, ident16, identb):
                    made(g.affine_select(out=m[:, :], in_=m[:, :], compare_op=ALU.not_equal, fill=1.0,
                                         base=0, pattern=[[-1, P]], channel_multiplier=1))
                made(g.affine_select(out=causal[:, :, :], in_=causal[:, :, :], compare_op=ALU.is_ge, fill=-1e30,
                                     base=0, pattern=[[0, 4], [-1, P]], channel_multiplier=1))
                made(g.memset(v_aug[:, :, :, :, DC:DC + 1].rearrange("p s r h a -> p (s r h) a"), 1.0))
                assert n[0] == NCONSTS

                def rope_sum_of(b, n):
                    s = n % 2
                    wait(pool, sin_done, 4 * b.idx + n + 1)
                    wait(pool, r_hi_made, 4 * b.idx + n - 1)
                    if n < 2:
                        wait(pool, q_lo_made, 2 * b.idx - 1 + n)
                    else:
                        wait(pool, k_lo_made, 2 * b.idx + n - 1)
                    g.tensor_tensor(rope_sum[:, s], rope_cos[:, s], rope_sin[:, s], ALU.add).then_inc(sum_done, 1)

                def k_lo(b, n):
                    wait(pool, r_hi_made, 4 * b.idx + n + 1)
                    if n == 0:
                        wait_parked(pool, b)
                    g.tensor_tensor(parts[:, 0, 1, 2 * n:2 * n + 2, :],
                                    rope_sum[:, n].rearrange("p (g t) -> p g t", g=2),
                                    parts[:, 0, 0, 2 * n:2 * n + 2, :], ALU.subtract).then_inc(k_lo_made, 1)

                def mask(b, a):
                    exps, = counts(pool, UNITS * b.idx + 3 * a + 3)
                    pool.wait_ge(consts_made, NCONSTS)
                    wait(pool, exp_done, exps)
                    for k, tile in enumerate((p0[:, 4 * a:4 * a + 4, 0:P], p1[:, 4 * a:4 * a + 4, :])):
                        ins = g.affine_select(out=tile, in_=tile, compare_op=ALU.is_ge, fill=fill0, base=0,
                                              pattern=[[0, 4], [1, P]], channel_multiplier=-1)
                        ins.then_inc(masked, 1)

                def rstd_kv_of(b):
                    reads, used = counts(pool, 4 * b.idx + 4, b.idx)
                    pool.wait_ge(consts_made, NCONSTS)
                    wait(pool, qkv_read, reads)
                    wait(pool, kvn_made, used)
                    g.tensor_scalar(ms[:, :], ssq[:, b.slot], 1.0 / KR, 1e-6, ALU.mult, ALU.add).then_inc(ms_made, 1)
                    wait(pool, ms_made, b.idx + 1)
                    g.tensor_tensor(rstd_kv[:, :], ms[:, :], neghalf[:, :], ALU.pow).then_inc(rstd_kv_made, 1)

                def x_lo(b):
                    wait(pool, x_hi_made, b.idx + 1)
                    g.tensor_tensor(x_split[:, 1], x_in[:, b.slot].rearrange("p r c -> p (r c)"), x_split[:, 0],
                                    ALU.subtract).then_inc(x_lo_made, 1)

                def rstd1_of(b):
                    variances, used = counts(pool, 2 * b.idx + 2, 2 * b.idx)
                    pool.wait_ge(consts_made, NCONSTS)
                    wait(pool, var_made, variances)
                    wait(pool, x1_made, used)
                    g.tensor_scalar(var_eps[:, :], mean_var[:, :, 1], 1e-5, None, ALU.add).then_inc(eps_added, 1)
                    wait(pool, eps_added, b.idx + 1)
                    g.tensor_tensor(rstd1[:, :], var_eps[:, :], neghalf[:, :], ALU.pow).then_inc(rstd1_made, 1)

                fill0 = g.to_reg(0.0)

                def step(at):
                    if b := at(3):
                        rstd_kv_of(b)
                    if b := at(-1):
                        mask(b, 2)
                    if b := at(3):
                        rope_sum_of(b, 0)
                        k_lo(b, 0)
                    if b := at(-1):
                        mask(b, 3)
                    if b := at(3):
                        rope_sum_of(b, 1)
                        k_lo(b, 1)
                    if b := at(4):
                        x_lo(b)
                    if b := at(0):
                        mask(b, 0)
                    if b := at(3):
                        rope_sum_of(b, 2)
                    if b := at(0):
                        mask(b, 1)
                    if b := at(3):
                        rope_sum_of(b, 3)
                    if b := at(-1):
                        rstd1_of(b)
                run_steps(pool, NB, step)

            @block.scalar
            def _(act):
                a = nc.scalar

                def copy(dst, src):
                    return a.activation(dst, src, ACT.Copy)

                def x_hi(b):
                    act.wait_ge(x_loaded[b.slot], b.turn * 16 + 16)
                    wait(act, xT_ready, b.idx)
                    copy(x_split[:, 0], x_in[:, b.slot].rearrange("p r c -> p (r c)")).then_inc(x_hi_made, 1)

                def xT_copy(b):
                    act.wait_ge(xT_ready, b.idx + 1)
                    copy(xT[:, b.slot].rearrange("p s t -> p (s t)"), f16_proj[:, 0:512]).then_inc(xT_copied, 1)

                def qkv_copy(b):
                    act.wait_ge(qkv_ready, b.idx + 1)
                    wait(act, split_made, 2 * b.idx)
                    pq = ps_proj[:, 0:RB * (QR + KR)].rearrange("p (r n) -> p r n", r=RB)
                    for r in range(RB):
                        a.activation(sq_junk[:, r], pq[:, r, QR:QR + KR], ACT.Square,
                                     accum_out=ssq[:, b.slot, r:r + 1]).then_inc(qkv_read, 1)
                    copy(qkv[:, :, :], pq).then_inc(qkv_read, 1)
                    wait(act, splitT_ready, b.idx)
                    copy(qkv_split[:, :, 0, :], pq[:, :, 0:QR]).then_inc(qkv_read, 1)

                def splitT_copy(b):
                    act.wait_ge(splitT_ready, b.idx + 1)
                    copy(qkvT[:, b.slot].rearrange("p s t -> p (s t)"), f16_proj[:, 0:512]).then_inc(splitT_copied, 1)

                def c_hi_of(b):
                    act.wait_ge(content_ready, b.idx + 1)
                    wait_parked(act, b)
                    copy(parts[:, :, 0, NG], ps_proj[:, :].rearrange("p (s t) -> p s t", s=2)).then_inc(c_hi_made, 1)

                def v_copy(b):
                    act.wait_ge(v_ready, b.idx + 1)
                    copy(v_aug[:, b.slot, :, :, 0:DC].rearrange("p r h d -> p (r h) d"),
                         ps_proj[:, 0:RB * P].rearrange("p (n d) -> p n d", d=DC)).then_inc(v_copied, 1)

                def r_hi_of(b, n):
                    act.wait_ge(sum_done, b.idx * 4 + n + 1)
                    if n == 0:
                        wait_parked(act, b)
                    g = 2 * (n % 2)
                    copy(parts[:, n // 2, 0, g:g + 2, :].rearrange("p g t -> p (g t)"),
                         rope_sum[:, n % 2]).then_inc(r_hi_made, 1)

                def neg_maxT_copy(b):
                    act.wait_ge(neg_maxT_ready, b.idx + 1)
                    copy(neg_maxT[:, b.slot], f16_proj[0:H, 0:T]).then_inc(neg_maxT_copied, 1)

                def exp(b, u):
                    act.wait_ge(exp_in, b.idx * UNITS + u + 1)
                    grp, r = u // 3, u % 3
                    if r == 0:
                        wait(act, pv_done, 2 * b.idx - 1 + grp // 2)
                    if r < 2:
                        dst = p0[:, 4 * grp + 2 * r:4 * grp + 2 * r + 2, :].rearrange("p h t -> p (h t)")
                    else:
                        dst = p1[:, 4 * grp:4 * grp + 4, :].rearrange("p h t -> p (h t)")
                    a.activation(dst, ps_exp[:, u % 2], ACT.Exp, scale=SCALE).then_inc(exp_done, 1)

                def oT_copy(b, half):
                    act.wait_ge(pv_done, b.idx * 2 + half + 1)
                    if half == 0:
                        wait(act, o_ready, 2 * b.idx)
                    copy(oT[:, 2 * half:2 * half + 2, :].rearrange("p g t -> p (g t)"), ps_out[:, :]).then_inc(oT_copied, 1)

                def onT_copy(b):
                    act.wait_ge(onT_ready, b.idx + 1)
                    copy(onT[:, :], ps_out[:, 0:T]).then_inc(onT_copied, 1)

                def x1T_copy(b):
                    act.wait_ge(x1T_ready, b.idx + 1)
                    copy(x1T[:, :], ps_out[:, 0:T]).then_inc(x1T_copied, 1)

                def logits_copy(b):
                    act.wait_ge(logits_ready, b.idx + 1)
                    src = ps_out[:, 0:RB * 8].rearrange("p (r e) -> p r e", r=RB)
                    copy(logits[:, bass.ds(b.idx * RB, RB), :], src).then_inc(logits_copied, 1)

                def step(at):
                    for s in range(UNITS):
                        if b := at(-1 if s < 4 else 0):
                            exp(b, (s - 4) % UNITS)
                        if s == 1 and (b := at(0)):
                            neg_maxT_copy(b)
                        if s == 1 and (b := at(-2)):
                            x1T_copy(b)
                        if s == 2 and (b := at(3)):
                            splitT_copy(b)
                            r_hi_of(b, 0)
                        if s == 2 and (b := at(-2)):
                            logits_copy(b)
                        if s == 4 and (b := at(3)):
                            c_hi_of(b)
                        if s == 5 and (b := at(3)):
                            r_hi_of(b, 1)
                        if s == 5 and (b := at(-1)):
                            oT_copy(b, 1)
                        if s == 5 and (b := at(4)):
                            x_hi(b)
                        if s == 7 and (b := at(2)):
                            v_copy(b)
                        if s == 8 and (b := at(-1)):
                            onT_copy(b)
                        if s == 8 and (b := at(3)):
                            r_hi_of(b, 2)
                        if s == 9 and (b := at(4)):
                            xT_copy(b)
                        if s == 10 and (b := at(3)):
                            r_hi_of(b, 3)
                        if s == 11 and (b := at(0)):
                            oT_copy(b, 0)
                        if s == 11 and (b := at(4)):
                            qkv_copy(b)
                act.wait_ge(consts_made, NCONSTS)
                run_steps(act, NB, step)

            @block.vector
            def _(dve):
                v = nc.vector
                n = [0]

                def link(ins):
                    n[0] += 1
                    ins.then_inc(dve_step, 1)
                    dve.wait_ge(dve_step, n[0])

                def by_dim(a):
                    return a.rearrange("p (h d) -> p d h", h=H)

                dve.wait_ge(const_in, 16 * NLOADS)
                v.tensor_copy(w_qkv[:, 0], raws[:, 0, 0:QR + KR]).then_inc(dve_step, 1)
                n[0] += 1
                for side in range(2):
                    src = raw[:, side].rearrange("p (j g i) -> p g i j", j=4, g=NG)
                    for sw in range(2):
                        hi = w_rope[:, side, sw, 0].rearrange("p g (i j) -> p g i j", j=4)
                        for g in range(NG):
                            for half in range(2):
                                h2 = half ^ sw
                                v.tensor_copy(hi[:, g, 16 * half:16 * half + 16, :],
                                              src[:, g, 16 * h2:16 * h2 + 16, :]).then_inc(dve_step, 1)
                                n[0] += 1
                v.tensor_copy(w_qc[:, 0].rearrange("p (d h) -> p d h", h=H), by_dim(raws[:, 1])).then_inc(dve_step, 1)
                n[0] += 1
                for k in range(2):
                    v.tensor_scalar(raws[:, 2 + k], raws[:, 2 + k], gk[:, 0:1], None, ALU.mult).then_inc(dve_step, 1)
                    n[0] += 1
                dve.wait_ge(dve_step, n[0])
                v.tensor_tensor(w_qkv[:, 1], raws[:, 0, 0:QR + KR], w_qkv[:, 0], ALU.subtract).then_inc(weights_made, 1)
                v.tensor_tensor(w_qc[:, 1].rearrange("p (d h) -> p d h", h=H), by_dim(raws[:, 1]),
                                w_qc[:, 0].rearrange("p (d h) -> p d h", h=H), ALU.subtract).then_inc(weights_made, 1)
                for side in range(2):
                    src = raw[:, side].rearrange("p (j g i) -> p g i j", j=4, g=NG)
                    for sw in range(2):
                        hi = w_rope[:, side, sw, 0].rearrange("p g (i j) -> p g i j", j=4)
                        lo = w_rope[:, side, sw, 1].rearrange("p g (i j) -> p g i j", j=4)
                        for g in range(NG):
                            for half in range(2):
                                h2 = half ^ sw
                                v.tensor_tensor(lo[:, g, 16 * half:16 * half + 16, :],
                                                src[:, g, 16 * h2:16 * h2 + 16, :],
                                                hi[:, g, 16 * half:16 * half + 16, :],
                                                ALU.subtract).then_inc(weights_made, 1)
                def arranged(a, k, head_major):
                    if k:
                        return a
                    return by_dim(a) if head_major else a.rearrange("p (d h) -> p d h", h=H)

                for k in range(2):
                    link(v.tensor_copy(w_kv_split[:, k, 0], raws[:, 2 + k]))
                    link(v.tensor_tensor(w_kv_split[:, k, 1], raws[:, 2 + k], w_kv_split[:, k, 0], ALU.subtract))
                    v.tensor_copy(arranged(w_kv_stack[0:64, k], k, False), arranged(w_kv_split[0:64, k, 0], k, True)).then_inc(weights_made, 1)
                    v.tensor_copy(arranged(w_kv_stack[64:128, k], k, False), arranged(w_kv_split[64:128, k, 1], k, True)).then_inc(weights_made, 1)

                def max_of(b, u):
                    dve.wait_ge(max_in, b.idx * UNITS + u + 1)
                    grp, r = u // 3, u % 3
                    if u == 0:
                        wait(dve, neg_max_made, b.idx)
                    if r < 2:
                        h = 4 * grp + 2 * r
                        v.tensor_reduce(row_max[:, 1, h:h + 2], ps_max[:, u % 2].rearrange("p (h t) -> p h t", h=2),
                                        AX.X, ALU.max).then_inc(max_done, 1)
                    else:
                        v.tensor_reduce(row_max[:, 0, 4 * grp:4 * grp + 4],
                                        ps_max[:, u % 2].rearrange("p (h t) -> p h t", h=4),
                                        AX.X, ALU.max).then_inc(max_done, 1)

                def neg_max_of(b):
                    dve.wait_ge(max_done, b.idx * UNITS + UNITS)
                    wait(dve, neg_maxT_ready, b.idx)
                    v.tensor_scalar(neg_max[:, :, :].rearrange("p r h -> p (r h)"),
                                    row_max[:, :, :].rearrange("p r h -> p (r h)"), -1.0 / MSCALE, None,
                                    ALU.mult).then_inc(neg_max_made, 1)

                def splits(b):
                    dve.wait_ge(qkv_read, b.idx * 4 + 4)
                    wait(dve, splitT_ready, b.idx)
                    v.tensor_tensor(qkv_split[:, :, 1, :], qkv[:, :, 0:QR], qkv_split[:, :, 0, :],
                                    ALU.subtract).then_inc(split_made, 1)
                    dve.wait_ge(rstd_kv_made, b.idx + 1)
                    v.tensor_tensor(kvn[:, :, :], qkv[:, :, QR:QR + KR],
                                    rstd_kv[:, :].unsqueeze(2).broadcast_to([P, RB, KR]),
                                    ALU.mult).then_inc(kvn_made, 1)
                    dve.wait_ge(kvn_made, b.idx + 1)
                    twice = kvn[:, :, :].unsqueeze(2).broadcast_to([P, RB, 2, KR])
                    v.tensor_copy(qkv_split[:, :, 2:4, 0:KR], twice).then_inc(kv_hi_made, 1)
                    dve.wait_ge(kv_hi_made, b.idx + 1)
                    v.tensor_tensor(qkv_split[:, :, 2:4, KR:2 * KR], twice, qkv_split[:, :, 2:4, 0:KR],
                                    ALU.subtract).then_inc(split_made, 1)

                def c_lo_of(b):
                    dve.wait_ge(c_hi_made, b.idx + 1)
                    v.tensor_tensor(parts[:, :, 1, NG], ps_proj[:, :].rearrange("p (s t) -> p s t", s=2),
                                    parts[:, :, 0, NG], ALU.subtract).then_inc(c_lo_made, 1)

                def rope(b, n):
                    s = n % 2
                    for sem_in, bank, table, dst, done in ((rope_a, 0, cos_sb, rope_cos, cos_done),
                                                           (rope_b, 1, sin_sb, rope_sin, sin_done)):
                        dve.wait_ge(sem_in, b.idx * 4 + n + 1)
                        wait(dve, sum_done, 4 * b.idx + n - 1)
                        v.tensor_tensor(dst[:, s].rearrange("p (g t) -> p g t", g=2),
                                        ps_rope[:, bank].rearrange("p (g t) -> p g t", g=2),
                                        table[:, :].unsqueeze(1).broadcast_to([P, 2, T]), ALU.mult).then_inc(done, 1)

                def q_lo(b, n):
                    dve.wait_ge(r_hi_made, b.idx * 4 + n + 3)
                    v.tensor_tensor(parts[:, 1, 1, 2 * n:2 * n + 2, :],
                                    rope_sum[:, n].rearrange("p (g t) -> p g t", g=2),
                                    parts[:, 1, 0, 2 * n:2 * n + 2, :], ALU.subtract).then_inc(q_lo_made, 1)

                def norm(b, r):
                    dve.wait_ge(o_ready, b.idx * 2 + r + 1)
                    o = ps_out[:, :].rearrange("p (h n) -> p h n", n=32)
                    v.reciprocal(rden[:, :].unsqueeze(2), o[:, :, DC:DC + 1]).then_inc(rden_made, 1)
                    dve.wait_ge(rden_made, b.idx * 2 + r + 1)
                    v.tensor_tensor(on[:, r], o[:, :, 0:DC], rden[:, :].unsqueeze(2).broadcast_to([P, H, DC]),
                                    ALU.mult).then_inc(norm_done, 1)

                def resid_of(b):
                    dve.wait_ge(attn_ready, b.idx + 1)
                    dve.wait_ge(res_loaded[b.slot], b.turn * 16 + 16)
                    v.tensor_tensor(resid[:, :, :].rearrange("p r c -> p (r c)"), ps_out[:, 0:RB * C],
                                    x_res[:, b.slot].rearrange("p r c -> p (r c)"), ALU.add).then_inc(resid_made, 1)
                    dve.wait_ge(resid_made, b.idx + 1)
                    for r in range(RB):
                        v.bn_stats(stats[:, r], resid[:, r]).then_inc(stats_made, 1)
                    halves, = counts(dve, b.idx * 2 + 2)
                    dve.wait_ge(const_in, 16 * NLOADS)
                    dve.wait_ge(stats_made, halves)
                    for r in range(RB):
                        v.bn_aggr(mean_var[:, r], stats[:, r]).then_inc(var_made, 1)

                def x1_of(b):
                    dve.wait_ge(rstd1_made, b.idx + 1)
                    if isinstance(b.idx, int):
                        wait(dve, x1_stored[b.slot], 16 * (b.idx // RING))
                    else:
                        dve.wait_ge(x1_stored[b.slot], b.turn * 16)
                    for r in range(RB):
                        v.tensor_scalar(x1[:, b.slot, r], resid[:, r], mean_var[:, r, 0:1], rstd1[:, r:r + 1],
                                        ALU.subtract, ALU.mult).then_inc(x1_made, 1)

                def step(at):
                    for s in range(UNITS):
                        if b := at(1):
                            max_of(b, s)
                        if s == 0 and (b := at(-2)):
                            x1_of(b)
                        if s == 0 and (b := at(3)):
                            splits(b)
                        if s == 1 and (b := at(3)):
                            rope(b, 0)
                        if s == 4 and (b := at(3)):
                            rope(b, 1)
                        if s == 5 and (b := at(3)):
                            c_lo_of(b)
                        if s == 7 and (b := at(-1)):
                            norm(b, 0)
                        if s == 7 and (b := at(3)):
                            rope(b, 2)
                        if s == 8 and (b := at(-1)):
                            norm(b, 1)
                        if s == 9 and (b := at(3)):
                            q_lo(b, 0)
                            rope(b, 3)
                        if s == 10 and (b := at(-1)):
                            resid_of(b)
                        if s == 11 and (b := at(3)):
                            q_lo(b, 1)
                        if s == 11 and (b := at(1)):
                            neg_max_of(b)
                run_steps(dve, NB, step)

            @block.tensor
            def _(pe):
                t = nc.tensor
                pe.wait_ge(consts_made, NCONSTS)
                pe.wait_ge(weights_made, 38)
                pe.wait_ge(const_in, 16 * NLOADS)

                def group(out, terms, sem_done=None):
                    for k, (l, r) in enumerate(terms):
                        ins = t.matmul(out, l, r, start=(k == 0), stop=(k == len(terms) - 1))
                    return ins

                def xT_of(b):
                    pe.wait_ge(x_lo_made, b.idx + 1)
                    wait(pe, v_copied, b.idx - 1)
                    if isinstance(b.idx, int) and b.idx < 2:
                        wait(pe, c_lo_made, b.idx)
                    for k in range(2):
                        for r in range(RB):
                            ins = t.transpose(f16_proj[:, (2 * k + r) * P:(2 * k + r + 1) * P],
                                              x_split[:, k, r * C:(r + 1) * C], ident16[:, :])
                    ins.then_inc(xT_ready, 1)

                def qkv_of(b):
                    pe.wait_ge(xT_copied, b.idx + 1)
                    for r in range(RB):
                        hi, lo = (xT[:, b.slot, k, r * P:(r + 1) * P] for k in range(2))
                        ins = group(ps_proj[:, r * (QR + KR):(r + 1) * (QR + KR)],
                                    [(hi, w_qkv[:, 0]), (lo, w_qkv[:, 0]), (hi, w_qkv[:, 1])])
                    ins.then_inc(qkv_ready, 1)

                def neg_maxT_of(b, more):
                    pe.wait_ge(neg_max_made, b.idx + 1)
                    if more:
                        pe.wait_ge(qkv_read, b.idx * 4 + 16)
                    else:
                        wait(pe, v_copied, min(b.idx + 2, NB))
                    for r in range(RB):
                        ins = t.transpose(f16_proj[0:H, r * P:(r + 1) * P], neg_max[:, r], ident16[:, :])
                    ins.then_inc(neg_maxT_ready, 1)

                def splitT_of(b):
                    pe.wait_ge(split_made, b.idx * 2 + 2)
                    pe.wait_ge(qkv_read, b.idx * 4 + 4)
                    wait(pe, neg_maxT_copied, b.idx - 2)
                    for k in range(2):
                        for r in range(RB):
                            ins = t.transpose(f16_proj[:, (2 * k + r) * P:(2 * k + r + 1) * P],
                                              qkv_split[:, r, 2 * k:2 * k + 2, :].rearrange("p a n -> p (a n)"),
                                              ident16[:, :])
                    ins.then_inc(splitT_ready, 1)

                def content(b):
                    pe.wait_ge(splitT_copied, b.idx + 1)
                    t.matmul(ps_proj[:, 0:T], w_kv_stack[:, 0], qkvT[:, b.slot, 1], start=True, stop=True)
                    group(ps_proj[:, T:2 * T], [(w_qc[:, k], qkvT[:, b.slot, 0]) for k in range(2)]).then_inc(content_ready, 1)

                def v_of(b, more):
                    pe.wait_ge(c_lo_made, b.idx + (2 if more else 1))
                    for r in range(RB):
                        ins = t.matmul(ps_proj[:, r * P:(r + 1) * P], qkvT[:, b.slot, 1, r * P:(r + 1) * P],
                                       w_kv_stack[:, 1], start=True, stop=True)
                    ins.then_inc(v_ready, 1)

                def rope(b, n):
                    side = n // 2
                    if side:
                        pe.wait_ge(splitT_copied, b.idx + 1)
                    for sw, read, done in ((0, cos_done, rope_a), (1, sin_done, rope_b)):
                        wait(pe, read, 4 * b.idx + n)
                        for k in range(2):
                            g = 2 * (n % 2) + k
                            hi, lo = (w_rope[:, side, sw, m, g] for m in range(2))
                            if side == 0:
                                xh, xl = xT[:, b.slot, 0], xT[:, b.slot, 1]
                                terms = [(hi, xh), (hi, xl), (lo, xh)]
                            else:
                                terms = [(hi, qkvT[:, b.slot, 0]), (lo, qkvT[:, b.slot, 0])]
                            ins = group(ps_rope[:, sw, k * T:(k + 1) * T], terms)
                        ins.then_inc(done, 1)

                def scores_max(b, u):
                    if u == 0:
                        pe.wait_ge(stacked[b.slot], b.turn * STACK + STACK)
                    wait(pe, max_done, UNITS * b.idx + u - 1)
                    grp, r = u // 3, u % 3
                    bank = ps_max[:, u % 2]
                    ks, qs = k_stack[0:SROWS, b.slot], q_stack[0:SROWS, b.slot]
                    if r < 2:
                        for k in range(2):
                            h = 4 * grp + 2 * r + k
                            t.matmul(bank[:, k * T:(k + 1) * T], qs[:, h, P:T], ks[:, h, :], start=(k == 0), stop=False,
                                     skip_group_check=True)
                        ins = t.matmul(bank.rearrange("p (h t) -> p h t", h=2)[:, :, P:T], identb[:, :],
                                       causal[:, 0:2, :], start=False, stop=True, skip_group_check=True)
                    else:
                        for k in range(4):
                            h = 4 * grp + k
                            t.matmul(bank[:, k * P:(k + 1) * P], qs[:, h, 0:P], ks[:, h, 0:P], start=(k == 0), stop=False,
                                     skip_group_check=True)
                        ins = t.matmul(bank, identb[:, :], causal[:, :, :].rearrange("p a t -> p (a t)"),
                                       start=False, stop=True, skip_group_check=True)
                    ins.then_inc(max_in, 1)

                def scores_exp(b, u):
                    if u == 0:
                        pe.wait_ge(max_row_in[b.slot], b.turn * 16 + 16)
                    wait(pe, exp_done, UNITS * b.idx + u - 1)
                    grp, r = u // 3, u % 3
                    bank = ps_exp[:, u % 2]
                    ks, qs = k_stack[0:SROWS + 1, b.slot], q_stack[0:SROWS + 1, b.slot]
                    if r < 2:
                        for k in range(2):
                            h = 4 * grp + 2 * r + k
                            ins = t.matmul(bank[:, k * T:(k + 1) * T], ks[:, h, 0:P], qs[:, h, :], start=True, stop=True)
                    else:
                        for k in range(4):
                            h = 4 * grp + k
                            ins = t.matmul(bank[:, k * P:(k + 1) * P], ks[:, h, P:T], qs[:, h, P:T], start=True, stop=True)
                    ins.then_inc(exp_in, 1)

                def pv(b, half):
                    pe.wait_ge(masked, b.idx * 8 + 4 * half + 4)
                    if half == 0:
                        wait(pe, resid_made, b.idx)
                    else:
                        wait(pe, logits_copied, b.idx)
                        pe.wait_ge(oT_copied, b.idx * 2 + 1)
                    for k in range(2):
                        for j in range(4):
                            h = 4 * (2 * half + k) + j
                            out = ps_out[32 * j:32 * j + 32, k * T:(k + 1) * T]
                            t.matmul(out, v_aug[:, b.slot, 0, h], p0[:, h, :], start=True, stop=False, skip_group_check=True)
                        for j in range(4):
                            h = 4 * (2 * half + k) + j
                            out = ps_out[32 * j:32 * j + 32, k * T:(k + 1) * T]
                            ins = t.matmul(out[:, P:T], v_aug[:, b.slot, 1, h], p1[:, h, :], start=False, stop=True,
                                           skip_group_check=True)
                    ins.then_inc(pv_done, 1)

                def o_of(b, r):
                    if r == 0:
                        pe.wait_ge(oT_copied, b.idx * 2 + 2)
                    else:
                        pe.wait_ge(norm_done, b.idx * 2 + 1)
                    for g in range(NG):
                        ins = t.transpose(ps_out[:, g * P:(g + 1) * P], oT[:, g, r * P:(r + 1) * P], ident[:, :])
                    ins.then_inc(o_ready, 1)

                def onT_of(b):
                    pe.wait_ge(norm_done, b.idx * 2 + 2)
                    for r in range(RB):
                        ins = t.transpose(ps_out[:, r * P:(r + 1) * P], on[:, r].rearrange("p h d -> p (h d)"), ident[:, :])
                    ins.then_inc(onT_ready, 1)

                def attn(b):
                    pe.wait_ge(onT_copied, b.idx + 1)
                    for r in range(RB):
                        ins = t.matmul(ps_out[:, r * C:(r + 1) * C], onT[:, r * P:(r + 1) * P], wo[:, :], start=True, stop=True)
                    ins.then_inc(attn_ready, 1)

                def x1T_of(b, more):
                    pe.wait_ge(x1_made, b.idx * 2 + 2)
                    if more:
                        pe.wait_ge(oT_copied, b.idx * 2 + 3)
                    for r in range(RB):
                        ins = t.transpose(ps_out[:, r * P:(r + 1) * P], x1[:, b.slot, r], ident[:, :])
                    ins.then_inc(x1T_ready, 1)

                def logits_of(b):
                    pe.wait_ge(x1T_copied, b.idx + 1)
                    for r in range(RB):
                        ins = t.matmul(ps_out[:, r * 8:(r + 1) * 8], x1T[:, r * P:(r + 1) * P], gate_t[:, :],
                                       start=True, stop=True)
                    ins.then_inc(logits_ready, 1)

                def step(at):
                    for s in range(UNITS):
                        if b := at(1):
                            scores_max(b, s)
                        if b := at(-1 if s < 4 else 0):
                            scores_exp(b, (s - 4) % UNITS)
                        if s == 0 and (b := at(3)):
                            rope(b, 0)
                        if s == 1 and (b := at(0)):
                            neg_maxT_of(b, at(3) is not None)
                        if s == 1 and (b := at(-2)):
                            x1T_of(b, at(-1) is not None)
                        if s == 2 and (b := at(3)):
                            splitT_of(b)
                        if s == 2 and (b := at(-2)):
                            logits_of(b)
                        if s == 3 and (b := at(3)):
                            rope(b, 1)
                        if s == 4 and (b := at(3)):
                            content(b)
                        if s == 5 and (b := at(-1)):
                            pv(b, 1)
                        if s == 6 and (b := at(3)):
                            rope(b, 2)
                        if s == 6 and (b := at(-1)):
                            o_of(b, 0)
                        if s == 7 and (b := at(-1)):
                            o_of(b, 1)
                        if s == 7 and (b := at(2)):
                            v_of(b, at(3) is not None)
                        if s == 8 and (b := at(3)):
                            rope(b, 3)
                        if s == 8 and (b := at(-1)):
                            onT_of(b)
                        if s == 9 and (b := at(-1)):
                            attn(b)
                        if s == 9 and (b := at(4)):
                            xT_of(b)
                        if s == 11 and (b := at(0)):
                            pv(b, 0)
                        if s == 11 and (b := at(4)):
                            qkv_of(b)
                run_steps(pe, NB, step)


def experts(nc, logits, x1_dram, xs_dram, y_dram, out, w1, b1T, w2, b2):
    N = x1_dram.shape[0] * x1_dram.shape[1]
    NT = N // P
    NR = route_tiles(N)
    NGRP = NT // GT

    with ExitStack() as ctx:
        def sb(name, shape, dt):
            return ctx.enter_context(nc.sbuf_tensor(name, shape, dt))

        def psum(name, shape, dt):
            return ctx.enter_context(nc.psum_tensor(name, shape, dt))

        def sem(name):
            return ctx.enter_context(nc.semaphore(name))

        def ring_sems(name, n):
            return [sem(f"{name}{i}") for i in range(n)]

        w1_raw = sb("w1_raw", [C, E, HID], F32)
        w1_split = sb("w1_split", [C, E, 2, HID], F16)
        w2_sb = sb("w2_sb", [P, E, HC, C], F32)
        b1_sb = sb("b1_sb", [P, E * HC], F32)
        b2_sb = sb("b2_sb", [P, E, C], F32)
        r_ident16 = sb("r_ident16", [P, P], F16)
        below = sb("below", [P, P], F16)
        ones = sb("ones", [P, P], F16)
        rank_key = sb("rank_key", [P, E], F32)
        tile_row = sb("tile_row", [P, NR], F32)
        first_row = sb("first_row", [P, E], F32)
        filling = sb("filling", [P, 2 * E * RB, ROWLEN], F32)
        ids = sb("ids", [P, 2, NT], I32)
        r_neghalf = sb("r_neghalf", [P, GT], F32)
        zero_tiles = sb("zero_tiles", [P, NT], F32)
        cell = [P, NT, E]
        prob = sb("prob", cell, F32)
        left = sb("left", cell, F32)
        key = sb("key", cell, F32)
        pick = [sb(f"pick{k}", cell, F32) for k in range(2)]
        member = sb("member", cell, F16)
        place = sb("place", cell, F32)
        total = sb("total", [P, E, NT], F32)
        upto = sb("upto", [P, E, NT], F32)
        best = sb("best", [P, 2, NT], F32)
        top_w = sb("top_w", [P, 2, NT], F32)
        tmp = sb("tmp", [P, NT], F32)
        slot_f = sb("slot_f", [P, 2, NT], F32)
        slot = sb("slot", [P, 2, NT], I32)
        count_i = sb("count_i", [P, E], I32)
        tiles_f = sb("tiles_f", [P, E], F32)
        tiles_end = sb("tiles_end", [P, E], F32)
        fill_row = sb("fill_row", [P, E], I32)
        spare = sb("spare", [P, E], F32)
        row_f = sb("row_f", [P, NR], F32)
        row_of = sb("row_of", [P, NR], I32)
        passed = sb("passed", [P, NR, E], F32)
        expert_f = sb("expert_f", [P, NR], F32)
        expert_of = sb("expert_of", [P, NR], I32)
        staged = sb("staged", [P, 2, 2, GT, ROWLEN], F32)
        index = sb("index", [P, 2, 2, GT], I32)
        xs = sb("xs", [P, XRING, RB, ROWLEN], F32)
        xs_split = sb("xs_split", [P, 2, RB, C], F16)
        xsT = sb("xsT", [C, 2, 2, ROWS], F16)
        hid = sb("hid", [P, 2, HC, ROWS], F32)
        ys = sb("ys", [P, XRING, RB, C], F32)
        y0 = sb("y0", [P, 2, GT, C], F32)
        y1 = sb("y1", [P, 2, GT, C], F32)
        xr = sb("xr", [P, 2, GT, C], F32)
        z = sb("z", [P, 2, GT, C], F32)
        zst = sb("zst", [P, 2, GT, 6], F32)
        zmv = sb("zmv", [P, 2, GT, 2], F32)
        zve = sb("zve", [P, GT], F32)
        zr = sb("zr", [P, 2, GT], F32)
        zb = sb("zb", [P, 2, GT], F32)
        zo = sb("zo", [P, 2, GT, C], F32)

        ps_t = psum("ps_t", [P, 512], F32)
        ps_h = psum("ps_h", [P, 2, 2, 512], F32)
        ps_y = psum("ps_y", [P, 2, 512], F32)
        t16 = ps_t[:, :].bitcast(F16)

        w_in = sem("w_in")
        made = sem("made")
        step_done = sem("step_done")
        shifted = sem("shifted")
        exp_taken = sem("exp_taken")
        counted = sem("counted")
        routed = sem("routed")
        fill_ready = sem("fill_ready")
        filled = sem("filled")
        w1_hi = sem("w1_hi")
        w1_lo = sem("w1_lo")
        staged_in = ring_sems("staged_in", 2)
        index_made = sem("index_made")
        scattered = ring_sems("scattered", 2)
        xs_in = ring_sems("xs_in", XRING)
        xs_hi_made = sem("xs_hi_made")
        xs_lo_made = sem("xs_lo_made")
        xsT_ready = sem("xsT_ready")
        xsT_copied = sem("xsT_copied")
        hid_ready = sem("hid_ready")
        gelu_done = sem("gelu_done")
        y_ready = sem("y_ready")
        y_made = sem("y_made")
        y_out = ring_sems("y_out", XRING)
        comb_in = ring_sems("comb_in", 2)
        z_made = sem("z_made")
        zst_made = sem("zst_made")
        zmv_made = sem("zmv_made")
        zve_made = sem("zve_made")
        zr_made = sem("zr_made")
        zb_made = sem("zb_made")
        zo_made = sem("zo_made")
        stored = ring_sems("stored", 2)

        x1_rows = x1_dram.rearrange("b t c -> (b t) c")
        out_rows = out.rearrange("b t c -> (b t) c")

        def tiles_at(a, first, n):
            return a[bass.ds(first * P, n * P), :].rearrange("(n p) c -> p n c", p=P)

        def rows_at(a, row):
            return a[bass.ds(row, ROWS), :].rearrange("(r p) c -> p r c", p=P)

        with nc.Block() as block:
            @block.sync
            def _(sp):
                for dst, src in ((w1_raw[:, :, :], w1.rearrange("e d h -> d e h")),
                                 (w2_sb[:, :, :, :], w2.rearrange("e (c p) d -> p e c d", p=P)),
                                 (b1_sb[:, :], b1T),
                                 (b2_sb[:, :, :].rearrange("p e c -> p (e c)"),
                                  b2.rearrange("e c -> (e c)").partition_broadcast(P))):
                    sp.dma_start(dst, src).then_inc(w_in, 16)

                sp.wait_ge(fill_ready, 1)
                for e in range(E):
                    row = sp.value_load(fill_row[0:1, e:e + 1], min_val=0, max_val=E * room(N))
                    sp.dma_start(rows_at(xs_dram, row), filling[:, e * RB:(e + 1) * RB]).then_inc(filled, 16)
                sp.dma_start(xs_dram[E * room(N):].rearrange("(r p) c -> p r c", p=P),
                             filling[:, E * RB:]).then_inc(filled, 16)

                def stage_x1(s, n):
                    for k in range(2):
                        sp.dma_start(staged[:, s, k, :, 0:C], tiles_at(x1_rows, n * GT, GT)).then_inc(staged_in[s], 16)
                for s in range(2):
                    stage_x1(s, s)
                with sp.Fori(1, NGRP // 2) as i:
                    for s in range(2):
                        sp.wait_ge(scattered[s], i * (2 * GT * 16))
                        stage_x1(s, i * 2 + s)
                for s in range(2):
                    sp.wait_ge(scattered[s], NGRP // 2 * 2 * GT * 16)

                def step(at):
                    if b := at(3):
                        wait(sp, y_out[b.slot], 16 * RB * b.turn)
                        row = sp.value_load(row_of[0:1, bass.ds(b.idx, 1)], min_val=0, max_val=E * (room(N) + ROWS) - ROWS)
                        sp.dma_start(xs[:, b.slot], rows_at(xs_dram, row)).then_inc(xs_in[b.slot], 16)
                sp.wait_ge(filled, 16 * (E + 1))
                sp.wait_ge(routed, 2)
                run_steps(sp, NR, step, -1, 3, XRING)
                for s in range(XRING):
                    sp.wait_ge(y_out[s], 16 * RB * len(range(s, NR, XRING)))

                def load(s, n):
                    if not (isinstance(n, int) and n < 2):
                        sp.wait_ge(z_made, (n - 2) * (2 * GT) + 2 * GT)
                    for dst, rows_ in ((y0, y_dram[0:N]), (y1, y_dram[N:2 * N]), (xr, x1_rows)):
                        sp.dma_start(dst[:, s], tiles_at(rows_, n * GT, GT)).then_inc(comb_in[s], 16)

                def store(s, n):
                    sp.wait_ge(zo_made, n * GT + GT)
                    sp.dma_start(tiles_at(out_rows, n * GT, GT), zo[:, s]).then_inc(stored[s], 16)
                for s in range(2):
                    load(s, s)
                with sp.Fori(1, NGRP // 2) as i:
                    for s in range(2):
                        load(s, i * 2 + s)
                        store(s, i * 2 + s - 2)
                for s in range(2):
                    store(s, NGRP - 2 + s)
                for s in range(2):
                    sp.wait_ge(stored[s], NGRP // 2 * 16)

            @block.gpsimd
            def _(pool):
                g = nc.gpsimd
                g.memset(r_ident16[:, :], 0.0).then_inc(made, 1)
                g.memset(below[:, :], 1.0).then_inc(made, 1)
                g.memset(ones[:, :], 1.0).then_inc(made, 1)
                g.memset(r_neghalf[:, :], -0.5).then_inc(made, 1)
                g.memset(zero_tiles[:, :], 0.0).then_inc(made, 1)
                g.iota(rank_key[:, :], pattern=[[-1, E]], base=E, channel_multiplier=0,
                       allow_small_or_imprecise_dtypes=True).then_inc(made, 1)
                g.memset(filling[:, :, :], 0.0).then_inc(made, 1)
                g.memset(staged[:, :, :, :, C:ROWLEN].rearrange("p s k n a -> p (s k n) a"), 0.0).then_inc(made, 1)
                g.iota(first_row[:, :], pattern=[[room(N), E]], base=0, channel_multiplier=0,
                       allow_small_or_imprecise_dtypes=True).then_inc(made, 1)
                g.iota(tile_row[:, :], pattern=[[ROWS, NR]], base=0, channel_multiplier=0,
                       allow_small_or_imprecise_dtypes=True).then_inc(made, 1)
                g.iota(ids[:, :, :], pattern=[[N, 2], [P, NT]], base=0, channel_multiplier=1).then_inc(made, 1)
                pool.wait_ge(made, 11)
                g.iota(filling[:, :, C:C + 1].bitcast(I32), pattern=[[P, 2 * E * RB], [0, 1]], base=2 * N,
                       channel_multiplier=1).then_inc(made, 1)
                g.affine_select(out=r_ident16[:, :], in_=r_ident16[:, :], compare_op=ALU.not_equal, fill=1.0, base=0,
                                pattern=[[-1, P]], channel_multiplier=1).then_inc(made, 1)
                g.affine_select(out=below[:, :], in_=below[:, :], compare_op=ALU.is_gt, fill=0.0, base=0,
                                pattern=[[1, P]], channel_multiplier=-1).then_inc(made, 1)

                with pool.Fori(0, NGRP // 2) as i:
                    for s in range(2):
                        rows_in, indices = counts(pool, i * 32 + 32, i * 4 + (2 * s + 2))
                        pool.wait_ge(made, 14)
                        pool.wait_ge(staged_in[s], rows_in)
                        pool.wait_ge(index_made, indices)
                        for k in range(2):
                            for n in range(GT):
                                g.indirect_dma_start(
                                    out=xs_dram, out_offset=bass.IndirectOffsetOnAxis(ap=index[:, s, k, n:n + 1], axis=0),
                                    in_=staged[:, s, k, n], in_offset=None).then_inc(scattered[s], 16)

                def step(at):
                    if b := at(-1):
                        products, = counts(pool, b.idx + 1)
                        pool.wait_ge(made, 14)
                        pool.wait_ge(y_made, products)
                        for r in range(RB):
                            g.indirect_dma_start(
                                out=y_dram,
                                out_offset=bass.IndirectOffsetOnAxis(ap=xs[:, b.slot, r, C:C + 1].bitcast(I32), axis=0),
                                in_=ys[:, b.slot, r], in_offset=None).then_inc(y_out[b.slot], 16)
                run_steps(pool, NR, step, -1, 3, XRING)

                def rstd(s, n):
                    variances, powers = counts(pool, n * GT + GT, n)
                    pool.wait_ge(made, 14)
                    pool.wait_ge(zmv_made, variances)
                    wait(pool, zr_made, powers)
                    g.tensor_scalar(zve[:, :], zmv[:, s, :, 1], 1e-5, None, ALU.add).then_inc(zve_made, 1)
                    pool.wait_ge(zve_made, n + 1)
                    if not (isinstance(n, int) and n < 2):
                        pool.wait_ge(zo_made, n * GT - GT)
                    g.tensor_tensor(zr[:, s], zve[:, :], r_neghalf[:, :], ALU.pow).then_inc(zr_made, 1)
                for s in range(2):
                    rstd(s, s)
                with pool.Fori(1, NGRP // 2) as i:
                    for s in range(2):
                        rstd(s, i * 2 + s)

            @block.scalar
            def _(act):
                a = nc.scalar
                act.wait_ge(shifted, 1)
                a.activation(prob[:, :, :].rearrange("p t e -> p (t e)"), left[:, :, :].rearrange("p t e -> p (t e)"),
                             ACT.Exp).then_inc(exp_taken, 1)
                act.wait_ge(w_in, 16 * 4)
                a.activation(w1_split[:, :, 0], w1_raw[:, :, :], ACT.Copy).then_inc(w1_hi, 1)

                def xs_hi(b):
                    act.wait_ge(xs_in[b.slot], b.turn * 16 + 16)
                    wait(act, xsT_ready, b.idx)
                    a.activation(xs_split[:, 0], xs[:, b.slot, :, 0:C], ACT.Copy).then_inc(xs_hi_made, 1)

                def step(at):
                    if b := at(1):
                        act.wait_ge(xsT_ready, b.idx + 1)
                        a.activation(xsT[:, b.par].rearrange("p s t -> p (s t)"), t16[:, 0:2 * ROWS],
                                     ACT.Copy).then_inc(xsT_copied, 1)
                    if b := at(0):
                        e = act.value_load(expert_of[0:1, bass.ds(b.idx, 1)], min_val=0, max_val=E - 1)
                        for c in range(HC):
                            if c % 2 == 0:
                                act.wait_ge(hid_ready, b.idx * 2 + (c // 2 + 1))
                            if c == 0:
                                wait(act, y_ready, b.idx - 1)
                            a.activation(hid[:, b.par, c], ps_h[:, b.par, c // 2, (c % 2) * ROWS:(c % 2 + 1) * ROWS],
                                         ACT.Gelu, bias=b1_sb[:, bass.ds(e * HC + c, 1)]).then_inc(gelu_done, 1)
                    if b := at(2):
                        xs_hi(b)
                act.wait_ge(routed, 2)
                run_steps(act, NR, step, -1, 3, XRING)

                def normalize(s, n):
                    act.wait_ge(zb_made, n + 1)
                    if not (isinstance(n, int) and n < 2):
                        act.wait_ge(stored[s], (n - s) * 8)
                    for k in range(GT):
                        a.activation(zo[:, s, k], z[:, s, k], ACT.Identity, bias=zb[:, s, k:k + 1],
                                     scale=zr[:, s, k:k + 1]).then_inc(zo_made, 1)
                for s in range(2):
                    normalize(s, s)
                with act.Fori(1, NGRP // 2) as i:
                    for s in range(2):
                        normalize(s, i * 2 + s)

            @block.vector
            def _(dve):
                v = nc.vector
                n = [0]

                def link(ins):
                    n[0] += 1
                    ins.then_inc(step_done, 1)
                    dve.wait_ge(step_done, n[0])

                def over_e(a):
                    return a.unsqueeze(2).broadcast_to(cell)

                link(v.tensor_reduce(tmp[:, :], logits[:, :, :], AX.X, ALU.max))
                v.tensor_tensor(left[:, :, :], logits[:, :, :], over_e(tmp[:, :]), ALU.subtract).then_inc(shifted, 1)
                dve.wait_ge(exp_taken, 1)
                link(v.tensor_reduce(tmp[:, :], prob[:, :, :], AX.X, ALU.add))
                link(v.reciprocal(tmp[:, :], tmp[:, :]))
                link(v.tensor_tensor(prob[:, :, :], prob[:, :, :], over_e(tmp[:, :]), ALU.mult))
                dve.wait_ge(made, 14)
                for k in range(2):
                    src = left if k else prob
                    link(v.tensor_reduce(best[:, k], src[:, :, :], AX.X, ALU.max))
                    link(v.tensor_tensor(key[:, :, :], src[:, :, :], over_e(best[:, k]), ALU.is_equal))
                    link(v.tensor_tensor(key[:, :, :], key[:, :, :],
                                         rank_key[:, :].unsqueeze(1).broadcast_to(cell), ALU.mult))
                    link(v.tensor_reduce(tmp[:, :], key[:, :, :], AX.X, ALU.max))
                    link(v.tensor_tensor(pick[k][:, :, :], key[:, :, :], over_e(tmp[:, :]), ALU.is_equal))
                    if k == 0:
                        link(v.scalar_tensor_tensor(out=left[:, :, :].rearrange("p t e -> p (t e)"),
                                                    in0=pick[0][:, :, :].rearrange("p t e -> p (t e)"), scalar=-2.0,
                                                    in1=prob[:, :, :].rearrange("p t e -> p (t e)"),
                                                    op0=ALU.mult, op1=ALU.add))
                v.tensor_tensor(member[:, :, :], pick[0][:, :, :], pick[1][:, :, :], ALU.add).then_inc(counted, 1)
                link(v.tensor_tensor(tmp[:, :], best[:, 0], best[:, 1], ALU.add))
                link(v.tensor_scalar(tmp[:, :], tmp[:, :], 1e-9, None, ALU.add))
                link(v.reciprocal(tmp[:, :], tmp[:, :]))
                link(v.tensor_tensor(top_w[:, :, :], best[:, :, :], tmp[:, :].unsqueeze(1).broadcast_to([P, 2, NT]), ALU.mult))
                dve.wait_ge(counted, 3)
                by_e = ps_y[:, 1, 0:NT * E].rearrange("p (t e) -> p e t", e=E)
                link(v.tensor_copy(total[:, :, :], by_e))
                for e in range(E):
                    ins = v.tensor_tensor_scan(out=upto[:, e], data0=total[:, e], data1=zero_tiles[:, :], initial=0.0,
                                               op0=ALU.add, op1=ALU.add)
                    ins.then_inc(step_done, 1)
                    n[0] += 1
                dve.wait_ge(step_done, n[0])
                link(v.tensor_scalar(count_i[:, :], upto[:, :, NT - 1], float(ROWS - 1), None, ALU.add))
                link(v.tensor_scalar(count_i[:, :], count_i[:, :], ROWS.bit_length() - 1, None, ALU.logical_shift_right))
                link(v.tensor_copy(tiles_f[:, :], count_i[:, :]))
                link(v.tensor_tensor_scan(out=tiles_end[:, :], data0=tiles_f[:, :], data1=zero_tiles[:, 0:E], initial=0.0,
                                          op0=ALU.add, op1=ALU.add))
                link(v.tensor_scalar(tiles_end[:, :], tiles_end[:, :], float(ROWS), None, ALU.mult))
                v.tensor_tensor(fill_row[:, :], upto[:, :, NT - 1], first_row[:, :], ALU.add).then_inc(fill_ready, 1)
                dve.wait_ge(fill_ready, 1)
                link(v.tensor_tensor(upto[:, :, :], upto[:, :, :], total[:, :, :], ALU.subtract))
                link(v.tensor_tensor(upto[:, :, :], upto[:, :, :],
                                     first_row[:, :].unsqueeze(2).broadcast_to([P, E, NT]), ALU.add))
                link(v.tensor_tensor(place[:, :, :], ps_y[:, 0, 0:NT * E].rearrange("p (t e) -> p t e", e=E),
                                     upto[:, :, :].rearrange("p e t -> p t e"), ALU.add))
                for k in range(2):
                    link(v.tensor_tensor(key[:, :, :], pick[k][:, :, :], place[:, :, :], ALU.mult))
                    link(v.tensor_reduce(slot_f[:, k], key[:, :, :], AX.X, ALU.add))
                link(v.tensor_copy(slot[:, :, :], slot_f[:, :, :]))
                link(v.tensor_scalar(spare[:, :], tiles_f[:, :], -float(ROWS), float(room(N)), ALU.mult, ALU.add))
                link(v.tensor_tensor(passed[:, :, :], tile_row[:, :].unsqueeze(2).broadcast_to([P, NR, E]),
                                     tiles_end[:, :].unsqueeze(1).broadcast_to([P, NR, E]), ALU.is_ge))
                link(v.tensor_reduce(expert_f[:, :], passed[:, :, :], AX.X, ALU.add))
                link(v.tensor_tensor(passed[:, :, :], passed[:, :, :],
                                     spare[:, :].unsqueeze(1).broadcast_to([P, NR, E]), ALU.mult))
                link(v.tensor_reduce(row_f[:, :], passed[:, :, :], AX.X, ALU.add))
                link(v.tensor_tensor(row_f[:, :], row_f[:, :], tile_row[:, :], ALU.add))
                v.tensor_copy(row_of[:, :], row_f[:, :]).then_inc(routed, 1)
                v.tensor_scalar(expert_of[:, :], expert_f[:, :], float(E - 1), None, ALU.min).then_inc(routed, 1)

                def stage(s, nn):
                    v.tensor_copy(index[:, s], slot[:, :, bass.ds(nn * GT, GT)]).then_inc(index_made, 1)
                    v.tensor_copy(staged[:, s, :, :, C].bitcast(I32), ids[:, :, bass.ds(nn * GT, GT)]).then_inc(index_made, 1)
                for s in range(2):
                    stage(s, s)
                with dve.Fori(1, NGRP // 2) as i:
                    for s in range(2):
                        dve.wait_ge(scattered[s], i * (2 * GT * 16))
                        stage(s, i * 2 + s)
                dve.wait_ge(w1_hi, 1)
                for e in range(E):
                    v.tensor_tensor(w1_split[:, e, 1], w1_raw[:, e], w1_split[:, e, 0], ALU.subtract).then_inc(w1_lo, 1)

                def step(at):
                    if b := at(2):
                        dve.wait_ge(xs_hi_made, b.idx + 1)
                        v.tensor_tensor(xs_split[:, 1], xs[:, b.slot, :, 0:C], xs_split[:, 0],
                                        ALU.subtract).then_inc(xs_lo_made, 1)
                    if b := at(-1):
                        e = dve.value_load(expert_of[0:1, bass.ds(b.idx, 1)], min_val=0, max_val=E - 1)
                        dve.wait_ge(y_ready, b.idx + 1)
                        wait(dve, y_out[b.slot], b.turn * (16 * RB))
                        bias = b2_sb[:, bass.ds(e, 1), :].broadcast_to([P, RB, C])
                        v.tensor_tensor(ys[:, b.slot], ps_y[:, b.par, 0:RB * C].rearrange("p (r c) -> p r c", r=RB),
                                        bias, ALU.add).then_inc(y_made, 1)
                dve.wait_ge(w_in, 16 * 4)
                run_steps(dve, NR, step, -1, 3, XRING)

                def combine(s, nn, turn):
                    dve.wait_ge(comb_in[s], turn * 48 + 48)
                    if not (isinstance(nn, int) and nn < 2):
                        dve.wait_ge(zo_made, nn * GT - GT)
                    for k in range(GT):
                        v.scalar_tensor_tensor(out=z[:, s, k], in0=y0[:, s, k], scalar=top_w[:, 0, bass.ds(nn * GT + k, 1)],
                                               in1=xr[:, s, k], op0=ALU.mult, op1=ALU.add).then_inc(z_made, 1)
                    dve.wait_ge(z_made, nn * (2 * GT) + GT)
                    for k in range(GT):
                        v.scalar_tensor_tensor(out=z[:, s, k], in0=y1[:, s, k], scalar=top_w[:, 1, bass.ds(nn * GT + k, 1)],
                                               in1=z[:, s, k], op0=ALU.mult, op1=ALU.add).then_inc(z_made, 1)
                    dve.wait_ge(z_made, nn * (2 * GT) + 2 * GT)
                    for k in range(GT):
                        v.bn_stats(zst[:, s, k], z[:, s, k]).then_inc(zst_made, 1)
                    blocks, = counts(dve, nn * GT + GT)
                    dve.wait_ge(made, 14)
                    dve.wait_ge(zst_made, blocks)
                    for k in range(GT):
                        v.bn_aggr(zmv[:, s, k], zst[:, s, k]).then_inc(zmv_made, 1)

                def shift(s, nn):
                    dve.wait_ge(zr_made, nn + 1)
                    v.scalar_tensor_tensor(out=zb[:, s], in0=zmv[:, s, :, 0], scalar=-1.0, in1=zr[:, s],
                                           op0=ALU.mult, op1=ALU.mult).then_inc(zb_made, 1)
                combine(0, 0, 0)
                combine(1, 1, 0)
                shift(0, 0)
                with dve.Fori(1, NGRP // 2) as i:
                    for s in range(2):
                        combine(s, i * 2 + s, i)
                        shift(1 - s, i * 2 + s - 1)
                shift(1, NGRP - 1)

            @block.tensor
            def _(pe):
                t = nc.tensor
                pe.wait_ge(counted, 1)
                pe.wait_ge(made, 14)
                m = member[:, :, :].rearrange("p t e -> p (t e)")
                t.matmul(ps_y[:, 0, 0:NT * E], below[:, :], m, start=True, stop=True).then_inc(counted, 1)
                t.matmul(ps_y[:, 1, 0:NT * E], ones[:, :], m, start=True, stop=True).then_inc(counted, 1)
                pe.wait_ge(w1_hi, 1)
                pe.wait_ge(w1_lo, E)
                pe.wait_ge(w_in, 16 * 4)
                pe.wait_ge(routed, 2)

                def step(at):
                    if b := at(0):
                        e = pe.value_load(expert_of[0:1, bass.ds(b.idx, 1)], min_val=0, max_val=E - 1)
                        pe.wait_ge(xsT_copied, b.idx + 1)
                        for half in range(2):
                            for c in (2 * half, 2 * half + 1):
                                hi, lo = (w1_split[:, bass.ds(e, 1), k, c * P:(c + 1) * P].rearrange("p a n -> p (a n)")
                                          for k in range(2))
                                xh, xl = xsT[:, b.par, 0], xsT[:, b.par, 1]
                                out_ = ps_h[:, b.par, half, (c % 2) * ROWS:(c % 2 + 1) * ROWS]
                                t.matmul(out_, hi, xh, start=True, stop=False)
                                t.matmul(out_, hi, xl, start=False, stop=False)
                                ins = t.matmul(out_, lo, xh, start=False, stop=True)
                            ins.then_inc(hid_ready, 1)
                    if b := at(1):
                        pe.wait_ge(xs_lo_made, b.idx + 1)
                        wait(pe, xsT_copied, b.idx)
                        for k in range(2):
                            for r in range(RB):
                                ins = t.transpose(t16[:, (k * RB + r) * P:(k * RB + r + 1) * P], xs_split[:, k, r],
                                                  r_ident16[:, :])
                        ins.then_inc(xsT_ready, 1)
                    if b := at(-1):
                        e = pe.value_load(expert_of[0:1, bass.ds(b.idx, 1)], min_val=0, max_val=E - 1)
                        pe.wait_ge(gelu_done, b.idx * HC + HC)
                        wait(pe, y_made, b.idx - 1)
                        for r in range(RB):
                            for c in range(HC):
                                w = w2_sb[:, bass.ds(e, 1), c].rearrange("p a n -> p (a n)")
                                ins = t.matmul(ps_y[:, b.par, r * C:(r + 1) * C], hid[:, b.par, c, r * P:(r + 1) * P], w,
                                               start=(c == 0), stop=(c == HC - 1))
                        ins.then_inc(y_ready, 1)
                run_steps(pe, NR, step, -1, 3, XRING)


def program(nc, x, W_kv, g_kv, W_kdec, W_vdec, W_q, W_qdec, W_krope, W_qrope, W_o, gate_wT, w1, b1T, w2, b2,
            cos_t, sin_t, x1_dram, scratch, xs_dram, y_dram, out):
    with nc.sbuf_tensor("logits", [P, RB * x.shape[0], E], F32) as logits:
        attention(nc, logits, x, W_kv, g_kv, W_kdec, W_vdec, W_q, W_qdec, W_krope, W_qrope, W_o, gate_wT, cos_t, sin_t,
                  x1_dram, scratch)
        experts(nc, logits, x1_dram, xs_dram, y_dram, out, w1, b1T, w2, b2)


def rope_tables():
    inv_freq = 1.0 / 10000.0 ** (np.arange(0, DR, 2, dtype=np.float32) / DR)
    freqs = np.outer(np.arange(T, dtype=np.float32), inv_freq)
    angle = np.concatenate([freqs, freqs], -1)
    sign = np.where(np.arange(DR) < DR // 2, -1, 1).astype(np.float32)
    return [np.ascontiguousarray(np.repeat(a.T, 4, 0)).astype(np.float32)
            for a in (np.cos(angle), np.sin(angle) * sign)]


def kernel(**inputs):
    import concourse.bacc as bacc
    from concourse.bass_utils import run_bass_kernel_spmd

    nc = bacc.Bacc("TRN2", target_bir_lowering=False, num_devices=1)
    given = {name.split("_", 2)[2]: np.ascontiguousarray(a) for name, a in inputs.items()}
    arrays = {name: given[name] for name in
              ("x", "W_kv", "g_kv", "W_kdec", "W_vdec", "W_q", "W_qdec", "W_krope", "W_qrope", "W_o")}
    arrays["gate_wT"] = np.ascontiguousarray(given["gate_w"].T)
    arrays["w1"] = given["w1"]
    arrays["b1T"] = np.ascontiguousarray(given["b1"].reshape(E, HC, P).transpose(2, 0, 1)).reshape(P, E * HC)
    arrays["w2"], arrays["b2"] = given["w2"], given["b2"]
    arrays["cos_t"], arrays["sin_t"] = rope_tables()
    args = [nc.dram_tensor(name, a.shape, F32, kind="ExternalInput").ap() for name, a in arrays.items()]
    n = given["x"].shape[0] * T
    for name, shape, dtype in (("x1_dram", given["x"].shape, F32),
                               ("scratch", (RING, 2, 2, P, (NG + 1) * T), F16),
                               ("xs_dram", (E * (room(n) + ROWS), ROWLEN), F32),
                               ("y_dram", (2 * n + 2 * E * ROWS, C), F32)):
        args.append(nc.dram_tensor(name, shape, dtype, kind="Internal").ap())
    args.append(nc.dram_tensor("out", given["x"].shape, F32, kind="ExternalOutput").ap())
    program(nc, *args)
    return run_bass_kernel_spmd(nc, [arrays], core_ids=[0]).results[0]["out"]
```

```python
import numpy as np
from contextlib import ExitStack

import concourse.bass as bass
from concourse import mybir

ALU = mybir.AluOpType
ACT = mybir.ActivationFunctionType
AX = mybir.AxisListType
F32 = mybir.dt.float32
F16 = mybir.dt.float16
BF16 = mybir.dt.bfloat16
I32 = mybir.dt.int32

P = 128
C = 128
T = 256
RB = T // P
H = 16
DC = 8
DR = 32
QR = 64
KR = 32
NG = 4
SROWS = 3 * (DR + DC)
MROW = SROWS
MSCALE = 32768.0
RING = 3
UNITS = 12
STACK = 8 * 16
NLOADS = 23
NCONSTS = 20


E = 8
HID = 512
HC = HID // P
ROWS = RB * P
ROWLEN = C + 4
RANKING = 9
PLACING = 5
GT = 4
CRING = 4
XRING = 6


def route_tiles(n):
    return 2 * n // ROWS + E


def room(n):
    return n + ROWS


class Batch:

    def __init__(self, idx, turn, slot, par):
        self.idx, self.turn, self.slot, self.par = idx, turn, slot, par


def wait(eng, sem, value):
    if isinstance(value, int) and value <= 0:
        return
    eng.wait_ge(sem, value)


def counts(eng, *values):
    return [v if isinstance(v, int) else eng.to_reg(v) for v in values]


def run_steps(eng, nb, step, back=-3, ahead=4, ring=RING):
    def fixed(t):
        def at(d):
            b = t + d
            return Batch(b, b // ring, b % ring, b % 2) if 0 <= b < nb else None
        return at

    first = ring - back
    turns = (nb - ahead - first) // ring
    for t in range(-ahead, first):
        step(fixed(t))
    if turns > 0:
        with eng.Fori(0, turns) as i:
            for q in range(ring):
                def at(d):
                    k = first + q + d
                    return Batch(i * ring + k, i + k // ring, k % ring, k % 2)
                step(at)
    for t in range(first + max(turns, 0) * ring, nb - back):
        step(fixed(t))


def attention(nc, logits, ranks, next_row, x1_all, x, W_kv, g_kv, W_kdec, W_vdec, W_q, W_qdec, W_krope, W_qrope, W_o, gate_wT, cos_t, sin_t, xs_dram, scratch):
    NB = x.shape[0]
    N = NB * T
    SCALE = float(DC + DR) ** -0.5

    with ExitStack() as ctx:
        def sb(name, shape, dt):
            return ctx.enter_context(nc.sbuf_tensor(name, shape, dt))

        def psum(name, shape, dt):
            return ctx.enter_context(nc.psum_tensor(name, shape, dt))

        def sem(name):
            return ctx.enter_context(nc.semaphore(name))

        def ring_sems(name):
            return [sem(f"{name}{i}") for i in range(RING)]

        ps_max = psum("ps_max", [P, 2, 512], F32)
        ps_exp = psum("ps_exp", [P, 2, 512], F32)
        ps_rope = psum("ps_rope", [P, 2, 512], F32)
        ps_proj = psum("ps_proj", [P, 512], F32)
        ps_out = psum("ps_out", [P, 512], F32)

        ident = sb("ident", [P, P], F32)
        ident16 = sb("ident16", [P, P], F16)
        identb = sb("identb", [P, P], BF16)
        causal = sb("causal", [P, 4, P], BF16)
        cos_sb = sb("cos_sb", [P, T], F32)
        sin_sb = sb("sin_sb", [P, T], F32)
        neghalf = sb("neghalf", [P, 2], F32)
        raw = sb("raw", [P, 2, 512], F32)
        raws = sb("raws", [P, 4, P], F32)
        gk = sb("gk", [P, 1], F32)
        w_qkv = sb("w_qkv", [P, 2, QR + KR], F16)
        w_rope = sb("w_rope", [P, 2, 2, 2, NG, P], F16)
        w_qc = sb("w_qc", [P, 2, P], F16)
        w_kv_split = sb("w_kv_split", [P, 2, 2, P], F16)
        w_kv_stack = sb("w_kv_stack", [P, 2, P], F16)
        wo = sb("wo", [P, C], F32)
        gate_t = sb("gate_t", [C, E], F32)
        below = sb("below", [P, P], F16)
        ones = sb("ones", [P, P], F16)
        earlier = sb("earlier", [P, E, E], F32)
        ids = sb("ids", [P, 2, RB * NB], I32)

        x_in = sb("x_in", [P, RING, RB, C], F32)
        x_res = sb("x_res", [P, RING, RB, C], F32)
        x_split = sb("x_split", [P, 2, RB * C], F16)
        xT = sb("xT", [C, RING, 2, T], F16)
        ssq = sb("ssq", [P, RING, RB], F32)
        sq_junk = sb("sq_junk", [P, RB, KR], F32)
        ms = sb("ms", [P, RB], F32)
        rstd_kv = sb("rstd_kv", [P, RB], F32)
        qkv = sb("qkv", [P, RB, QR + KR], F32)
        kvn = sb("kvn", [P, RB, KR], F32)
        qkv_split = sb("qkv_split", [P, RB, 4, QR], F16)
        qkvT = sb("qkvT", [P, RING, 2, T], F16)
        rope_cos = sb("rope_cos", [P, 2, 512], F32)
        rope_sin = sb("rope_sin", [P, 2, 512], F32)
        rope_sum = sb("rope_sum", [P, 2, 512], F32)
        parts = sb("parts", [P, 2, 2, NG + 1, T], F16)
        k_stack = sb("k_stack", [P, RING, H, T], F16)
        q_stack = sb("q_stack", [P, RING, H, T], F16)
        v_aug = sb("v_aug", [P, RING, RB, H, 32], F32)
        row_max = sb("row_max", [P, RB, H], F32)
        neg_max = sb("neg_max", [P, RB, H], F16)
        neg_maxT = sb("neg_maxT", [H, RING, T], F16)
        p0 = sb("p0", [P, H, T], F32)
        p1 = sb("p1", [P, H, P], F32)
        oT = sb("oT", [P, NG, T], F32)
        rden = sb("rden", [P, H], F32)
        on = sb("on", [P, RB, H, DC], F32)
        onT = sb("onT", [P, T], F32)
        resid = sb("resid", [P, RB, C], F32)
        stats = sb("stats", [P, RB, 6], F32)
        mean_var = sb("mean_var", [P, RB, 2], F32)
        rstd1 = sb("rstd1", [P, RB], F32)
        var_eps = sb("var_eps", [P, RB], F32)
        x1 = sb("x1", [P, RING, 2, RB, ROWLEN], F32)
        x1T = sb("x1T", [C, T], F32)
        score = sb("score", [P, RB, E], F32)
        above = sb("above", [P, RB, E, E], F32)
        no_less = sb("no_less", [P, RB, E, E], F32)
        rank = sb("rank", [P, RB, E], F32)
        pick = sb("pick", [P, 2, RB, E], F32)
        member = sb("member", [P, RB, E], F16)
        place = sb("place", [P, RB, E], F32)
        picked = sb("picked", [P, 2, RB, E], F32)
        row_f = sb("row_f", [P, 2, RB], F32)
        row_no = sb("row_no", [P, RING, 2, RB], I32)

        const_in = sem("const_in")
        consts_made = sem("consts_made")
        weights_made = sem("weights_made")
        dve_step = sem("dve_step")
        x_loaded = ring_sems("x_loaded")
        res_loaded = ring_sems("res_loaded")
        x_hi_made = sem("x_hi_made")
        x_lo_made = sem("x_lo_made")
        xT_ready = sem("xT_ready")
        xT_copied = sem("xT_copied")
        qkv_ready = sem("qkv_ready")
        qkv_read = sem("qkv_read")
        ms_made = sem("ms_made")
        rstd_kv_made = sem("rstd_kv_made")
        kvn_made = sem("kvn_made")
        kv_hi_made = sem("kv_hi_made")
        split_made = sem("split_made")
        splitT_ready = sem("splitT_ready")
        splitT_copied = sem("splitT_copied")
        content_ready = sem("content_ready")
        c_hi_made = sem("c_hi_made")
        c_lo_made = sem("c_lo_made")
        v_ready = sem("v_ready")
        v_copied = sem("v_copied")
        rope_a = sem("rope_a")
        rope_b = sem("rope_b")
        cos_done = sem("cos_done")
        sin_done = sem("sin_done")
        sum_done = sem("sum_done")
        r_hi_made = sem("r_hi_made")
        k_lo_made = sem("k_lo_made")
        q_lo_made = sem("q_lo_made")
        parked = [ring_sems("k_parked"), ring_sems("q_parked")]
        stacked = ring_sems("stacked")
        max_in = sem("max_in")
        max_done = sem("max_done")
        neg_max_made = sem("neg_max_made")
        neg_maxT_ready = sem("neg_maxT_ready")
        neg_maxT_copied = sem("neg_maxT_copied")
        max_row_in = ring_sems("max_row_in")
        exp_in = sem("exp_in")
        exp_done = sem("exp_done")
        masked = sem("masked")
        pv_done = sem("pv_done")
        oT_copied = sem("oT_copied")
        o_ready = sem("o_ready")
        rden_made = sem("rden_made")
        norm_done = sem("norm_done")
        onT_ready = sem("onT_ready")
        onT_copied = sem("onT_copied")
        attn_ready = sem("attn_ready")
        resid_made = sem("resid_made")
        stats_made = sem("stats_made")
        var_made = sem("var_made")
        eps_added = sem("eps_added")
        rstd1_made = sem("rstd1_made")
        x1_made = sem("x1_made")
        x1T_ready = sem("x1T_ready")
        x1T_copied = sem("x1T_copied")
        logits_ready = sem("logits_ready")
        logits_copied = sem("logits_copied")
        x1_copied = sem("x1_copied")
        x1_kept = ring_sems("x1_kept")
        ids_set = sem("ids_set")
        ranked = sem("ranked")
        counted = sem("counted")
        placed = sem("placed")
        scattered = ring_sems("scattered")

        f16_proj = ps_proj[:, :].bitcast(F16)

        def rows(b):
            def of(a):
                if isinstance(b.idx, int):
                    return a[b.idx].rearrange("(r p) c -> p r c", p=P)
                return a[bass.ds(b.idx, 1), :, :].rearrange("a (r p) c -> p (a r) c", p=P)
            return of

        with nc.Block() as block:
            def wait_parked(eng, b, side):
                if isinstance(b.idx, int):
                    wait(eng, parked[side][(b.idx - 1) % RING], 16 * ((b.idx - 1) // RING + 1) if b.idx else 0)
                else:
                    eng.wait_ge(parked[side][(b.slot - 1) % RING], (b.turn + (1 if b.slot else 0)) * 16)

            @block.sync
            def _(sp):
                n = [0]

                def load(dst, src):
                    sp.dma_start(dst, src).then_inc(const_in, 16)
                    n[0] += 1
                load(raws[:, 0, 0:QR], W_q)
                load(raws[:, 0, QR:QR + KR], W_kv)
                load(cos_sb[:, :], cos_t)
                load(sin_sb[:, :], sin_t)
                load(raw[:, 0, :], W_krope)
                for k in range(2):
                    load(raw[64 * k:64 * k + 64, 1, :], W_qrope)
                    load(raws[64 * k:64 * k + 64, 1, :], W_qdec)
                for k in range(4):
                    load(raws[32 * k:32 * k + 32, 2, :], W_kdec)
                    load(raws[32 * k:32 * k + 32, 3, :], W_vdec)
                    load(gk[32 * k:32 * k + 32, :], g_kv.rearrange("(p a) -> p a", a=1))
                load(wo[:, :], W_o)
                load(gate_t[:, :], gate_wT)
                assert n[0] == NLOADS

                def park(b, side):
                    dst = scratch[b.slot, side].rearrange("m p n -> p m n")
                    sp.dma_start(dst, parts[:, side].rearrange("p m g t -> p m (g t)")).then_inc(parked[side][b.slot], 16)

                def stack(b, side, tile, at, part, count):
                    src = scratch[b.slot, side, part:part + count].rearrange("m p n -> (m p) n")
                    rope = src[:, 0:NG * T].rearrange("(i j) n -> i j n", j=4)
                    sp.dma_start(tile[DR * at:DR * (at + count), b.slot].rearrange("p (j g) t -> p j (g t)", j=4),
                                 rope).then_inc(stacked[b.slot], 16)
                    first = 3 * DR + DC * at
                    sp.dma_start(tile[first:first + DC * count, b.slot],
                                 src[:, NG * T:].rearrange("(d h) n -> d h n", h=H)).then_inc(stacked[b.slot], 16)

                def step(at):
                    if b := at(4):
                        wait(sp, x_lo_made, b.idx - RING + 1)
                        sp.dma_start(x_in[:, b.slot], rows(b)(x)).then_inc(x_loaded[b.slot], 16)
                    if b := at(0):
                        wait(sp, resid_made, b.idx - RING + 1)
                        sp.dma_start(x_res[:, b.slot], rows(b)(x)).then_inc(res_loaded[b.slot], 16)
                    if b := at(0):
                        wait(sp, neg_maxT_copied, b.idx + 1)
                        sp.dma_start(q_stack[MROW:MROW + 1, b.slot], neg_maxT[:, b.slot]).then_inc(max_row_in[b.slot], 16)
                    if b := at(2):
                        wait(sp, r_hi_made, 4 * b.idx + 4)
                        wait(sp, q_lo_made, 2 * b.idx + 2)
                        park(b, 1)
                    if b := at(2):
                        wait(sp, exp_in, UNITS * (b.idx - RING + 1))
                        wait(sp, consts_made, NCONSTS)
                        for side in range(2):
                            wait(sp, parked[side][b.slot], 16 * (b.turn + 1))
                        stack(b, 0, k_stack, 0, 0, 2)
                        stack(b, 1, q_stack, 0, 0, 1)
                        stack(b, 1, q_stack, 1, 0, 2)
                        stack(b, 0, k_stack, 2, 0, 1)
                    if b := at(-2):
                        wait(sp, x1_made, 2 * b.idx + 2)
                        sp.dma_start(x1_all[:, bass.ds(b.idx * RB, RB)], x1[:, b.slot, 0, :, 0:C]).then_inc(x1_kept[b.slot], 16)
                    if b := at(3):
                        wait(sp, stacked[b.slot], STACK * b.turn)
                        wait(sp, r_hi_made, 4 * b.idx + 2)
                        wait(sp, k_lo_made, 2 * b.idx + 2)
                        wait(sp, c_lo_made, b.idx + 1)
                        park(b, 0)
                run_steps(sp, NB, step)
                for s in range(RING):
                    wait(sp, x1_kept[s], 16 * len(range(s, NB, RING)))

            @block.gpsimd
            def _(pool):
                g = nc.gpsimd
                n = [0]

                def made(ins):
                    ins.then_inc(consts_made, 1)
                    n[0] += 1
                made(g.memset(neghalf[:, :], -0.5))
                for m in (ident, ident16, identb):
                    made(g.memset(m[:, :], 0.0))
                made(g.memset(causal[:, :, :], 0.0))
                made(g.memset(v_aug[:, :, :, :, :], 0.0))
                made(g.memset(below[:, :], 1.0))
                made(g.memset(ones[:, :], 1.0))
                made(g.memset(earlier[:, :, :], 1.0))
                made(g.memset(x1[:, :, :, :, C:ROWLEN].rearrange("p s k r a -> p (s k r) a"), 0.0))
                made(g.iota(next_row[:, :], pattern=[[room(N), E]], base=0, channel_multiplier=0,
                            allow_small_or_imprecise_dtypes=True))
                made(g.iota(ids[:, :, :], pattern=[[N, 2], [P, RB * NB]], base=0, channel_multiplier=1))
                pool.wait_ge(consts_made, n[0])
                made(g.memset(k_stack[96:128, :, :, :], MSCALE))
                pool.wait_ge(consts_made, n[0])
                for m in (ident, ident16, identb):
                    made(g.affine_select(out=m[:, :], in_=m[:, :], compare_op=ALU.not_equal, fill=1.0,
                                         base=0, pattern=[[-1, P]], channel_multiplier=1))
                made(g.affine_select(out=causal[:, :, :], in_=causal[:, :, :], compare_op=ALU.is_ge, fill=-1e30,
                                     base=0, pattern=[[0, 4], [-1, P]], channel_multiplier=1))
                made(g.affine_select(out=below[:, :], in_=below[:, :], compare_op=ALU.is_gt, fill=0.0, base=0,
                                     pattern=[[1, P]], channel_multiplier=-1))
                made(g.affine_select(out=earlier[:, :, :], in_=earlier[:, :, :], compare_op=ALU.is_gt, fill=0.0, base=0,
                                     pattern=[[1, E], [-1, E]], channel_multiplier=0))
                made(g.memset(v_aug[:, :, :, :, DC:DC + 1].rearrange("p s r h a -> p (s r h) a"), 1.0))
                assert n[0] == NCONSTS

                def rope_sum_of(b, n):
                    s = n % 2
                    wait(pool, sin_done, 4 * b.idx + n + 1)
                    wait(pool, r_hi_made, 4 * b.idx + n - 1)
                    if n < 2:
                        wait(pool, q_lo_made, 2 * b.idx - 1 + n)
                    else:
                        wait(pool, k_lo_made, 2 * b.idx + n - 1)
                    g.tensor_tensor(rope_sum[:, s], rope_cos[:, s], rope_sin[:, s], ALU.add).then_inc(sum_done, 1)

                def k_lo(b, n):
                    wait(pool, r_hi_made, 4 * b.idx + n + 1)
                    if n == 0:
                        wait_parked(pool, b, 0)
                    g.tensor_tensor(parts[:, 0, 1, 2 * n:2 * n + 2, :],
                                    rope_sum[:, n].rearrange("p (g t) -> p g t", g=2),
                                    parts[:, 0, 0, 2 * n:2 * n + 2, :], ALU.subtract).then_inc(k_lo_made, 1)

                def mask(b, a):
                    exps, = counts(pool, UNITS * b.idx + 3 * a + 3)
                    pool.wait_ge(consts_made, NCONSTS)
                    wait(pool, exp_done, exps)
                    for k, tile in enumerate((p0[:, 4 * a:4 * a + 4, 0:P], p1[:, 4 * a:4 * a + 4, :])):
                        ins = g.affine_select(out=tile, in_=tile, compare_op=ALU.is_ge, fill=fill0, base=0,
                                              pattern=[[0, 4], [1, P]], channel_multiplier=-1)
                        ins.then_inc(masked, 1)

                def rstd_kv_of(b):
                    reads, used = counts(pool, 4 * b.idx + 4, b.idx)
                    pool.wait_ge(consts_made, NCONSTS)
                    wait(pool, qkv_read, reads)
                    wait(pool, kvn_made, used)
                    g.tensor_scalar(ms[:, :], ssq[:, b.slot], 1.0 / KR, 1e-6, ALU.mult, ALU.add).then_inc(ms_made, 1)
                    wait(pool, ms_made, b.idx + 1)
                    g.tensor_tensor(rstd_kv[:, :], ms[:, :], neghalf[:, :], ALU.pow).then_inc(rstd_kv_made, 1)

                def x_lo(b):
                    wait(pool, x_hi_made, b.idx + 1)
                    g.tensor_tensor(x_split[:, 1], x_in[:, b.slot].rearrange("p r c -> p (r c)"), x_split[:, 0],
                                    ALU.subtract).then_inc(x_lo_made, 1)

                def rstd1_of(b):
                    variances, used = counts(pool, 2 * b.idx + 2, 2 * b.idx)
                    pool.wait_ge(consts_made, NCONSTS)
                    wait(pool, var_made, variances)
                    wait(pool, x1_made, used)
                    g.tensor_scalar(var_eps[:, :], mean_var[:, :, 1], 1e-5, None, ALU.add).then_inc(eps_added, 1)
                    wait(pool, eps_added, b.idx + 1)
                    g.tensor_tensor(rstd1[:, :], var_eps[:, :], neghalf[:, :], ALU.pow).then_inc(rstd1_made, 1)

                def scatter(b, k):
                    placings, copies = counts(pool, PLACING * b.idx + PLACING, b.idx + 1)
                    pool.wait_ge(consts_made, NCONSTS)
                    wait(pool, placed, placings)
                    wait(pool, x1_copied, copies)
                    for r in range(RB):
                        g.indirect_dma_start(
                            out=xs_dram, out_offset=bass.IndirectOffsetOnAxis(ap=row_no[:, b.slot, k, r:r + 1], axis=0),
                            in_=x1[:, b.slot, k, r], in_offset=None).then_inc(scattered[b.slot], 16)

                fill0 = g.to_reg(0.0)

                def step(at):
                    if b := at(3):
                        rstd_kv_of(b)
                    if b := at(-1):
                        mask(b, 2)
                    if b := at(-2):
                        rstd1_of(b)
                    if b := at(3):
                        rope_sum_of(b, 0)
                    if b := at(-1):
                        mask(b, 3)
                    if b := at(3):
                        k_lo(b, 0)
                        rope_sum_of(b, 1)
                    if b := at(4):
                        x_lo(b)
                    if b := at(0):
                        mask(b, 0)
                    if b := at(3):
                        k_lo(b, 1)
                    if b := at(3):
                        rope_sum_of(b, 2)
                    if b := at(0):
                        mask(b, 1)
                    if b := at(-3):
                        scatter(b, 0)
                    if b := at(3):
                        rope_sum_of(b, 3)
                    if b := at(-3):
                        scatter(b, 1)
                run_steps(pool, NB, step)
                for s in range(RING):
                    wait(pool, scattered[s], 64 * len(range(s, NB, RING)))

            @block.scalar
            def _(act):
                a = nc.scalar

                def copy(dst, src):
                    return a.activation(dst, src, ACT.Copy)

                def x_hi(b):
                    act.wait_ge(x_loaded[b.slot], b.turn * 16 + 16)
                    wait(act, xT_ready, b.idx)
                    copy(x_split[:, 0], x_in[:, b.slot].rearrange("p r c -> p (r c)")).then_inc(x_hi_made, 1)

                def xT_copy(b):
                    act.wait_ge(xT_ready, b.idx + 1)
                    copy(xT[:, b.slot].rearrange("p s t -> p (s t)"), f16_proj[:, 0:512]).then_inc(xT_copied, 1)

                def qkv_copy(b):
                    act.wait_ge(qkv_ready, b.idx + 1)
                    wait(act, split_made, 2 * b.idx)
                    pq = ps_proj[:, 0:RB * (QR + KR)].rearrange("p (r n) -> p r n", r=RB)
                    for r in range(RB):
                        a.activation(sq_junk[:, r], pq[:, r, QR:QR + KR], ACT.Square,
                                     accum_out=ssq[:, b.slot, r:r + 1]).then_inc(qkv_read, 1)
                    copy(qkv[:, :, :], pq).then_inc(qkv_read, 1)
                    wait(act, splitT_ready, b.idx)
                    copy(qkv_split[:, :, 0, :], pq[:, :, 0:QR]).then_inc(qkv_read, 1)

                def splitT_copy(b):
                    act.wait_ge(splitT_ready, b.idx + 1)
                    copy(qkvT[:, b.slot].rearrange("p s t -> p (s t)"), f16_proj[:, 0:512]).then_inc(splitT_copied, 1)

                def c_hi_of(b):
                    act.wait_ge(content_ready, b.idx + 1)
                    for side in range(2):
                        wait_parked(act, b, side)
                    copy(parts[:, :, 0, NG], ps_proj[:, :].rearrange("p (s t) -> p s t", s=2)).then_inc(c_hi_made, 1)

                def v_copy(b):
                    act.wait_ge(v_ready, b.idx + 1)
                    copy(v_aug[:, b.slot, :, :, 0:DC].rearrange("p r h d -> p (r h) d"),
                         ps_proj[:, 0:RB * P].rearrange("p (n d) -> p n d", d=DC)).then_inc(v_copied, 1)

                def r_hi_of(b, n):
                    act.wait_ge(sum_done, b.idx * 4 + n + 1)
                    if n % 2 == 0:
                        wait_parked(act, b, n // 2)
                    g = 2 * (n % 2)
                    copy(parts[:, n // 2, 0, g:g + 2, :].rearrange("p g t -> p (g t)"),
                         rope_sum[:, n % 2]).then_inc(r_hi_made, 1)

                def neg_maxT_copy(b):
                    act.wait_ge(neg_maxT_ready, b.idx + 1)
                    copy(neg_maxT[:, b.slot], f16_proj[0:H, 0:T]).then_inc(neg_maxT_copied, 1)

                def exp(b, u):
                    act.wait_ge(exp_in, b.idx * UNITS + u + 1)
                    grp, r = u // 3, u % 3
                    if r == 0:
                        wait(act, pv_done, 2 * b.idx - 1 + grp // 2)
                    if r < 2:
                        dst = p0[:, 4 * grp + 2 * r:4 * grp + 2 * r + 2, :].rearrange("p h t -> p (h t)")
                    else:
                        dst = p1[:, 4 * grp:4 * grp + 4, :].rearrange("p h t -> p (h t)")
                    a.activation(dst, ps_exp[:, u % 2], ACT.Exp, scale=SCALE).then_inc(exp_done, 1)

                def oT_copy(b, half):
                    act.wait_ge(pv_done, b.idx * 2 + half + 1)
                    if half == 0:
                        wait(act, o_ready, 2 * b.idx)
                    copy(oT[:, 2 * half:2 * half + 2, :].rearrange("p g t -> p (g t)"), ps_out[:, :]).then_inc(oT_copied, 1)

                def onT_copy(b):
                    act.wait_ge(onT_ready, b.idx + 1)
                    copy(onT[:, :], ps_out[:, 0:T]).then_inc(onT_copied, 1)

                def x1T_copy(b):
                    act.wait_ge(x1T_ready, b.idx + 1)
                    copy(x1T[:, :], ps_out[:, 0:T]).then_inc(x1T_copied, 1)

                def logits_copy(b):
                    act.wait_ge(logits_ready, b.idx + 1)
                    wait(act, ranked, RANKING * b.idx)
                    src = ps_out[:, 0:RB * E].rearrange("p (r e) -> p r e", r=RB)
                    copy(score[:, :, :], src).then_inc(logits_copied, 1)
                    copy(logits[:, bass.ds(b.idx * RB, RB), :], src).then_inc(logits_copied, 1)

                def x1_copy(b):
                    wait(act, x1_made, 2 * b.idx + 2)
                    wait(act, scattered[b.slot], 64 * b.turn)
                    copy(x1[:, b.slot, 1, :, 0:C], x1[:, b.slot, 0, :, 0:C]).then_inc(x1_copied, 1)

                def step(at):
                    for s in range(UNITS):
                        if s == 3 and (b := at(-1)):
                            oT_copy(b, 0)
                        if s == 5 and (b := at(-2)):
                            x1T_copy(b)
                        if s == 5 and (b := at(3)):
                            c_hi_of(b)
                        if s == 6 and (b := at(-2)):
                            logits_copy(b)
                            x1_copy(b)
                        if s == 7 and (b := at(-1)):
                            oT_copy(b, 1)
                        if s == 11 and (b := at(-1)):
                            onT_copy(b)
                        if b := at(-1 if s < 4 else 0):
                            exp(b, (s - 4) % UNITS)
                        if s == 1 and (b := at(0)):
                            neg_maxT_copy(b)
                        if s == 2 and (b := at(3)):
                            splitT_copy(b)
                        if s == 0 and (b := at(2)):
                            r_hi_of(b, 3)
                        if s == 4 and (b := at(3)):
                            r_hi_of(b, 0)
                        if s == 7 and (b := at(3)):
                            r_hi_of(b, 1)
                        if s == 5 and (b := at(4)):
                            x_hi(b)
                        if s == 8 and (b := at(2)):
                            v_copy(b)
                        if s == 10 and (b := at(4)):
                            xT_copy(b)
                        if s == 10 and (b := at(3)):
                            r_hi_of(b, 2)
                        if s == 11 and (b := at(4)):
                            qkv_copy(b)
                act.wait_ge(consts_made, NCONSTS)
                run_steps(act, NB, step)

            @block.vector
            def _(dve):
                v = nc.vector
                n = [0]

                def link(ins):
                    n[0] += 1
                    ins.then_inc(dve_step, 1)
                    dve.wait_ge(dve_step, n[0])

                def by_dim(a):
                    return a.rearrange("p (h d) -> p d h", h=H)

                dve.wait_ge(const_in, 16 * NLOADS)
                v.tensor_copy(w_qkv[:, 0], raws[:, 0, 0:QR + KR]).then_inc(dve_step, 1)
                n[0] += 1
                for side in range(2):
                    src = raw[:, side].rearrange("p (j g i) -> p g i j", j=4, g=NG)
                    for sw in range(2):
                        hi = w_rope[:, side, sw, 0].rearrange("p g (i j) -> p g i j", j=4)
                        for g in range(NG):
                            for half in range(2):
                                h2 = half ^ sw
                                v.tensor_copy(hi[:, g, 16 * half:16 * half + 16, :],
                                              src[:, g, 16 * h2:16 * h2 + 16, :]).then_inc(dve_step, 1)
                                n[0] += 1
                v.tensor_copy(w_qc[:, 0].rearrange("p (d h) -> p d h", h=H), by_dim(raws[:, 1])).then_inc(dve_step, 1)
                n[0] += 1
                for k in range(2):
                    v.tensor_scalar(raws[:, 2 + k], raws[:, 2 + k], gk[:, 0:1], None, ALU.mult).then_inc(dve_step, 1)
                    n[0] += 1
                dve.wait_ge(dve_step, n[0])
                v.tensor_tensor(w_qkv[:, 1], raws[:, 0, 0:QR + KR], w_qkv[:, 0], ALU.subtract).then_inc(weights_made, 1)
                v.tensor_tensor(w_qc[:, 1].rearrange("p (d h) -> p d h", h=H), by_dim(raws[:, 1]),
                                w_qc[:, 0].rearrange("p (d h) -> p d h", h=H), ALU.subtract).then_inc(weights_made, 1)
                for side in range(2):
                    src = raw[:, side].rearrange("p (j g i) -> p g i j", j=4, g=NG)
                    for sw in range(2):
                        hi = w_rope[:, side, sw, 0].rearrange("p g (i j) -> p g i j", j=4)
                        lo = w_rope[:, side, sw, 1].rearrange("p g (i j) -> p g i j", j=4)
                        for g in range(NG):
                            for half in range(2):
                                h2 = half ^ sw
                                v.tensor_tensor(lo[:, g, 16 * half:16 * half + 16, :],
                                                src[:, g, 16 * h2:16 * h2 + 16, :],
                                                hi[:, g, 16 * half:16 * half + 16, :],
                                                ALU.subtract).then_inc(weights_made, 1)
                def arranged(a, k, head_major):
                    if k:
                        return a
                    return by_dim(a) if head_major else a.rearrange("p (d h) -> p d h", h=H)

                for k in range(2):
                    link(v.tensor_copy(w_kv_split[:, k, 0], raws[:, 2 + k]))
                    link(v.tensor_tensor(w_kv_split[:, k, 1], raws[:, 2 + k], w_kv_split[:, k, 0], ALU.subtract))
                    v.tensor_copy(arranged(w_kv_stack[0:64, k], k, False), arranged(w_kv_split[0:64, k, 0], k, True)).then_inc(weights_made, 1)
                    v.tensor_copy(arranged(w_kv_stack[64:128, k], k, False), arranged(w_kv_split[64:128, k, 1], k, True)).then_inc(weights_made, 1)

                def max_of(b, u):
                    dve.wait_ge(max_in, b.idx * UNITS + u + 1)
                    grp, r = u // 3, u % 3
                    if u == 0:
                        wait(dve, neg_max_made, b.idx)
                    if r < 2:
                        h = 4 * grp + 2 * r
                        v.tensor_reduce(row_max[:, 1, h:h + 2], ps_max[:, u % 2].rearrange("p (h t) -> p h t", h=2),
                                        AX.X, ALU.max).then_inc(max_done, 1)
                    else:
                        v.tensor_reduce(row_max[:, 0, 4 * grp:4 * grp + 4],
                                        ps_max[:, u % 2].rearrange("p (h t) -> p h t", h=4),
                                        AX.X, ALU.max).then_inc(max_done, 1)

                def neg_max_of(b):
                    dve.wait_ge(max_done, b.idx * UNITS + UNITS)
                    wait(dve, neg_maxT_ready, b.idx)
                    v.tensor_scalar(neg_max[:, :, :].rearrange("p r h -> p (r h)"),
                                    row_max[:, :, :].rearrange("p r h -> p (r h)"), -1.0 / MSCALE, None,
                                    ALU.mult).then_inc(neg_max_made, 1)

                def split_q(b):
                    dve.wait_ge(qkv_read, b.idx * 4 + 4)
                    wait(dve, splitT_ready, b.idx)
                    v.tensor_tensor(qkv_split[:, :, 1, :], qkv[:, :, 0:QR], qkv_split[:, :, 0, :],
                                    ALU.subtract).then_inc(split_made, 1)

                def split_kv(b):
                    dve.wait_ge(rstd_kv_made, b.idx + 1)
                    v.tensor_tensor(kvn[:, :, :], qkv[:, :, QR:QR + KR],
                                    rstd_kv[:, :].unsqueeze(2).broadcast_to([P, RB, KR]),
                                    ALU.mult).then_inc(kvn_made, 1)
                    dve.wait_ge(kvn_made, b.idx + 1)
                    twice = kvn[:, :, :].unsqueeze(2).broadcast_to([P, RB, 2, KR])
                    v.tensor_copy(qkv_split[:, :, 2:4, 0:KR], twice).then_inc(kv_hi_made, 1)
                    dve.wait_ge(kv_hi_made, b.idx + 1)
                    v.tensor_tensor(qkv_split[:, :, 2:4, KR:2 * KR], twice, qkv_split[:, :, 2:4, 0:KR],
                                    ALU.subtract).then_inc(split_made, 1)

                def c_lo_of(b):
                    dve.wait_ge(c_hi_made, b.idx + 1)
                    v.tensor_tensor(parts[:, :, 1, NG], ps_proj[:, :].rearrange("p (s t) -> p s t", s=2),
                                    parts[:, :, 0, NG], ALU.subtract).then_inc(c_lo_made, 1)

                def rope(b, n):
                    s = n % 2
                    for sem_in, bank, table, dst, done in ((rope_a, 0, cos_sb, rope_cos, cos_done),
                                                           (rope_b, 1, sin_sb, rope_sin, sin_done)):
                        dve.wait_ge(sem_in, b.idx * 4 + n + 1)
                        wait(dve, sum_done, 4 * b.idx + n - 1)
                        v.tensor_tensor(dst[:, s].rearrange("p (g t) -> p g t", g=2),
                                        ps_rope[:, bank].rearrange("p (g t) -> p g t", g=2),
                                        table[:, :].unsqueeze(1).broadcast_to([P, 2, T]), ALU.mult).then_inc(done, 1)

                def q_lo(b, n):
                    dve.wait_ge(r_hi_made, b.idx * 4 + n + 3)
                    v.tensor_tensor(parts[:, 1, 1, 2 * n:2 * n + 2, :],
                                    rope_sum[:, n].rearrange("p (g t) -> p g t", g=2),
                                    parts[:, 1, 0, 2 * n:2 * n + 2, :], ALU.subtract).then_inc(q_lo_made, 1)

                def norm(b, r):
                    dve.wait_ge(o_ready, b.idx * 2 + r + 1)
                    o = ps_out[:, :].rearrange("p (h n) -> p h n", n=32)
                    v.reciprocal(rden[:, :].unsqueeze(2), o[:, :, DC:DC + 1]).then_inc(rden_made, 1)
                    dve.wait_ge(rden_made, b.idx * 2 + r + 1)
                    v.tensor_tensor(on[:, r], o[:, :, 0:DC], rden[:, :].unsqueeze(2).broadcast_to([P, H, DC]),
                                    ALU.mult).then_inc(norm_done, 1)

                def resid_of(b):
                    dve.wait_ge(attn_ready, b.idx + 1)
                    dve.wait_ge(res_loaded[b.slot], b.turn * 16 + 16)
                    v.tensor_tensor(resid[:, :, :].rearrange("p r c -> p (r c)"), ps_out[:, 0:RB * C],
                                    x_res[:, b.slot].rearrange("p r c -> p (r c)"), ALU.add).then_inc(resid_made, 1)
                    dve.wait_ge(resid_made, b.idx + 1)
                    for r in range(RB):
                        v.bn_stats(stats[:, r], resid[:, r]).then_inc(stats_made, 1)
                    halves, = counts(dve, b.idx * 2 + 2)
                    dve.wait_ge(const_in, 16 * NLOADS)
                    dve.wait_ge(stats_made, halves)
                    for r in range(RB):
                        v.bn_aggr(mean_var[:, r], stats[:, r]).then_inc(var_made, 1)

                def x1_of(b):
                    dve.wait_ge(rstd1_made, b.idx + 1)
                    wait(dve, x1_kept[b.slot], 16 * b.turn)
                    wait(dve, scattered[b.slot], 64 * b.turn)
                    v.tensor_copy(x1[:, b.slot, :, :, C].bitcast(I32), ids[:, :, bass.ds(b.idx * RB, RB)]).then_inc(ids_set, 1)
                    for r in range(RB):
                        v.tensor_scalar(x1[:, b.slot, 0, r, 0:C], resid[:, r], mean_var[:, r, 0:1], rstd1[:, r:r + 1],
                                        ALU.subtract, ALU.mult).then_inc(x1_made, 1)

                def compare(b):
                    dve.wait_ge(logits_copied, 2 * b.idx + 1)
                    wait(dve, ranked, RANKING * b.idx)
                    f, e = (score[:, :, :].unsqueeze(a).broadcast_to([P, RB, E, E]) for a in (2, 3))
                    v.tensor_tensor(above[:, :, :, :], f, e, ALU.is_gt).then_inc(ranked, 1)
                    v.tensor_tensor(no_less[:, :, :, :], f, e, ALU.is_ge).then_inc(ranked, 1)

                def break_ties(b):
                    wait(dve, ranked, RANKING * b.idx + 2)
                    v.tensor_tensor(no_less[:, :, :, :], no_less[:, :, :, :],
                                    earlier[:, :, :].unsqueeze(1).broadcast_to([P, RB, E, E]), ALU.mult).then_inc(ranked, 1)

                def rank_above(b):
                    wait(dve, ranked, RANKING * b.idx + 3)
                    v.tensor_tensor(above[:, :, :, :], above[:, :, :, :], no_less[:, :, :, :], ALU.max).then_inc(ranked, 1)

                def rank_of(b):
                    wait(dve, ranked, RANKING * b.idx + 4)
                    v.tensor_reduce(rank[:, :, :], above[:, :, :, :], AX.X, ALU.add).then_inc(ranked, 1)

                def picks(b):
                    wait(dve, ranked, RANKING * b.idx + 5)
                    wait(dve, counted, b.idx)
                    wait(dve, placed, PLACING * b.idx)
                    v.tensor_scalar(member[:, :, :], rank[:, :, :], 1.5, None, ALU.is_lt).then_inc(ranked, 1)
                    for k in range(2):
                        v.tensor_scalar(pick[:, k], rank[:, :, :], float(k), None, ALU.is_equal).then_inc(ranked, 1)
                    v.tensor_copy(ranks[:, bass.ds(b.idx * RB, RB), :], rank[:, :, :]).then_inc(ranked, 1)

                def place_of(b):
                    dve.wait_ge(counted, b.idx + 1)
                    wait(dve, placed, PLACING * b.idx)
                    v.tensor_tensor(place[:, :, :], ps_proj[:, 0:RB * E].rearrange("p (r e) -> p r e", r=RB),
                                    next_row[:, :].unsqueeze(1).broadcast_to([P, RB, E]), ALU.add).then_inc(placed, 1)
                    wait(dve, placed, PLACING * b.idx + 1)
                    v.tensor_tensor(next_row[:, :], ps_proj[:, RB * E:(RB + 1) * E], next_row[:, :], ALU.add).then_inc(placed, 1)

                def picked_of(b):
                    wait(dve, placed, PLACING * b.idx + 2)
                    wait(dve, ranked, RANKING * b.idx + RANKING)
                    v.tensor_tensor(picked[:, :, :, :], pick[:, :, :, :],
                                    place[:, :, :].unsqueeze(1).broadcast_to([P, 2, RB, E]), ALU.mult).then_inc(placed, 1)

                def row_no_of(b):
                    wait(dve, placed, PLACING * b.idx + 3)
                    wait(dve, scattered[b.slot], 64 * b.turn)
                    v.tensor_reduce(row_f[:, :, :], picked[:, :, :, :], AX.X, ALU.add).then_inc(placed, 1)
                    wait(dve, placed, PLACING * b.idx + 4)
                    v.tensor_copy(row_no[:, b.slot], row_f[:, :, :]).then_inc(placed, 1)

                def step(at):
                    for s in range(UNITS):
                        if b := at(1):
                            max_of(b, s)
                        if s == 7 and (b := at(-2)):
                            compare(b)
                        if s == 9 and (b := at(-2)):
                            break_ties(b)
                        if s == 11 and (b := at(-2)):
                            rank_above(b)
                        if s == 1 and (b := at(-3)):
                            rank_of(b)
                        if s == 3 and (b := at(-3)):
                            picks(b)
                        if s == 7 and (b := at(-3)):
                            place_of(b)
                        if s == 8 and (b := at(-3)):
                            picked_of(b)
                        if s == 9 and (b := at(-3)):
                            row_no_of(b)
                        if s == 0 and (b := at(3)):
                            split_q(b)
                        if s == 0 and (b := at(-2)):
                            resid_of(b)
                        if s == 0 and (b := at(3)):
                            split_kv(b)
                        if s == 2 and (b := at(-2)):
                            x1_of(b)
                        if s == 1 and (b := at(3)):
                            rope(b, 0)
                        if s == 4 and (b := at(3)):
                            rope(b, 1)
                        if s == 5 and (b := at(3)):
                            c_lo_of(b)
                        if s == 7 and (b := at(3)):
                            rope(b, 2)
                        if s == 8 and (b := at(-1)):
                            norm(b, 0)
                        if s == 10 and (b := at(3)):
                            rope(b, 3)
                        if s == 10 and (b := at(-1)):
                            norm(b, 1)
                        if s == 11 and (b := at(1)):
                            neg_max_of(b)
                        if s == 11 and (b := at(3)):
                            q_lo(b, 0)
                        if s == 1 and (b := at(2)):
                            q_lo(b, 1)
                run_steps(dve, NB, step)

            @block.tensor
            def _(pe):
                t = nc.tensor
                pe.wait_ge(consts_made, NCONSTS)
                pe.wait_ge(weights_made, 38)
                pe.wait_ge(const_in, 16 * NLOADS)

                def group(out, terms, sem_done=None):
                    for k, (l, r) in enumerate(terms):
                        ins = t.matmul(out, l, r, start=(k == 0), stop=(k == len(terms) - 1))
                    return ins

                def xT_of(b):
                    pe.wait_ge(x_lo_made, b.idx + 1)
                    wait(pe, v_copied, b.idx - 1)
                    if isinstance(b.idx, int) and b.idx < 2:
                        wait(pe, c_lo_made, b.idx)
                    for k in range(2):
                        for r in range(RB):
                            ins = t.transpose(f16_proj[:, (2 * k + r) * P:(2 * k + r + 1) * P],
                                              x_split[:, k, r * C:(r + 1) * C], ident16[:, :])
                    ins.then_inc(xT_ready, 1)

                def qkv_of(b):
                    pe.wait_ge(xT_copied, b.idx + 1)
                    for r in range(RB):
                        hi, lo = (xT[:, b.slot, k, r * P:(r + 1) * P] for k in range(2))
                        ins = group(ps_proj[:, r * (QR + KR):(r + 1) * (QR + KR)],
                                    [(hi, w_qkv[:, 0]), (lo, w_qkv[:, 0]), (hi, w_qkv[:, 1])])
                    ins.then_inc(qkv_ready, 1)

                def neg_maxT_of(b, more):
                    pe.wait_ge(neg_max_made, b.idx + 1)
                    if more:
                        pe.wait_ge(qkv_read, b.idx * 4 + 16)
                    else:
                        wait(pe, v_copied, min(b.idx + 2, NB))
                        wait(pe, placed, PLACING * (b.idx - 4) + 2)
                    for r in range(RB):
                        ins = t.transpose(f16_proj[0:H, r * P:(r + 1) * P], neg_max[:, r], ident16[:, :])
                    ins.then_inc(neg_maxT_ready, 1)

                def splitT_of(b):
                    pe.wait_ge(split_made, b.idx * 2 + 2)
                    pe.wait_ge(qkv_read, b.idx * 4 + 4)
                    wait(pe, neg_maxT_copied, b.idx - 2)
                    for k in range(2):
                        for r in range(RB):
                            ins = t.transpose(f16_proj[:, (2 * k + r) * P:(2 * k + r + 1) * P],
                                              qkv_split[:, r, 2 * k:2 * k + 2, :].rearrange("p a n -> p (a n)"),
                                              ident16[:, :])
                    ins.then_inc(splitT_ready, 1)

                def content(b):
                    pe.wait_ge(splitT_copied, b.idx + 1)
                    t.matmul(ps_proj[:, 0:T], w_kv_stack[:, 0], qkvT[:, b.slot, 1], start=True, stop=True)
                    group(ps_proj[:, T:2 * T], [(w_qc[:, k], qkvT[:, b.slot, 0]) for k in range(2)]).then_inc(content_ready, 1)

                def counts_of(b, at):
                    wait(pe, ranked, RANKING * b.idx + 6)
                    if at(3):
                        pe.wait_ge(c_lo_made, b.idx + 7)
                    else:
                        wait(pe, c_lo_made, NB)
                        wait(pe, v_copied, at(2).idx if at(2) else NB)
                        wait(pe, neg_maxT_copied, at(0).idx + 1 if at(0) else NB)
                        wait(pe, placed, PLACING * (b.idx - 1) + 2)
                    t.matmul(ps_proj[:, 0:E], below[:, :], member[:, 0], start=True, stop=True)
                    group(ps_proj[:, E:2 * E], [(below[:, :], member[:, 1]), (ones[:, :], member[:, 0])])
                    group(ps_proj[:, 2 * E:3 * E], [(ones[:, :], member[:, r]) for r in range(RB)]).then_inc(counted, 1)

                def v_of(b, more):
                    pe.wait_ge(c_lo_made, b.idx + (2 if more else 1))
                    wait(pe, placed, PLACING * (b.idx - 5) + 2)
                    for r in range(RB):
                        ins = t.matmul(ps_proj[:, r * P:(r + 1) * P], qkvT[:, b.slot, 1, r * P:(r + 1) * P],
                                       w_kv_stack[:, 1], start=True, stop=True)
                    ins.then_inc(v_ready, 1)

                def rope(b, n):
                    side = n // 2
                    if side:
                        pe.wait_ge(splitT_copied, b.idx + 1)
                    for sw, read, done in ((0, cos_done, rope_a), (1, sin_done, rope_b)):
                        wait(pe, read, 4 * b.idx + n)
                        for k in range(2):
                            g = 2 * (n % 2) + k
                            hi, lo = (w_rope[:, side, sw, m, g] for m in range(2))
                            if side == 0:
                                xh, xl = xT[:, b.slot, 0], xT[:, b.slot, 1]
                                terms = [(hi, xh), (hi, xl), (lo, xh)]
                            else:
                                terms = [(hi, qkvT[:, b.slot, 0]), (lo, qkvT[:, b.slot, 0])]
                            ins = group(ps_rope[:, sw, k * T:(k + 1) * T], terms)
                        ins.then_inc(done, 1)

                def scores_max(b, u):
                    if u == 0:
                        pe.wait_ge(stacked[b.slot], b.turn * STACK + STACK)
                    wait(pe, max_done, UNITS * b.idx + u - 1)
                    grp, r = u // 3, u % 3
                    bank = ps_max[:, u % 2]
                    ks, qs = k_stack[0:SROWS, b.slot], q_stack[0:SROWS, b.slot]
                    if r < 2:
                        for k in range(2):
                            h = 4 * grp + 2 * r + k
                            t.matmul(bank[:, k * T:(k + 1) * T], qs[:, h, P:T], ks[:, h, :], start=(k == 0), stop=False,
                                     skip_group_check=True)
                        ins = t.matmul(bank.rearrange("p (h t) -> p h t", h=2)[:, :, P:T], identb[:, :],
                                       causal[:, 0:2, :], start=False, stop=True, skip_group_check=True)
                    else:
                        for k in range(4):
                            h = 4 * grp + k
                            t.matmul(bank[:, k * P:(k + 1) * P], qs[:, h, 0:P], ks[:, h, 0:P], start=(k == 0), stop=False,
                                     skip_group_check=True)
                        ins = t.matmul(bank, identb[:, :], causal[:, :, :].rearrange("p a t -> p (a t)"),
                                       start=False, stop=True, skip_group_check=True)
                    ins.then_inc(max_in, 1)

                def scores_exp(b, u):
                    if u == 0:
                        pe.wait_ge(max_row_in[b.slot], b.turn * 16 + 16)
                    wait(pe, exp_done, UNITS * b.idx + u - 1)
                    grp, r = u // 3, u % 3
                    bank = ps_exp[:, u % 2]
                    ks, qs = k_stack[0:SROWS + 1, b.slot], q_stack[0:SROWS + 1, b.slot]
                    if r < 2:
                        for k in range(2):
                            h = 4 * grp + 2 * r + k
                            ins = t.matmul(bank[:, k * T:(k + 1) * T], ks[:, h, 0:P], qs[:, h, :], start=True, stop=True)
                    else:
                        for k in range(4):
                            h = 4 * grp + k
                            ins = t.matmul(bank[:, k * P:(k + 1) * P], ks[:, h, P:T], qs[:, h, P:T], start=True, stop=True)
                    ins.then_inc(exp_in, 1)

                def pv(b, half):
                    pe.wait_ge(masked, b.idx * 8 + 4 * half + 4)
                    if half == 0:
                        wait(pe, resid_made, b.idx)
                    else:
                        wait(pe, logits_copied, 2 * b.idx)
                        pe.wait_ge(oT_copied, b.idx * 2 + 1)
                    for k in range(2):
                        for j in range(4):
                            h = 4 * (2 * half + k) + j
                            out = ps_out[32 * j:32 * j + 32, k * T:(k + 1) * T]
                            t.matmul(out, v_aug[:, b.slot, 0, h], p0[:, h, :], start=True, stop=False, skip_group_check=True)
                        for j in range(4):
                            h = 4 * (2 * half + k) + j
                            out = ps_out[32 * j:32 * j + 32, k * T:(k + 1) * T]
                            ins = t.matmul(out[:, P:T], v_aug[:, b.slot, 1, h], p1[:, h, :], start=False, stop=True,
                                           skip_group_check=True)
                    ins.then_inc(pv_done, 1)

                def o_of(b, r):
                    if r == 0:
                        pe.wait_ge(oT_copied, b.idx * 2 + 2)
                    else:
                        pe.wait_ge(norm_done, b.idx * 2 + 1)
                    for g in range(NG):
                        ins = t.transpose(ps_out[:, g * P:(g + 1) * P], oT[:, g, r * P:(r + 1) * P], ident[:, :])
                    ins.then_inc(o_ready, 1)

                def onT_of(b):
                    pe.wait_ge(norm_done, b.idx * 2 + 2)
                    for r in range(RB):
                        ins = t.transpose(ps_out[:, r * P:(r + 1) * P], on[:, r].rearrange("p h d -> p (h d)"), ident[:, :])
                    ins.then_inc(onT_ready, 1)

                def attn(b):
                    pe.wait_ge(onT_copied, b.idx + 1)
                    for r in range(RB):
                        ins = t.matmul(ps_out[:, r * C:(r + 1) * C], onT[:, r * P:(r + 1) * P], wo[:, :], start=True, stop=True)
                    ins.then_inc(attn_ready, 1)

                def x1T_of(b, more):
                    pe.wait_ge(x1_made, b.idx * 2 + 2)
                    if more:
                        pe.wait_ge(oT_copied, b.idx * 2 + 3)
                    for r in range(RB):
                        ins = t.transpose(ps_out[:, r * P:(r + 1) * P], x1[:, b.slot, 0, r, 0:C], ident[:, :])
                    ins.then_inc(x1T_ready, 1)

                def logits_of(b):
                    pe.wait_ge(x1T_copied, b.idx + 1)
                    for r in range(RB):
                        ins = t.matmul(ps_out[:, r * 8:(r + 1) * 8], x1T[:, r * P:(r + 1) * P], gate_t[:, :],
                                       start=True, stop=True)
                    ins.then_inc(logits_ready, 1)

                def step(at):
                    for s in range(UNITS):
                        if b := at(1):
                            scores_max(b, s)
                        if b := at(-1 if s < 4 else 0):
                            scores_exp(b, (s - 4) % UNITS)
                        if s == 0 and (b := at(3)):
                            rope(b, 0)
                        if s == 1 and (b := at(0)):
                            neg_maxT_of(b, at(3) is not None)
                        if s == 2 and (b := at(3)):
                            splitT_of(b)
                        if s == 2 and (b := at(-1)):
                            pv(b, 0)
                        if s == 3 and (b := at(3)):
                            rope(b, 1)
                        if s == 4 and (b := at(-2)):
                            x1T_of(b, at(-1) is not None)
                        if s == 4 and (b := at(3)):
                            content(b)
                        if s == 5 and (b := at(-2)):
                            logits_of(b)
                        if s == 6 and (b := at(3)):
                            rope(b, 2)
                        if s == 6 and (b := at(-1)):
                            pv(b, 1)
                        if s == 7 and (b := at(-1)):
                            o_of(b, 0)
                        if s == 6 and (b := at(-3)):
                            counts_of(b, at)
                        if s == 8 and (b := at(2)):
                            v_of(b, at(3) is not None)
                        if s == 9 and (b := at(3)):
                            rope(b, 3)
                        if s == 9 and (b := at(-1)):
                            o_of(b, 1)
                        if s == 10 and (b := at(4)):
                            xT_of(b)
                        if s == 10 and (b := at(-1)):
                            onT_of(b)
                        if s == 11 and (b := at(-1)):
                            attn(b)
                        if s == 11 and (b := at(4)):
                            qkv_of(b)
                run_steps(pe, NB, step)


def experts(nc, logits, ranks, next_row, x1_all, xs_dram, y_dram, out, w1, b1T, w2, b2):
    N = out.shape[0] * out.shape[1]
    NT = N // P
    NR = route_tiles(N)
    NGRP = NT // GT

    with ExitStack() as ctx:
        def sb(name, shape, dt):
            return ctx.enter_context(nc.sbuf_tensor(name, shape, dt))

        def psum(name, shape, dt):
            return ctx.enter_context(nc.psum_tensor(name, shape, dt))

        def sem(name):
            return ctx.enter_context(nc.semaphore(name))

        def ring_sems(name, n):
            return [sem(f"{name}{i}") for i in range(n)]

        w1_raw = sb("w1_raw", [C, E, HID], F32)
        w1_split = sb("w1_split", [C, E, 2, HID], F16)
        w2_sb = sb("w2_sb", [P, E, HC, C], F32)
        b1_sb = sb("b1_sb", [P, E * HC], F32)
        b2_sb = sb("b2_sb", [P, E, C], F32)
        r_ident16 = sb("r_ident16", [P, P], F16)
        tile_row = sb("tile_row", [P, NR], F32)
        first_row = sb("first_row", [P, E], F32)
        filling = sb("filling", [P, 2 * E * RB, ROWLEN], F32)
        r_neghalf = sb("r_neghalf", [P, GT], F32)
        zeros = sb("zeros", [P, E], F32)
        prob = sb("prob", [P, NT, E], F32)
        second = sb("second", [P, NT, E], F32)
        largest = sb("largest", [P, NT], F32)
        total = sb("total", [P, NT], F32)
        best = sb("best", [P, 2, NT], F32)
        top_w = sb("top_w", [P, 2, NT], F32)
        fill_row = sb("fill_row", [P, E], I32)
        count_f = sb("count_f", [P, E], F32)
        count_i = sb("count_i", [P, E], I32)
        tiles_f = sb("tiles_f", [P, E], F32)
        tiles_end = sb("tiles_end", [P, E], F32)
        spare = sb("spare", [P, E], F32)
        passed = sb("passed", [P, NR, E], F32)
        row_f = sb("row_tile_f", [P, NR], F32)
        row_of = sb("row_of", [P, NR], I32)
        expert_f = sb("expert_f", [P, NR], F32)
        expert_of = sb("expert_of", [P, NR], I32)
        xs = sb("xs", [P, XRING, RB, ROWLEN], F32)
        xs_split = sb("xs_split", [P, 2, RB, C], F16)
        xsT = sb("xsT", [C, 2, 2, ROWS], F16)
        hid = sb("hid", [P, 2, HC, ROWS], F32)
        ys = sb("ys", [P, XRING, RB, C], F32)
        y0 = sb("y0", [P, CRING, GT, C], F32)
        y1 = sb("y1", [P, CRING, GT, C], F32)
        z = sb("z", [P, CRING, GT, C], F32)
        zst = sb("zst", [P, CRING, GT, 6], F32)
        zmv = sb("zmv", [P, CRING, GT, 2], F32)
        zve = sb("zve", [P, CRING, GT], F32)
        zr = sb("zr", [P, CRING, GT], F32)
        zb = sb("zb", [P, CRING, GT], F32)
        zo = sb("zo", [P, CRING, GT, C], F32)

        ps_t = psum("ps_t", [P, 512], F32)
        ps_h = psum("ps_h", [P, 2, 2, 512], F32)
        ps_y = psum("ps_y", [P, 2, 512], F32)
        t16 = ps_t[:, :].bitcast(F16)

        w_in = sem("w_in")
        made = sem("made")
        step_done = sem("step_done")
        shifted = sem("shifted")
        exp_taken = sem("exp_taken")
        routed = sem("routed")
        fill_ready = sem("fill_ready")
        filled = sem("filled")
        w1_hi = sem("w1_hi")
        w1_lo = sem("w1_lo")
        xs_in = ring_sems("xs_in", XRING)
        xs_hi_made = sem("xs_hi_made")
        xs_lo_made = sem("xs_lo_made")
        xsT_ready = sem("xsT_ready")
        xsT_copied = sem("xsT_copied")
        hid_ready = sem("hid_ready")
        gelu_done = sem("gelu_done")
        y_ready = sem("y_ready")
        y_made = sem("y_made")
        y_out = ring_sems("y_out", XRING)
        comb_in = ring_sems("comb_in", CRING)
        z_made = sem("z_made")
        zst_made = sem("zst_made")
        zmv_made = sem("zmv_made")
        zve_made = sem("zve_made")
        zr_made = sem("zr_made")
        zb_made = sem("zb_made")
        zo_made = sem("zo_made")
        stored = ring_sems("stored", CRING)

        out_rows = out.rearrange("b t c -> (b t) c")

        def tiles_at(a, first, n):
            return a[bass.ds(first * P, n * P), :].rearrange("(n p) c -> p n c", p=P)

        def rows_at(a, row):
            return a[bass.ds(row, ROWS), :].rearrange("(r p) c -> p r c", p=P)

        with nc.Block() as block:
            @block.sync
            def _(sp):
                for dst, src in ((w1_raw[:, :, :], w1.rearrange("e d h -> d e h")),
                                 (w2_sb[:, :, :, :], w2.rearrange("e (c p) d -> p e c d", p=P)),
                                 (b1_sb[:, :], b1T),
                                 (b2_sb[:, :, :].rearrange("p e c -> p (e c)"),
                                  b2.rearrange("e c -> (e c)").partition_broadcast(P))):
                    sp.dma_start(dst, src).then_inc(w_in, 16)

                sp.wait_ge(made, 8)
                sp.wait_ge(fill_ready, 1)
                for e in range(E):
                    row = sp.value_load(fill_row[0:1, e:e + 1], min_val=0, max_val=E * room(N))
                    sp.dma_start(rows_at(xs_dram, row), filling[:, e * RB:(e + 1) * RB]).then_inc(filled, 16)
                sp.dma_start(xs_dram[E * room(N):].rearrange("(r p) c -> p r c", p=P),
                             filling[:, E * RB:]).then_inc(filled, 16)

                def step(at):
                    if b := at(3):
                        wait(sp, y_out[b.slot], 16 * RB * b.turn)
                        row = sp.value_load(row_of[0:1, bass.ds(b.idx, 1)], min_val=0, max_val=E * (room(N) + ROWS) - ROWS)
                        sp.dma_start(xs[:, b.slot], rows_at(xs_dram, row)).then_inc(xs_in[b.slot], 16)
                sp.wait_ge(filled, 16 * (E + 1))
                sp.wait_ge(routed, 2)
                run_steps(sp, NR, step, -1, 3, XRING)
                for s in range(XRING):
                    sp.wait_ge(y_out[s], 16 * RB * len(range(s, NR, XRING)))

                def step(at):
                    if b := at(2):
                        wait(sp, z_made, (b.idx - CRING + 1) * (2 * GT))
                        for dst, first in ((y0, 0), (y1, N)):
                            sp.dma_start(dst[:, b.slot], tiles_at(y_dram[first:first + N], b.idx * GT, GT)
                                         ).then_inc(comb_in[b.slot], 16)
                    if b := at(-1):
                        wait(sp, zo_made, b.idx * GT + GT)
                        sp.dma_start(tiles_at(out_rows, b.idx * GT, GT), zo[:, b.slot]).then_inc(stored[b.slot], 16)
                run_steps(sp, NGRP, step, -1, 2, CRING)
                for s in range(CRING):
                    wait(sp, stored[s], 16 * len(range(s, NGRP, CRING)))

            @block.gpsimd
            def _(pool):
                g = nc.gpsimd
                g.memset(r_ident16[:, :], 0.0).then_inc(made, 1)
                g.memset(r_neghalf[:, :], -0.5).then_inc(made, 1)
                g.memset(zeros[:, :], 0.0).then_inc(made, 1)
                g.memset(filling[:, :, :], 0.0).then_inc(made, 1)
                g.iota(first_row[:, :], pattern=[[room(N), E]], base=0, channel_multiplier=0,
                       allow_small_or_imprecise_dtypes=True).then_inc(made, 1)
                g.iota(tile_row[:, :], pattern=[[ROWS, NR]], base=0, channel_multiplier=0,
                       allow_small_or_imprecise_dtypes=True).then_inc(made, 1)
                pool.wait_ge(made, 6)
                g.iota(filling[:, :, C:C + 1].bitcast(I32), pattern=[[P, 2 * E * RB], [0, 1]], base=2 * N,
                       channel_multiplier=1).then_inc(made, 1)
                g.affine_select(out=r_ident16[:, :], in_=r_ident16[:, :], compare_op=ALU.not_equal, fill=1.0, base=0,
                                pattern=[[-1, P]], channel_multiplier=1).then_inc(made, 1)

                def step(at):
                    if b := at(-1):
                        products, = counts(pool, b.idx + 1)
                        pool.wait_ge(made, 8)
                        pool.wait_ge(y_made, products)
                        for r in range(RB):
                            g.indirect_dma_start(
                                out=y_dram,
                                out_offset=bass.IndirectOffsetOnAxis(ap=xs[:, b.slot, r, C:C + 1].bitcast(I32), axis=0),
                                in_=ys[:, b.slot, r], in_offset=None).then_inc(y_out[b.slot], 16)
                run_steps(pool, NR, step, -1, 3, XRING)

                def step(at):
                    if b := at(0):
                        variances, used = counts(pool, b.idx * GT + GT, b.idx - CRING + 1)
                        pool.wait_ge(made, 8)
                        pool.wait_ge(zmv_made, variances)
                        wait(pool, zr_made, used)
                        g.tensor_scalar(zve[:, b.slot], zmv[:, b.slot, :, 1], 1e-5, None, ALU.add).then_inc(zve_made, 1)
                        pool.wait_ge(zve_made, b.idx + 1)
                        wait(pool, zo_made, (b.idx - CRING + 1) * GT)
                        g.tensor_tensor(zr[:, b.slot], zve[:, b.slot], r_neghalf[:, :], ALU.pow).then_inc(zr_made, 1)
                run_steps(pool, NGRP, step, -1, 2, CRING)

            @block.scalar
            def _(act):
                a = nc.scalar
                act.wait_ge(shifted, 1)
                a.activation(prob[:, :, :], prob[:, :, :], ACT.Exp).then_inc(exp_taken, 1)
                act.wait_ge(w_in, 16 * 4)
                a.activation(w1_split[:, :, 0], w1_raw[:, :, :], ACT.Copy).then_inc(w1_hi, 1)

                def xs_hi(b):
                    act.wait_ge(xs_in[b.slot], b.turn * 16 + 16)
                    wait(act, xsT_ready, b.idx)
                    a.activation(xs_split[:, 0], xs[:, b.slot, :, 0:C], ACT.Copy).then_inc(xs_hi_made, 1)

                def step(at):
                    if b := at(1):
                        act.wait_ge(xsT_ready, b.idx + 1)
                        a.activation(xsT[:, b.par].rearrange("p s t -> p (s t)"), t16[:, 0:2 * ROWS],
                                     ACT.Copy).then_inc(xsT_copied, 1)
                    if b := at(0):
                        e = act.value_load(expert_of[0:1, bass.ds(b.idx, 1)], min_val=0, max_val=E - 1)
                        for c in range(HC):
                            if c % 2 == 0:
                                act.wait_ge(hid_ready, b.idx * 2 + (c // 2 + 1))
                            if c == 0:
                                wait(act, y_ready, b.idx - 1)
                            a.activation(hid[:, b.par, c], ps_h[:, b.par, c // 2, (c % 2) * ROWS:(c % 2 + 1) * ROWS],
                                         ACT.Gelu, bias=b1_sb[:, bass.ds(e * HC + c, 1)]).then_inc(gelu_done, 1)
                    if b := at(2):
                        xs_hi(b)
                act.wait_ge(routed, 2)
                run_steps(act, NR, step, -1, 3, XRING)

                def step(at):
                    if b := at(-1):
                        act.wait_ge(zb_made, b.idx + 1)
                        wait(act, stored[b.slot], b.turn * 16)
                        for k in range(GT):
                            a.activation(zo[:, b.slot, k], z[:, b.slot, k], ACT.Identity, bias=zb[:, b.slot, k:k + 1],
                                         scale=zr[:, b.slot, k:k + 1]).then_inc(zo_made, 1)
                run_steps(act, NGRP, step, -1, 2, CRING)

            @block.vector
            def _(dve):
                v = nc.vector
                n = [0]

                def link(ins):
                    n[0] += 1
                    ins.then_inc(step_done, 1)
                    dve.wait_ge(step_done, n[0])

                v.tensor_copy(fill_row[:, :], next_row[:, :]).then_inc(fill_ready, 1)
                dve.wait_ge(made, 8)
                link(v.tensor_tensor(count_f[:, :], next_row[:, :], first_row[:, :], ALU.subtract))
                link(v.tensor_scalar(count_i[:, :], count_f[:, :], float(ROWS - 1), None, ALU.add))
                link(v.tensor_scalar(count_i[:, :], count_i[:, :], ROWS.bit_length() - 1, None, ALU.logical_shift_right))
                link(v.tensor_copy(tiles_f[:, :], count_i[:, :]))
                link(v.tensor_tensor_scan(out=tiles_end[:, :], data0=tiles_f[:, :], data1=zeros[:, :], initial=0.0,
                                          op0=ALU.add, op1=ALU.add))
                link(v.tensor_scalar(tiles_end[:, :], tiles_end[:, :], float(ROWS), None, ALU.mult))
                link(v.tensor_scalar(spare[:, :], tiles_f[:, :], -float(ROWS), float(room(N)), ALU.mult, ALU.add))
                link(v.tensor_tensor(passed[:, :, :], tile_row[:, :].unsqueeze(2).broadcast_to([P, NR, E]),
                                     tiles_end[:, :].unsqueeze(1).broadcast_to([P, NR, E]), ALU.is_ge))
                link(v.tensor_reduce(expert_f[:, :], passed[:, :, :], AX.X, ALU.add))
                link(v.tensor_tensor(passed[:, :, :], passed[:, :, :],
                                     spare[:, :].unsqueeze(1).broadcast_to([P, NR, E]), ALU.mult))
                link(v.tensor_reduce(row_f[:, :], passed[:, :, :], AX.X, ALU.add))
                link(v.tensor_tensor(row_f[:, :], row_f[:, :], tile_row[:, :], ALU.add))
                v.tensor_copy(row_of[:, :], row_f[:, :]).then_inc(routed, 1)
                v.tensor_scalar(expert_of[:, :], expert_f[:, :], float(E - 1), None, ALU.min).then_inc(routed, 1)

                cell = [P, NT, E]

                def over_e(a):
                    return a.unsqueeze(2).broadcast_to(cell)
                link(v.tensor_reduce(largest[:, :], logits[:, :, :], AX.X, ALU.max))
                v.tensor_tensor(prob[:, :, :], logits[:, :, :], over_e(largest[:, :]), ALU.subtract).then_inc(shifted, 1)
                dve.wait_ge(exp_taken, 1)
                link(v.tensor_reduce(total[:, :], prob[:, :, :], AX.X, ALU.add))
                link(v.reciprocal(total[:, :], total[:, :]))
                link(v.tensor_tensor(prob[:, :, :], prob[:, :, :], over_e(total[:, :]), ALU.mult))
                link(v.tensor_scalar(second[:, :, :], ranks[:, :, :], 1.0, None, ALU.is_equal))
                link(v.tensor_tensor(second[:, :, :], second[:, :, :], prob[:, :, :], ALU.mult))
                link(v.tensor_reduce(best[:, 0], prob[:, :, :], AX.X, ALU.max))
                link(v.tensor_reduce(best[:, 1], second[:, :, :], AX.X, ALU.add))
                link(v.tensor_tensor(total[:, :], best[:, 0], best[:, 1], ALU.add))
                link(v.tensor_scalar(total[:, :], total[:, :], 1e-9, None, ALU.add))
                link(v.reciprocal(total[:, :], total[:, :]))
                link(v.tensor_tensor(top_w[:, :, :], best[:, :, :], total[:, :].unsqueeze(1).broadcast_to([P, 2, NT]), ALU.mult))

                dve.wait_ge(w1_hi, 1)
                for e in range(E):
                    v.tensor_tensor(w1_split[:, e, 1], w1_raw[:, e], w1_split[:, e, 0], ALU.subtract).then_inc(w1_lo, 1)

                def step(at):
                    if b := at(2):
                        dve.wait_ge(xs_hi_made, b.idx + 1)
                        v.tensor_tensor(xs_split[:, 1], xs[:, b.slot, :, 0:C], xs_split[:, 0],
                                        ALU.subtract).then_inc(xs_lo_made, 1)
                    if b := at(-1):
                        e = dve.value_load(expert_of[0:1, bass.ds(b.idx, 1)], min_val=0, max_val=E - 1)
                        dve.wait_ge(y_ready, b.idx + 1)
                        wait(dve, y_out[b.slot], b.turn * (16 * RB))
                        bias = b2_sb[:, bass.ds(e, 1), :].broadcast_to([P, RB, C])
                        v.tensor_tensor(ys[:, b.slot], ps_y[:, b.par, 0:RB * C].rearrange("p (r c) -> p r c", r=RB),
                                        bias, ALU.add).then_inc(y_made, 1)
                dve.wait_ge(w_in, 16 * 4)
                run_steps(dve, NR, step, -1, 3, XRING)

                def combine(b):
                    dve.wait_ge(comb_in[b.slot], b.turn * 32 + 32)
                    wait(dve, zo_made, (b.idx - CRING + 1) * GT)
                    for k in range(GT):
                        v.scalar_tensor_tensor(out=z[:, b.slot, k], in0=y0[:, b.slot, k],
                                               scalar=top_w[:, 0, bass.ds(b.idx * GT + k, 1)],
                                               in1=x1_all[:, bass.ds(b.idx * GT + k, 1), :].rearrange("p a c -> p (a c)"),
                                               op0=ALU.mult, op1=ALU.add).then_inc(z_made, 1)
                    dve.wait_ge(z_made, b.idx * (2 * GT) + GT)
                    for k in range(GT):
                        v.scalar_tensor_tensor(out=z[:, b.slot, k], in0=y1[:, b.slot, k],
                                               scalar=top_w[:, 1, bass.ds(b.idx * GT + k, 1)], in1=z[:, b.slot, k],
                                               op0=ALU.mult, op1=ALU.add).then_inc(z_made, 1)
                    dve.wait_ge(z_made, b.idx * (2 * GT) + 2 * GT)
                    for k in range(GT):
                        v.bn_stats(zst[:, b.slot, k], z[:, b.slot, k]).then_inc(zst_made, 1)
                    blocks, = counts(dve, b.idx * GT + GT)
                    dve.wait_ge(made, 8)
                    dve.wait_ge(zst_made, blocks)
                    for k in range(GT):
                        v.bn_aggr(zmv[:, b.slot, k], zst[:, b.slot, k]).then_inc(zmv_made, 1)

                def shift(b):
                    dve.wait_ge(zr_made, b.idx + 1)
                    v.scalar_tensor_tensor(out=zb[:, b.slot], in0=zmv[:, b.slot, :, 0], scalar=-1.0, in1=zr[:, b.slot],
                                           op0=ALU.mult, op1=ALU.mult).then_inc(zb_made, 1)

                def step(at):
                    if b := at(0):
                        combine(b)
                    if b := at(-1):
                        shift(b)
                run_steps(dve, NGRP, step, -1, 2, CRING)

            @block.tensor
            def _(pe):
                t = nc.tensor
                pe.wait_ge(w1_hi, 1)
                pe.wait_ge(w1_lo, E)
                pe.wait_ge(w_in, 16 * 4)
                pe.wait_ge(routed, 2)

                def step(at):
                    if b := at(0):
                        e = pe.value_load(expert_of[0:1, bass.ds(b.idx, 1)], min_val=0, max_val=E - 1)
                        pe.wait_ge(xsT_copied, b.idx + 1)
                        for half in range(2):
                            for c in (2 * half, 2 * half + 1):
                                hi, lo = (w1_split[:, bass.ds(e, 1), k, c * P:(c + 1) * P].rearrange("p a n -> p (a n)")
                                          for k in range(2))
                                xh, xl = xsT[:, b.par, 0], xsT[:, b.par, 1]
                                out_ = ps_h[:, b.par, half, (c % 2) * ROWS:(c % 2 + 1) * ROWS]
                                t.matmul(out_, hi, xh, start=True, stop=False)
                                t.matmul(out_, hi, xl, start=False, stop=False)
                                ins = t.matmul(out_, lo, xh, start=False, stop=True)
                            ins.then_inc(hid_ready, 1)
                    if b := at(1):
                        pe.wait_ge(xs_lo_made, b.idx + 1)
                        wait(pe, xsT_copied, b.idx)
                        for k in range(2):
                            for r in range(RB):
                                ins = t.transpose(t16[:, (k * RB + r) * P:(k * RB + r + 1) * P], xs_split[:, k, r],
                                                  r_ident16[:, :])
                        ins.then_inc(xsT_ready, 1)
                    if b := at(-1):
                        e = pe.value_load(expert_of[0:1, bass.ds(b.idx, 1)], min_val=0, max_val=E - 1)
                        pe.wait_ge(gelu_done, b.idx * HC + HC)
                        wait(pe, y_made, b.idx - 1)
                        for r in range(RB):
                            for c in range(HC):
                                w = w2_sb[:, bass.ds(e, 1), c].rearrange("p a n -> p (a n)")
                                ins = t.matmul(ps_y[:, b.par, r * C:(r + 1) * C], hid[:, b.par, c, r * P:(r + 1) * P], w,
                                               start=(c == 0), stop=(c == HC - 1))
                        ins.then_inc(y_ready, 1)
                run_steps(pe, NR, step, -1, 3, XRING)


def program(nc, x, W_kv, g_kv, W_kdec, W_vdec, W_q, W_qdec, W_krope, W_qrope, W_o, gate_wT, w1, b1T, w2, b2,
            cos_t, sin_t, scratch, xs_dram, y_dram, out):
    NT = RB * x.shape[0]
    with (nc.sbuf_tensor("logits", [P, NT, E], F32) as logits, nc.sbuf_tensor("ranks", [P, NT, E], F32) as ranks,
          nc.sbuf_tensor("next_row", [P, E], F32) as next_row, nc.sbuf_tensor("x1_all", [P, NT, C], F32) as x1_all):
        attention(nc, logits, ranks, next_row, x1_all, x, W_kv, g_kv, W_kdec, W_vdec, W_q, W_qdec, W_krope, W_qrope, W_o,
                  gate_wT, cos_t, sin_t, xs_dram, scratch)
        experts(nc, logits, ranks, next_row, x1_all, xs_dram, y_dram, out, w1, b1T, w2, b2)


def rope_tables():
    inv_freq = 1.0 / 10000.0 ** (np.arange(0, DR, 2, dtype=np.float32) / DR)
    freqs = np.outer(np.arange(T, dtype=np.float32), inv_freq)
    angle = np.concatenate([freqs, freqs], -1)
    sign = np.where(np.arange(DR) < DR // 2, -1, 1).astype(np.float32)
    return [np.ascontiguousarray(np.repeat(a.T, 4, 0)).astype(np.float32)
            for a in (np.cos(angle), np.sin(angle) * sign)]


def kernel(**inputs):
    import concourse.bacc as bacc
    from concourse.bass_utils import run_bass_kernel_spmd

    nc = bacc.Bacc("TRN2", target_bir_lowering=False, num_devices=1)
    given = {name.split("_", 2)[2]: np.ascontiguousarray(a) for name, a in inputs.items()}
    arrays = {name: given[name] for name in
              ("x", "W_kv", "g_kv", "W_kdec", "W_vdec", "W_q", "W_qdec", "W_krope", "W_qrope", "W_o")}
    arrays["gate_wT"] = np.ascontiguousarray(given["gate_w"].T)
    arrays["w1"] = given["w1"]
    arrays["b1T"] = np.ascontiguousarray(given["b1"].reshape(E, HC, P).transpose(2, 0, 1)).reshape(P, E * HC)
    arrays["w2"], arrays["b2"] = given["w2"], given["b2"]
    arrays["cos_t"], arrays["sin_t"] = rope_tables()
    args = [nc.dram_tensor(name, a.shape, F32, kind="ExternalInput").ap() for name, a in arrays.items()]
    n = given["x"].shape[0] * T
    for name, shape, dtype in (("scratch", (RING, 2, 2, P, (NG + 1) * T), F16),
                               ("xs_dram", (E * (room(n) + ROWS), ROWLEN), F32),
                               ("y_dram", (2 * n + 2 * E * ROWS, C), F32)):
        args.append(nc.dram_tensor(name, shape, dtype, kind="Internal").ap())
    args.append(nc.dram_tensor("out", given["x"].shape, F32, kind="ExternalOutput").ap())
    program(nc, *args)
    return run_bass_kernel_spmd(nc, [arrays], core_ids=[0]).results[0]["out"]
```

```python
import numpy as np
from contextlib import ExitStack

import concourse.bass as bass
from concourse import mybir

ALU = mybir.AluOpType
ACT = mybir.ActivationFunctionType
AX = mybir.AxisListType
F32 = mybir.dt.float32
F16 = mybir.dt.float16
BF16 = mybir.dt.bfloat16
I32 = mybir.dt.int32

P = 128
C = 128
T = 256
RB = T // P
H = 16
DC = 8
DR = 32
QR = 64
KR = 32
NG = 4
SROWS = 3 * (DR + DC)
MROW = SROWS
MSCALE = 32768.0
RING = 3
UNITS = 12
STACK = 8 * 16
NWEIGHTS = 14
NCONSTS = 20


E = 8
HID = 512
HC = HID // P
ROWS = RB * P
ROWLEN = C + 4
RANKING = 9
PLACING = 5
GT = 4
CRING = 4
XRING = 12


def route_tiles(n):
    return (2 * n + E * (ROWS - 1)) // ROWS


def room(n):
    return n + ROWS


class Batch:

    def __init__(self, idx, turn, slot, par):
        self.idx, self.turn, self.slot, self.par = idx, turn, slot, par


def wait(eng, sem, value):
    if isinstance(value, int) and value <= 0:
        return
    eng.wait_ge(sem, value)


def counts(eng, *values):
    return [v if isinstance(v, int) else eng.to_reg(v) for v in values]


def run_steps(eng, nb, step, back=-4, ahead=4, ring=RING):
    def fixed(t):
        def at(d):
            b = t + d
            return Batch(b, b // ring, b % ring, b % 2) if 0 <= b < nb else None
        return at

    first = ring - back
    turns = (nb - ahead - first) // ring
    for t in range(-ahead, first):
        step(fixed(t))
    if turns > 0:
        with eng.Fori(0, turns) as i:
            for q in range(ring):
                def at(d):
                    k = first + q + d
                    return Batch(i * ring + k, i + k // ring, k % ring, k % 2)
                step(at)
    for t in range(first + max(turns, 0) * ring, nb - back):
        step(fixed(t))


def attention(nc, logits, ranks, next_row, x1_all, x, weights, tables, xs_dram, scratch):
    NB = x.shape[0]
    N = NB * T
    SCALE = float(DC + DR) ** -0.5

    with ExitStack() as ctx:
        def sb(name, shape, dt):
            return ctx.enter_context(nc.sbuf_tensor(name, shape, dt))

        def psum(name, shape, dt):
            return ctx.enter_context(nc.psum_tensor(name, shape, dt))

        def sem(name):
            return ctx.enter_context(nc.semaphore(name))

        def ring_sems(name):
            return [sem(f"{name}{i}") for i in range(RING)]

        ps_max = psum("ps_max", [P, 2, 512], F32)
        ps_exp = psum("ps_exp", [P, 2, 512], F32)
        ps_rope = psum("ps_rope", [P, 2, 512], F32)
        ps_proj = psum("ps_proj", [P, 512], F32)
        ps_out = psum("ps_out", [P, 512], F32)

        ident = sb("ident", [P, P], F32)
        ident16 = sb("ident16", [P, P], F16)
        identb = sb("identb", [P, P], BF16)
        causal = sb("causal", [P, 4, P], BF16)
        neghalf = sb("neghalf", [P, 2], F32)
        weights_sb = sb("weights_sb", list(weights.shape), F32)
        raws = weights_sb[:, 0:4 * P].rearrange("p (a n) -> p a n", a=4)
        raw = weights_sb[:, 4 * P:12 * P].rearrange("p (a n) -> p a n", a=2)
        gk = weights_sb[:, 12 * P:12 * P + 1]
        tables_sb = sb("tables_sb", list(tables.shape), F32)
        cos_sb, sin_sb, wo, gate_t = (tables_sb[:, a:b] for a, b in
                                      ((0, T), (T, 2 * T), (2 * T, 2 * T + C), (2 * T + C, 2 * T + C + E)))
        scaled = sb("scaled", [H, RING * T], F16)
        w_qkv = sb("w_qkv", [P, 2, QR + KR], F16)
        w_rope = sb("w_rope", [P, 2, 2, 2, NG, P], F16)
        w_qc = sb("w_qc", [P, 2, P], F16)
        w_kv_split = sb("w_kv_split", [P, 2, 2, P], F16)
        w_kv_stack = sb("w_kv_stack", [P, 2, P], F16)
        below = sb("below", [P, P], F16)
        ones = sb("ones", [P, P], F16)
        earlier = sb("earlier", [P, E, E], F32)
        ids = sb("ids", [P, 2, RB * NB], I32)

        x_in = sb("x_in", [P, RING, RB, C], F32)
        x_res = sb("x_res", [P, RING, RB, C], F32)
        x_split = sb("x_split", [P, 2, RB * C], F16)
        xT = sb("xT", [C, RING, 2, T], F16)
        ssq = sb("ssq", [P, RING, RB], F32)
        sq_junk = sb("sq_junk", [P, RB, KR], F32)
        ms = sb("ms", [P, RB], F32)
        rstd_kv = sb("rstd_kv", [P, RB], F32)
        qkv = sb("qkv", [P, RB, QR + KR], F32)
        kvn = sb("kvn", [P, RB, KR], F32)
        qkv_split = sb("qkv_split", [P, RB, 4, QR], F16)
        qkvT = sb("qkvT", [P, RING, 2, T], F16)
        rope_cos = sb("rope_cos", [P, 2, 512], F32)
        rope_sin = sb("rope_sin", [P, 2, 512], F32)
        rope_sum = sb("rope_sum", [P, 2, 512], F32)
        parts = sb("parts", [P, 2, 2, NG + 1, T], F16)
        k_stack = sb("k_stack", [P, RING, H, T], F16)
        q_stack = sb("q_stack", [P, RING, H, T], F16)
        v_aug = sb("v_aug", [P, RING, RB, H, 32], F32)
        row_max = sb("row_max", [P, RB, H], F32)
        neg_max = sb("neg_max", [P, RB, H], F16)
        neg_maxT = sb("neg_maxT", [H, RING, T], F16)
        p0 = sb("p0", [P, H, T], F32)
        p1 = sb("p1", [P, H, P], F32)
        oT = sb("oT", [P, NG, T], F32)
        rden = sb("rden", [P, RB * H], F32)
        on = sb("on", [P, RB, H, DC], F32)
        onT = sb("onT", [P, T], F32)
        resid = sb("resid", [P, RB, C], F32)
        stats = sb("stats", [P, RB, 6], F32)
        mean_var = sb("mean_var", [P, RB, 2], F32)
        rstd1 = sb("rstd1", [P, RB], F32)
        var_eps = sb("var_eps", [P, RB], F32)
        x1 = sb("x1", [P, RING, 2, RB, ROWLEN], F32)
        x1T = sb("x1T", [C, T], F32)
        score = sb("score", [P, RB, E], F32)
        above = sb("above", [P, RB, E, E], F32)
        no_less = sb("no_less", [P, RB, E, E], F32)
        rank = sb("rank", [P, RB, E], F32)
        pick = sb("pick", [P, 2, RB, E], F32)
        member = sb("member", [P, RB, E], F16)
        place = sb("place", [P, RB, E], F32)
        picked = sb("picked", [P, 2, RB, E], F32)
        row_f = sb("row_f", [P, 2, RB], F32)
        row_no = sb("row_no", [P, RING, 2, RB], I32)

        weights_in = sem("weights_in")
        tables_in = sem("tables_in")
        scale_row_in = sem("scale_row_in")
        consts_made = sem("consts_made")
        weights_made = sem("weights_made")
        dve_step = sem("dve_step")
        x_loaded = ring_sems("x_loaded")
        res_loaded = ring_sems("res_loaded")
        x_hi_made = sem("x_hi_made")
        x_lo_made = sem("x_lo_made")
        xT_ready = sem("xT_ready")
        xT_copied = sem("xT_copied")
        qkv_ready = sem("qkv_ready")
        qkv_read = sem("qkv_read")
        ms_made = sem("ms_made")
        rstd_kv_made = sem("rstd_kv_made")
        kvn_made = sem("kvn_made")
        kv_hi_made = sem("kv_hi_made")
        split_made = sem("split_made")
        splitT_ready = sem("splitT_ready")
        splitT_copied = sem("splitT_copied")
        content_ready = sem("content_ready")
        c_hi_made = sem("c_hi_made")
        c_lo_made = sem("c_lo_made")
        v_ready = sem("v_ready")
        v_copied = sem("v_copied")
        rope_a = sem("rope_a")
        rope_b = sem("rope_b")
        cos_done = sem("cos_done")
        sin_done = sem("sin_done")
        sum_done = sem("sum_done")
        r_hi_made = sem("r_hi_made")
        k_lo_made = sem("k_lo_made")
        q_lo_made = sem("q_lo_made")
        parked = [ring_sems("k_parked"), ring_sems("q_parked")]
        stacked = ring_sems("stacked")
        max_in = sem("max_in")
        max_done = sem("max_done")
        neg_max_made = sem("neg_max_made")
        neg_maxT_ready = sem("neg_maxT_ready")
        neg_maxT_copied = sem("neg_maxT_copied")
        max_row_in = ring_sems("max_row_in")
        exp_in = sem("exp_in")
        exp_done = sem("exp_done")
        masked = sem("masked")
        pv_done = sem("pv_done")
        oT_copied = sem("oT_copied")
        o_ready = sem("o_ready")
        rden_made = sem("rden_made")
        norm_done = sem("norm_done")
        onT_ready = sem("onT_ready")
        onT_copied = sem("onT_copied")
        attn_ready = sem("attn_ready")
        resid_made = sem("resid_made")
        stats_made = sem("stats_made")
        var_made = sem("var_made")
        eps_added = sem("eps_added")
        rstd1_made = sem("rstd1_made")
        x1_made = sem("x1_made")
        x1T_ready = sem("x1T_ready")
        x1T_copied = sem("x1T_copied")
        logits_ready = sem("logits_ready")
        logits_copied = sem("logits_copied")
        x1_copied = sem("x1_copied")
        x1_kept = ring_sems("x1_kept")
        ids_set = sem("ids_set")
        ranked = sem("ranked")
        counted = sem("counted")
        placed = sem("placed")
        scattered = ring_sems("scattered")

        f16_proj = ps_proj[:, :].bitcast(F16)

        def rows(b):
            def of(a):
                if isinstance(b.idx, int):
                    return a[b.idx].rearrange("(r p) c -> p r c", p=P)
                return a[bass.ds(b.idx, 1), :, :].rearrange("a (r p) c -> p (a r) c", p=P)
            return of

        with nc.Block() as block:
            def wait_parked(eng, b, side):
                if isinstance(b.idx, int):
                    wait(eng, parked[side][(b.idx - 1) % RING], 16 * ((b.idx - 1) // RING + 1) if b.idx else 0)
                else:
                    eng.wait_ge(parked[side][(b.slot - 1) % RING], (b.turn + (1 if b.slot else 0)) * 16)

            @block.sync
            def _(sp):
                sp.dma_start(weights_sb[:, :], weights).then_inc(weights_in, 16)
                sp.dma_start(tables_sb[:, :], tables).then_inc(tables_in, 16)
                sp.wait_ge(consts_made, 2)
                sp.dma_start(k_stack[MROW:MROW + 1].rearrange("a s h t -> a (s h t)").rearrange("a (h n) -> a h n", h=H),
                             scaled[:, :]).then_inc(scale_row_in, 16)

                def park(b, side):
                    dst = scratch[b.slot, side].rearrange("m p n -> p m n")
                    sp.dma_start(dst, parts[:, side].rearrange("p m g t -> p m (g t)")).then_inc(parked[side][b.slot], 16)

                def stack(b, side, tile, at, part, count):
                    src = scratch[b.slot, side, part:part + count].rearrange("m p n -> (m p) n")
                    rope = src[:, 0:NG * T].rearrange("(i j) n -> i j n", j=4)
                    sp.dma_start(tile[DR * at:DR * (at + count), b.slot].rearrange("p (j g) t -> p j (g t)", j=4),
                                 rope).then_inc(stacked[b.slot], 16)
                    first = 3 * DR + DC * at
                    sp.dma_start(tile[first:first + DC * count, b.slot],
                                 src[:, NG * T:].rearrange("(d h) n -> d h n", h=H)).then_inc(stacked[b.slot], 16)

                def step(at):
                    if b := at(4):
                        wait(sp, x_lo_made, b.idx - RING + 1)
                        sp.dma_start(x_in[:, b.slot], rows(b)(x)).then_inc(x_loaded[b.slot], 16)
                    if b := at(0):
                        wait(sp, resid_made, b.idx - RING + 1)
                        sp.dma_start(x_res[:, b.slot], rows(b)(x)).then_inc(res_loaded[b.slot], 16)
                    if b := at(0):
                        wait(sp, neg_maxT_copied, b.idx + 1)
                        sp.dma_start(q_stack[MROW:MROW + 1, b.slot], neg_maxT[:, b.slot]).then_inc(max_row_in[b.slot], 16)
                    if b := at(2):
                        wait(sp, r_hi_made, 4 * b.idx + 4)
                        wait(sp, q_lo_made, 2 * b.idx + 2)
                        park(b, 1)
                    if b := at(2):
                        wait(sp, exp_in, UNITS * (b.idx - RING + 1))
                        wait(sp, scale_row_in, 16)
                        for side in range(2):
                            wait(sp, parked[side][b.slot], 16 * (b.turn + 1))
                        stack(b, 0, k_stack, 0, 0, 2)
                        stack(b, 1, q_stack, 0, 0, 1)
                        stack(b, 1, q_stack, 1, 0, 2)
                        stack(b, 0, k_stack, 2, 0, 1)
                    if b := at(-2):
                        wait(sp, x1_made, 2 * b.idx + 2)
                        sp.dma_start(x1_all[:, bass.ds(b.idx * RB, RB)], x1[:, b.slot, 0, :, 0:C]).then_inc(x1_kept[b.slot], 16)
                    if b := at(3):
                        wait(sp, stacked[b.slot], STACK * b.turn)
                        wait(sp, r_hi_made, 4 * b.idx + 2)
                        wait(sp, k_lo_made, 2 * b.idx + 2)
                        wait(sp, c_lo_made, b.idx + 1)
                        park(b, 0)
                run_steps(sp, NB, step)
                for s in range(RING):
                    wait(sp, x1_kept[s], 16 * len(range(s, NB, RING)))

            @block.gpsimd
            def _(pool):
                g = nc.gpsimd
                n = [0]

                def made(ins):
                    ins.then_inc(consts_made, 1)
                    n[0] += 1
                made(g.memset(neghalf[:, :], -0.5))
                made(g.memset(scaled[:, :], MSCALE))
                pool.wait_ge(consts_made, n[0])
                for m in (ident, ident16, identb):
                    made(g.memset(m[:, :], 0.0))
                made(g.memset(causal[:, :, :], 0.0))
                made(g.memset(v_aug[:, :, :, :, :], 0.0))
                made(g.memset(below[:, :], 1.0))
                made(g.memset(ones[:, :], 1.0))
                made(g.memset(earlier[:, :, :], 1.0))
                made(g.memset(x1[:, :, :, :, C:ROWLEN].rearrange("p s k r a -> p (s k r) a"), 0.0))
                made(g.iota(next_row[:, :], pattern=[[room(N), E]], base=0, channel_multiplier=0,
                            allow_small_or_imprecise_dtypes=True))
                made(g.iota(ids[:, :, :], pattern=[[N, 2], [P, RB * NB]], base=0, channel_multiplier=1))
                pool.wait_ge(consts_made, n[0])
                for m in (ident, ident16, identb):
                    made(g.affine_select(out=m[:, :], in_=m[:, :], compare_op=ALU.not_equal, fill=1.0,
                                         base=0, pattern=[[-1, P]], channel_multiplier=1))
                made(g.affine_select(out=causal[:, :, :], in_=causal[:, :, :], compare_op=ALU.is_ge, fill=-1e30,
                                     base=0, pattern=[[0, 4], [-1, P]], channel_multiplier=1))
                made(g.affine_select(out=below[:, :], in_=below[:, :], compare_op=ALU.is_gt, fill=0.0, base=0,
                                     pattern=[[1, P]], channel_multiplier=-1))
                made(g.affine_select(out=earlier[:, :, :], in_=earlier[:, :, :], compare_op=ALU.is_gt, fill=0.0, base=0,
                                     pattern=[[1, E], [-1, E]], channel_multiplier=0))
                made(g.memset(v_aug[:, :, :, :, DC:DC + 1].rearrange("p s r h a -> p (s r h) a"), 1.0))
                assert n[0] == NCONSTS

                def rope_sum_of(b, n):
                    s = n % 2
                    wait(pool, sin_done, 4 * b.idx + n + 1)
                    wait(pool, r_hi_made, 4 * b.idx + n - 1)
                    if n < 2:
                        wait(pool, q_lo_made, 2 * b.idx - 1 + n)
                    else:
                        wait(pool, k_lo_made, 2 * b.idx + n - 1)
                    g.tensor_tensor(rope_sum[:, s], rope_cos[:, s], rope_sin[:, s], ALU.add).then_inc(sum_done, 1)

                def k_lo(b, n):
                    wait(pool, r_hi_made, 4 * b.idx + n + 1)
                    if n == 0:
                        wait_parked(pool, b, 0)
                    g.tensor_tensor(parts[:, 0, 1, 2 * n:2 * n + 2, :],
                                    rope_sum[:, n].rearrange("p (g t) -> p g t", g=2),
                                    parts[:, 0, 0, 2 * n:2 * n + 2, :], ALU.subtract).then_inc(k_lo_made, 1)

                def mask(b, a):
                    exps, = counts(pool, UNITS * b.idx + 3 * a + 3)
                    pool.wait_ge(consts_made, NCONSTS)
                    wait(pool, exp_done, exps)
                    for k, tile in enumerate((p0[:, 4 * a:4 * a + 4, 0:P], p1[:, 4 * a:4 * a + 4, :])):
                        ins = g.affine_select(out=tile, in_=tile, compare_op=ALU.is_ge, fill=fill0, base=0,
                                              pattern=[[0, 4], [1, P]], channel_multiplier=-1)
                        ins.then_inc(masked, 1)

                def rstd_kv_of(b):
                    reads, used = counts(pool, 4 * b.idx + 4, b.idx)
                    pool.wait_ge(consts_made, NCONSTS)
                    wait(pool, qkv_read, reads)
                    wait(pool, kvn_made, used)
                    g.tensor_scalar(ms[:, :], ssq[:, b.slot], 1.0 / KR, 1e-6, ALU.mult, ALU.add).then_inc(ms_made, 1)
                    wait(pool, ms_made, b.idx + 1)
                    g.tensor_tensor(rstd_kv[:, :], ms[:, :], neghalf[:, :], ALU.pow).then_inc(rstd_kv_made, 1)

                def x_lo(b):
                    wait(pool, x_hi_made, b.idx + 1)
                    g.tensor_tensor(x_split[:, 1], x_in[:, b.slot].rearrange("p r c -> p (r c)"), x_split[:, 0],
                                    ALU.subtract).then_inc(x_lo_made, 1)

                def rstd1_of(b):
                    variances, used = counts(pool, 2 * b.idx + 2, 2 * b.idx)
                    pool.wait_ge(consts_made, NCONSTS)
                    wait(pool, var_made, variances)
                    wait(pool, x1_made, used)
                    g.tensor_scalar(var_eps[:, :], mean_var[:, :, 1], 1e-5, None, ALU.add).then_inc(eps_added, 1)
                    wait(pool, eps_added, b.idx + 1)
                    g.tensor_tensor(rstd1[:, :], var_eps[:, :], neghalf[:, :], ALU.pow).then_inc(rstd1_made, 1)

                def scatter(b, k):
                    placings, copies = counts(pool, PLACING * b.idx + PLACING, b.idx + 1)
                    pool.wait_ge(consts_made, NCONSTS)
                    wait(pool, placed, placings)
                    wait(pool, x1_copied, copies)
                    for r in range(RB):
                        g.indirect_dma_start(
                            out=xs_dram, out_offset=bass.IndirectOffsetOnAxis(ap=row_no[:, b.slot, k, r:r + 1], axis=0),
                            in_=x1[:, b.slot, k, r], in_offset=None).then_inc(scattered[b.slot], 16)

                fill0 = g.to_reg(0.0)

                def step(at):
                    if b := at(3):
                        rstd_kv_of(b)
                    if b := at(-1):
                        mask(b, 2)
                    if b := at(-2):
                        rstd1_of(b)
                    if b := at(3):
                        rope_sum_of(b, 0)
                    if b := at(-1):
                        mask(b, 3)
                    if b := at(-4):
                        scatter(b, 0)
                    if b := at(3):
                        k_lo(b, 0)
                        rope_sum_of(b, 1)
                    if b := at(4):
                        x_lo(b)
                    if b := at(0):
                        mask(b, 0)
                    if b := at(3):
                        k_lo(b, 1)
                    if b := at(3):
                        rope_sum_of(b, 2)
                    if b := at(-4):
                        scatter(b, 1)
                    if b := at(0):
                        mask(b, 1)
                    if b := at(3):
                        rope_sum_of(b, 3)
                run_steps(pool, NB, step)
                for s in range(RING):
                    wait(pool, scattered[s], 64 * len(range(s, NB, RING)))

            @block.scalar
            def _(act):
                a = nc.scalar

                def copy(dst, src):
                    return a.activation(dst, src, ACT.Copy)

                def x_hi(b):
                    act.wait_ge(x_loaded[b.slot], b.turn * 16 + 16)
                    wait(act, xT_ready, b.idx)
                    copy(x_split[:, 0], x_in[:, b.slot].rearrange("p r c -> p (r c)")).then_inc(x_hi_made, 1)

                def xT_copy(b):
                    act.wait_ge(xT_ready, b.idx + 1)
                    copy(xT[:, b.slot].rearrange("p s t -> p (s t)"), f16_proj[:, 0:512]).then_inc(xT_copied, 1)

                def qkv_copy(b):
                    act.wait_ge(qkv_ready, b.idx + 1)
                    wait(act, split_made, 2 * b.idx)
                    pq = ps_proj[:, 0:RB * (QR + KR)].rearrange("p (r n) -> p r n", r=RB)
                    for r in range(RB):
                        a.activation(sq_junk[:, r], pq[:, r, QR:QR + KR], ACT.Square,
                                     accum_out=ssq[:, b.slot, r:r + 1]).then_inc(qkv_read, 1)
                    copy(qkv[:, :, :], pq).then_inc(qkv_read, 1)
                    wait(act, splitT_ready, b.idx)
                    copy(qkv_split[:, :, 0, :], pq[:, :, 0:QR]).then_inc(qkv_read, 1)

                def splitT_copy(b):
                    act.wait_ge(splitT_ready, b.idx + 1)
                    copy(qkvT[:, b.slot].rearrange("p s t -> p (s t)"), f16_proj[:, 0:512]).then_inc(splitT_copied, 1)

                def c_hi_of(b):
                    act.wait_ge(content_ready, b.idx + 1)
                    for side in range(2):
                        wait_parked(act, b, side)
                    copy(parts[:, :, 0, NG], ps_proj[:, :].rearrange("p (s t) -> p s t", s=2)).then_inc(c_hi_made, 1)

                def v_copy(b):
                    act.wait_ge(v_ready, b.idx + 1)
                    copy(v_aug[:, b.slot, :, :, 0:DC].rearrange("p r h d -> p (r h) d"),
                         ps_proj[:, 0:RB * P].rearrange("p (n d) -> p n d", d=DC)).then_inc(v_copied, 1)

                def r_hi_of(b, n):
                    act.wait_ge(sum_done, b.idx * 4 + n + 1)
                    if n % 2 == 0:
                        wait_parked(act, b, n // 2)
                    g = 2 * (n % 2)
                    copy(parts[:, n // 2, 0, g:g + 2, :].rearrange("p g t -> p (g t)"),
                         rope_sum[:, n % 2]).then_inc(r_hi_made, 1)

                def neg_maxT_copy(b):
                    act.wait_ge(neg_maxT_ready, b.idx + 1)
                    copy(neg_maxT[:, b.slot], f16_proj[0:H, 0:T]).then_inc(neg_maxT_copied, 1)

                def exp(b, u):
                    act.wait_ge(exp_in, b.idx * UNITS + u + 1)
                    grp, r = u // 3, u % 3
                    if r == 0:
                        wait(act, pv_done, 2 * b.idx - 1 + grp // 2)
                    if r < 2:
                        dst = p0[:, 4 * grp + 2 * r:4 * grp + 2 * r + 2, :].rearrange("p h t -> p (h t)")
                    else:
                        dst = p1[:, 4 * grp:4 * grp + 4, :].rearrange("p h t -> p (h t)")
                    a.activation(dst, ps_exp[:, u % 2], ACT.Exp, scale=SCALE).then_inc(exp_done, 1)

                def oT_copy(b, half):
                    act.wait_ge(pv_done, b.idx * 2 + half + 1)
                    if half == 0:
                        wait(act, o_ready, b.idx)
                    copy(oT[:, 2 * half:2 * half + 2, :].rearrange("p g t -> p (g t)"), ps_out[:, :]).then_inc(oT_copied, 1)

                def onT_copy(b):
                    act.wait_ge(onT_ready, b.idx + 1)
                    copy(onT[:, :], ps_out[:, 0:T]).then_inc(onT_copied, 1)

                def x1T_copy(b):
                    act.wait_ge(x1T_ready, b.idx + 1)
                    copy(x1T[:, :], ps_out[:, 0:T]).then_inc(x1T_copied, 1)

                def logits_copy(b):
                    act.wait_ge(logits_ready, b.idx + 1)
                    wait(act, ranked, RANKING * b.idx)
                    src = ps_out[:, 0:RB * E].rearrange("p (r e) -> p r e", r=RB)
                    copy(score[:, :, :], src).then_inc(logits_copied, 1)
                    copy(logits[:, bass.ds(b.idx * RB, RB), :], src).then_inc(logits_copied, 1)

                def x1_copy(b):
                    wait(act, x1_made, 2 * b.idx + 2)
                    wait(act, scattered[b.slot], 64 * b.turn)
                    copy(x1[:, b.slot, 1, :, 0:C], x1[:, b.slot, 0, :, 0:C]).then_inc(x1_copied, 1)

                def step(at):
                    for s in range(UNITS):
                        if s == 4 and (b := at(-1)):
                            oT_copy(b, 0)
                        if s == 11 and (b := at(-1)):
                            onT_copy(b)
                        if s == 6 and (b := at(-2)):
                            x1T_copy(b)
                        if s == 6 and (b := at(3)):
                            c_hi_of(b)
                        if s == 7 and (b := at(-2)):
                            logits_copy(b)
                            x1_copy(b)
                        if s == 8 and (b := at(-1)):
                            oT_copy(b, 1)
                        if b := at(-1 if s < 4 else 0):
                            exp(b, (s - 4) % UNITS)
                        if s == 1 and (b := at(0)):
                            neg_maxT_copy(b)
                        if s == 4 and (b := at(3)):
                            splitT_copy(b)
                        if s == 0 and (b := at(2)):
                            r_hi_of(b, 3)
                        if s == 4 and (b := at(3)):
                            r_hi_of(b, 0)
                        if s == 7 and (b := at(3)):
                            r_hi_of(b, 1)
                        if s == 5 and (b := at(4)):
                            x_hi(b)
                        if s == 9 and (b := at(2)):
                            v_copy(b)
                        if s == 10 and (b := at(4)):
                            xT_copy(b)
                        if s == 10 and (b := at(3)):
                            r_hi_of(b, 2)
                        if s == 11 and (b := at(4)):
                            qkv_copy(b)
                act.wait_ge(consts_made, NCONSTS)
                run_steps(act, NB, step)

            @block.vector
            def _(dve):
                v = nc.vector
                n = [0]

                def link(ins):
                    n[0] += 1
                    ins.then_inc(dve_step, 1)
                    dve.wait_ge(dve_step, n[0])

                def by_dim(a):
                    return a.rearrange("p (h d) -> p d h", h=H)

                dve.wait_ge(weights_in, 16)
                v.tensor_copy(w_qkv[:, 0], raws[:, 0, 0:QR + KR]).then_inc(dve_step, 1)
                n[0] += 1
                def rope_parts(m):
                    for side in range(2):
                        src = raw[:, side].rearrange("p (j g i) -> p g i j", j=4, g=NG)
                        for sw in range(2):
                            for half in range(2):
                                h2 = half ^ sw
                                yield (*(w_rope[:, side, sw, k].rearrange("p g (i j) -> p g i j", j=4)
                                         [:, :, 16 * half:16 * half + 16, :] for k in range(m + 1)),
                                       src[:, :, 16 * h2:16 * h2 + 16, :])
                for hi, src in rope_parts(0):
                    v.tensor_copy(hi, src).then_inc(dve_step, 1)
                    n[0] += 1
                v.tensor_copy(w_qc[:, 0].rearrange("p (d h) -> p d h", h=H), by_dim(raws[:, 1])).then_inc(dve_step, 1)
                n[0] += 1
                for k in range(2):
                    v.tensor_scalar(raws[:, 2 + k], raws[:, 2 + k], gk[:, 0:1], None, ALU.mult).then_inc(dve_step, 1)
                    n[0] += 1
                dve.wait_ge(dve_step, n[0])
                v.tensor_tensor(w_qkv[:, 1], raws[:, 0, 0:QR + KR], w_qkv[:, 0], ALU.subtract).then_inc(weights_made, 1)
                v.tensor_tensor(w_qc[:, 1].rearrange("p (d h) -> p d h", h=H), by_dim(raws[:, 1]),
                                w_qc[:, 0].rearrange("p (d h) -> p d h", h=H), ALU.subtract).then_inc(weights_made, 1)
                for hi, lo, src in rope_parts(1):
                    v.tensor_tensor(lo, src, hi, ALU.subtract).then_inc(weights_made, 1)

                def arranged(a, k, head_major):
                    if k:
                        return a
                    return by_dim(a) if head_major else a.rearrange("p (d h) -> p d h", h=H)

                for k in range(2):
                    link(v.tensor_copy(w_kv_split[:, k, 0], raws[:, 2 + k]))
                    link(v.tensor_tensor(w_kv_split[:, k, 1], raws[:, 2 + k], w_kv_split[:, k, 0], ALU.subtract))
                    v.tensor_copy(arranged(w_kv_stack[0:64, k], k, False), arranged(w_kv_split[0:64, k, 0], k, True)).then_inc(weights_made, 1)
                    v.tensor_copy(arranged(w_kv_stack[64:128, k], k, False), arranged(w_kv_split[64:128, k, 1], k, True)).then_inc(weights_made, 1)

                def max_of(b, u):
                    dve.wait_ge(max_in, b.idx * UNITS + u + 1)
                    grp, r = u // 3, u % 3
                    if u == 0:
                        wait(dve, neg_max_made, b.idx)
                    if r < 2:
                        h = 4 * grp + 2 * r
                        v.tensor_reduce(row_max[:, 1, h:h + 2], ps_max[:, u % 2].rearrange("p (h t) -> p h t", h=2),
                                        AX.X, ALU.max).then_inc(max_done, 1)
                    else:
                        v.tensor_reduce(row_max[:, 0, 4 * grp:4 * grp + 4],
                                        ps_max[:, u % 2].rearrange("p (h t) -> p h t", h=4),
                                        AX.X, ALU.max).then_inc(max_done, 1)

                def neg_max_of(b):
                    dve.wait_ge(max_done, b.idx * UNITS + UNITS)
                    wait(dve, neg_maxT_ready, b.idx)
                    v.tensor_scalar(neg_max[:, :, :].rearrange("p r h -> p (r h)"),
                                    row_max[:, :, :].rearrange("p r h -> p (r h)"), -1.0 / MSCALE, None,
                                    ALU.mult).then_inc(neg_max_made, 1)

                def split_q(b):
                    dve.wait_ge(qkv_read, b.idx * 4 + 4)
                    wait(dve, splitT_ready, b.idx)
                    v.tensor_tensor(qkv_split[:, :, 1, :], qkv[:, :, 0:QR], qkv_split[:, :, 0, :],
                                    ALU.subtract).then_inc(split_made, 1)

                def split_kv(b):
                    dve.wait_ge(rstd_kv_made, b.idx + 1)
                    v.tensor_tensor(kvn[:, :, :], qkv[:, :, QR:QR + KR],
                                    rstd_kv[:, :].unsqueeze(2).broadcast_to([P, RB, KR]),
                                    ALU.mult).then_inc(kvn_made, 1)
                    dve.wait_ge(kvn_made, b.idx + 1)
                    twice = kvn[:, :, :].unsqueeze(2).broadcast_to([P, RB, 2, KR])
                    v.tensor_copy(qkv_split[:, :, 2:4, 0:KR], twice).then_inc(kv_hi_made, 1)
                    dve.wait_ge(kv_hi_made, b.idx + 1)
                    v.tensor_tensor(qkv_split[:, :, 2:4, KR:2 * KR], twice, qkv_split[:, :, 2:4, 0:KR],
                                    ALU.subtract).then_inc(split_made, 1)

                def c_lo_of(b):
                    dve.wait_ge(c_hi_made, b.idx + 1)
                    v.tensor_tensor(parts[:, :, 1, NG], ps_proj[:, :].rearrange("p (s t) -> p s t", s=2),
                                    parts[:, :, 0, NG], ALU.subtract).then_inc(c_lo_made, 1)

                def rope(b, n):
                    s = n % 2
                    for sem_in, bank, table, dst, done in ((rope_a, 0, cos_sb, rope_cos, cos_done),
                                                           (rope_b, 1, sin_sb, rope_sin, sin_done)):
                        dve.wait_ge(sem_in, b.idx * 4 + n + 1)
                        wait(dve, sum_done, 4 * b.idx + n - 1)
                        v.tensor_tensor(dst[:, s].rearrange("p (g t) -> p g t", g=2),
                                        ps_rope[:, bank].rearrange("p (g t) -> p g t", g=2),
                                        table[:, :].unsqueeze(1).broadcast_to([P, 2, T]), ALU.mult).then_inc(done, 1)

                def q_lo(b, n):
                    dve.wait_ge(r_hi_made, b.idx * 4 + n + 3)
                    v.tensor_tensor(parts[:, 1, 1, 2 * n:2 * n + 2, :],
                                    rope_sum[:, n].rearrange("p (g t) -> p g t", g=2),
                                    parts[:, 1, 0, 2 * n:2 * n + 2, :], ALU.subtract).then_inc(q_lo_made, 1)

                def norm(b):
                    dve.wait_ge(o_ready, b.idx + 1)
                    o = ps_out[:, 0:RB * H * (DC + 1)].rearrange("p (n d) -> p n d", d=DC + 1)
                    v.reciprocal(rden[:, :].unsqueeze(2), o[:, :, DC:DC + 1]).then_inc(rden_made, 1)
                    dve.wait_ge(rden_made, b.idx + 1)
                    v.tensor_tensor(on[:, :, :, :].rearrange("p r h d -> p (r h) d"), o[:, :, 0:DC],
                                    rden[:, :].unsqueeze(2).broadcast_to([P, RB * H, DC]), ALU.mult).then_inc(norm_done, 1)

                def resid_of(b):
                    dve.wait_ge(attn_ready, b.idx + 1)
                    dve.wait_ge(res_loaded[b.slot], b.turn * 16 + 16)
                    v.tensor_tensor(resid[:, :, :].rearrange("p r c -> p (r c)"), ps_out[:, 0:RB * C],
                                    x_res[:, b.slot].rearrange("p r c -> p (r c)"), ALU.add).then_inc(resid_made, 1)
                    dve.wait_ge(resid_made, b.idx + 1)
                    for r in range(RB):
                        v.bn_stats(stats[:, r], resid[:, r]).then_inc(stats_made, 1)
                    halves, = counts(dve, b.idx * 2 + 2)
                    dve.wait_ge(weights_in, 16)
                    dve.wait_ge(stats_made, halves)
                    for r in range(RB):
                        v.bn_aggr(mean_var[:, r], stats[:, r]).then_inc(var_made, 1)

                def x1_of(b):
                    dve.wait_ge(rstd1_made, b.idx + 1)
                    wait(dve, x1_kept[b.slot], 16 * b.turn)
                    wait(dve, scattered[b.slot], 64 * b.turn)
                    v.tensor_copy(x1[:, b.slot, :, :, C].bitcast(I32), ids[:, :, bass.ds(b.idx * RB, RB)]).then_inc(ids_set, 1)
                    for r in range(RB):
                        v.tensor_scalar(x1[:, b.slot, 0, r, 0:C], resid[:, r], mean_var[:, r, 0:1], rstd1[:, r:r + 1],
                                        ALU.subtract, ALU.mult).then_inc(x1_made, 1)

                def compare(b):
                    dve.wait_ge(logits_copied, 2 * b.idx + 1)
                    wait(dve, ranked, RANKING * b.idx)
                    f, e = (score[:, :, :].unsqueeze(a).broadcast_to([P, RB, E, E]) for a in (2, 3))
                    v.tensor_tensor(above[:, :, :, :], f, e, ALU.is_gt).then_inc(ranked, 1)
                    v.tensor_tensor(no_less[:, :, :, :], f, e, ALU.is_ge).then_inc(ranked, 1)

                def break_ties(b):
                    wait(dve, ranked, RANKING * b.idx + 2)
                    v.tensor_tensor(no_less[:, :, :, :], no_less[:, :, :, :],
                                    earlier[:, :, :].unsqueeze(1).broadcast_to([P, RB, E, E]), ALU.mult).then_inc(ranked, 1)

                def rank_above(b):
                    wait(dve, ranked, RANKING * b.idx + 3)
                    v.tensor_tensor(above[:, :, :, :], above[:, :, :, :], no_less[:, :, :, :], ALU.max).then_inc(ranked, 1)

                def rank_of(b):
                    wait(dve, ranked, RANKING * b.idx + 4)
                    v.tensor_reduce(rank[:, :, :], above[:, :, :, :], AX.X, ALU.add).then_inc(ranked, 1)

                def picks(b):
                    wait(dve, ranked, RANKING * b.idx + 5)
                    wait(dve, counted, b.idx)
                    wait(dve, placed, PLACING * b.idx)
                    v.tensor_scalar(member[:, :, :], rank[:, :, :], 1.5, None, ALU.is_lt).then_inc(ranked, 1)
                    for k in range(2):
                        v.tensor_scalar(pick[:, k], rank[:, :, :], float(k), None, ALU.is_equal).then_inc(ranked, 1)
                    v.tensor_copy(ranks[:, bass.ds(b.idx * RB, RB), :], rank[:, :, :]).then_inc(ranked, 1)

                def place_of(b):
                    dve.wait_ge(counted, b.idx + 1)
                    wait(dve, placed, PLACING * b.idx)
                    v.tensor_tensor(place[:, :, :], ps_proj[:, 0:RB * E].rearrange("p (r e) -> p r e", r=RB),
                                    next_row[:, :].unsqueeze(1).broadcast_to([P, RB, E]), ALU.add).then_inc(placed, 1)
                    wait(dve, placed, PLACING * b.idx + 1)
                    v.tensor_tensor(next_row[:, :], ps_proj[:, RB * E:(RB + 1) * E], next_row[:, :], ALU.add).then_inc(placed, 1)

                def picked_of(b):
                    wait(dve, placed, PLACING * b.idx + 2)
                    wait(dve, ranked, RANKING * b.idx + RANKING)
                    v.tensor_tensor(picked[:, :, :, :], pick[:, :, :, :],
                                    place[:, :, :].unsqueeze(1).broadcast_to([P, 2, RB, E]), ALU.mult).then_inc(placed, 1)

                def row_no_of(b):
                    wait(dve, placed, PLACING * b.idx + 3)
                    wait(dve, scattered[b.slot], 64 * b.turn)
                    v.tensor_reduce(row_f[:, :, :], picked[:, :, :, :], AX.X, ALU.add).then_inc(placed, 1)
                    wait(dve, placed, PLACING * b.idx + 4)
                    v.tensor_copy(row_no[:, b.slot], row_f[:, :, :]).then_inc(placed, 1)

                def step(at):
                    for s in range(UNITS):
                        if b := at(1):
                            max_of(b, s)
                        if s == 8 and (b := at(-2)):
                            compare(b)
                        if s == 10 and (b := at(-2)):
                            break_ties(b)
                        if s == 11 and (b := at(-2)):
                            rank_above(b)
                        if s == 1 and (b := at(-3)):
                            rank_of(b)
                        if s == 3 and (b := at(-3)):
                            picks(b)
                        if s == 9 and (b := at(-1)):
                            norm(b)
                        if s == 8 and (b := at(-3)):
                            place_of(b)
                        if s == 9 and (b := at(-3)):
                            picked_of(b)
                        if s == 10 and (b := at(-3)):
                            row_no_of(b)
                        if s == 0 and (b := at(3)):
                            split_q(b)
                        if s == 1 and (b := at(3)):
                            split_kv(b)
                        if s == 1 and (b := at(-2)):
                            resid_of(b)
                        if s == 3 and (b := at(-2)):
                            x1_of(b)
                        if s == 1 and (b := at(3)):
                            rope(b, 0)
                        if s == 4 and (b := at(3)):
                            rope(b, 1)
                        if s == 6 and (b := at(3)):
                            c_lo_of(b)
                        if s == 7 and (b := at(3)):
                            rope(b, 2)
                        if s == 10 and (b := at(3)):
                            rope(b, 3)
                        if s == 11 and (b := at(1)):
                            neg_max_of(b)
                        if s == 11 and (b := at(3)):
                            q_lo(b, 0)
                        if s == 2 and (b := at(2)):
                            q_lo(b, 1)
                dve.wait_ge(tables_in, 16)
                run_steps(dve, NB, step)

            @block.tensor
            def _(pe):
                t = nc.tensor
                pe.wait_ge(consts_made, NCONSTS)
                pe.wait_ge(weights_made, NWEIGHTS)
                pe.wait_ge(tables_in, 16)

                def group(out, terms, sem_done=None):
                    for k, (l, r) in enumerate(terms):
                        ins = t.matmul(out, l, r, start=(k == 0), stop=(k == len(terms) - 1))
                    return ins

                def xT_of(b):
                    pe.wait_ge(x_lo_made, b.idx + 1)
                    wait(pe, v_copied, b.idx - 1)
                    if isinstance(b.idx, int) and b.idx < 2:
                        wait(pe, c_lo_made, b.idx)
                    for k in range(2):
                        for r in range(RB):
                            ins = t.transpose(f16_proj[:, (2 * k + r) * P:(2 * k + r + 1) * P],
                                              x_split[:, k, r * C:(r + 1) * C], ident16[:, :])
                    ins.then_inc(xT_ready, 1)

                def qkv_of(b):
                    pe.wait_ge(xT_copied, b.idx + 1)
                    for r in range(RB):
                        hi, lo = (xT[:, b.slot, k, r * P:(r + 1) * P] for k in range(2))
                        ins = group(ps_proj[:, r * (QR + KR):(r + 1) * (QR + KR)],
                                    [(hi, w_qkv[:, 0]), (lo, w_qkv[:, 0]), (hi, w_qkv[:, 1])])
                    ins.then_inc(qkv_ready, 1)

                def neg_maxT_of(b, more):
                    pe.wait_ge(neg_max_made, b.idx + 1)
                    if more:
                        pe.wait_ge(qkv_read, b.idx * 4 + 16)
                    else:
                        wait(pe, v_copied, min(b.idx + 2, NB))
                        wait(pe, placed, PLACING * (b.idx - 4) + 2)
                    for r in range(RB):
                        ins = t.transpose(f16_proj[0:H, r * P:(r + 1) * P], neg_max[:, r], ident16[:, :])
                    ins.then_inc(neg_maxT_ready, 1)

                def splitT_of(b):
                    pe.wait_ge(split_made, b.idx * 2 + 2)
                    pe.wait_ge(qkv_read, b.idx * 4 + 4)
                    wait(pe, neg_maxT_copied, b.idx - 2)
                    for k in range(2):
                        for r in range(RB):
                            ins = t.transpose(f16_proj[:, (2 * k + r) * P:(2 * k + r + 1) * P],
                                              qkv_split[:, r, 2 * k:2 * k + 2, :].rearrange("p a n -> p (a n)"),
                                              ident16[:, :])
                    ins.then_inc(splitT_ready, 1)

                def content(b):
                    pe.wait_ge(splitT_copied, b.idx + 1)
                    t.matmul(ps_proj[:, 0:T], w_kv_stack[:, 0], qkvT[:, b.slot, 1], start=True, stop=True)
                    group(ps_proj[:, T:2 * T], [(w_qc[:, k], qkvT[:, b.slot, 0]) for k in range(2)]).then_inc(content_ready, 1)

                def counts_of(b, at):
                    wait(pe, ranked, RANKING * b.idx + 6)
                    if at(3):
                        pe.wait_ge(c_lo_made, b.idx + 7)
                    else:
                        wait(pe, c_lo_made, NB)
                        wait(pe, v_copied, at(2).idx if at(2) else NB)
                        wait(pe, neg_maxT_copied, at(0).idx + 1 if at(0) else NB)
                        wait(pe, placed, PLACING * (b.idx - 1) + 2)
                    t.matmul(ps_proj[:, 0:E], below[:, :], member[:, 0], start=True, stop=True)
                    group(ps_proj[:, E:2 * E], [(below[:, :], member[:, 1]), (ones[:, :], member[:, 0])])
                    group(ps_proj[:, 2 * E:3 * E], [(ones[:, :], member[:, r]) for r in range(RB)]).then_inc(counted, 1)

                def v_of(b, more):
                    pe.wait_ge(c_lo_made, b.idx + (2 if more else 1))
                    wait(pe, placed, PLACING * (b.idx - 5) + 2)
                    for r in range(RB):
                        ins = t.matmul(ps_proj[:, r * P:(r + 1) * P], qkvT[:, b.slot, 1, r * P:(r + 1) * P],
                                       w_kv_stack[:, 1], start=True, stop=True)
                    ins.then_inc(v_ready, 1)

                def rope(b, n):
                    side = n // 2
                    if side:
                        pe.wait_ge(splitT_copied, b.idx + 1)
                    for sw, read, done in ((0, cos_done, rope_a), (1, sin_done, rope_b)):
                        wait(pe, read, 4 * b.idx + n)
                        for k in range(2):
                            g = 2 * (n % 2) + k
                            hi, lo = (w_rope[:, side, sw, m, g] for m in range(2))
                            if side == 0:
                                xh, xl = xT[:, b.slot, 0], xT[:, b.slot, 1]
                                terms = [(hi, xh), (hi, xl), (lo, xh)]
                            else:
                                terms = [(hi, qkvT[:, b.slot, 0]), (lo, qkvT[:, b.slot, 0])]
                            ins = group(ps_rope[:, sw, k * T:(k + 1) * T], terms)
                        ins.then_inc(done, 1)

                def scores_max(b, u):
                    if u == 0:
                        pe.wait_ge(stacked[b.slot], b.turn * STACK + STACK)
                    wait(pe, max_done, UNITS * b.idx + u - 1)
                    grp, r = u // 3, u % 3
                    bank = ps_max[:, u % 2]
                    ks, qs = k_stack[0:SROWS, b.slot], q_stack[0:SROWS, b.slot]
                    if r < 2:
                        for k in range(2):
                            h = 4 * grp + 2 * r + k
                            t.matmul(bank[:, k * T:(k + 1) * T], qs[:, h, P:T], ks[:, h, :], start=(k == 0), stop=False,
                                     skip_group_check=True)
                        ins = t.matmul(bank.rearrange("p (h t) -> p h t", h=2)[:, :, P:T], identb[:, :],
                                       causal[:, 0:2, :], start=False, stop=True, skip_group_check=True)
                    else:
                        for k in range(4):
                            h = 4 * grp + k
                            t.matmul(bank[:, k * P:(k + 1) * P], qs[:, h, 0:P], ks[:, h, 0:P], start=(k == 0), stop=False,
                                     skip_group_check=True)
                        ins = t.matmul(bank, identb[:, :], causal[:, :, :].rearrange("p a t -> p (a t)"),
                                       start=False, stop=True, skip_group_check=True)
                    ins.then_inc(max_in, 1)

                def scores_exp(b, u):
                    if u == 0:
                        pe.wait_ge(max_row_in[b.slot], b.turn * 16 + 16)
                    wait(pe, exp_done, UNITS * b.idx + u - 1)
                    grp, r = u // 3, u % 3
                    bank = ps_exp[:, u % 2]
                    ks, qs = k_stack[0:SROWS + 1, b.slot], q_stack[0:SROWS + 1, b.slot]
                    if r < 2:
                        for k in range(2):
                            h = 4 * grp + 2 * r + k
                            ins = t.matmul(bank[:, k * T:(k + 1) * T], ks[:, h, 0:P], qs[:, h, :], start=True, stop=True)
                    else:
                        for k in range(4):
                            h = 4 * grp + k
                            ins = t.matmul(bank[:, k * P:(k + 1) * P], ks[:, h, P:T], qs[:, h, P:T], start=True, stop=True)
                    ins.then_inc(exp_in, 1)

                def pv(b, half):
                    pe.wait_ge(masked, b.idx * 8 + 4 * half + 4)
                    if half == 0:
                        wait(pe, resid_made, b.idx)
                    else:
                        wait(pe, logits_copied, 2 * b.idx)
                        pe.wait_ge(oT_copied, b.idx * 2 + 1)
                    for k in range(2):
                        for j in range(4):
                            h = 4 * (2 * half + k) + j
                            out = ps_out[32 * j:32 * j + 32, k * T:(k + 1) * T]
                            t.matmul(out, v_aug[:, b.slot, 0, h], p0[:, h, :], start=True, stop=False, skip_group_check=True)
                        for j in range(4):
                            h = 4 * (2 * half + k) + j
                            out = ps_out[32 * j:32 * j + 32, k * T:(k + 1) * T]
                            ins = t.matmul(out[:, P:T], v_aug[:, b.slot, 1, h], p1[:, h, :], start=False, stop=True,
                                           skip_group_check=True)
                    ins.then_inc(pv_done, 1)

                def o_of(b):
                    pe.wait_ge(oT_copied, b.idx * 2 + 2)
                    taken = ident[:, :].rearrange("p (j n) -> p j n", n=32)[:, :, 0:DC + 1]
                    for r in range(RB):
                        for g in range(NG):
                            at_ = (r * NG + g) * 4 * (DC + 1)
                            ins = t.matmul(ps_out[:, at_:at_ + 4 * (DC + 1)], oT[:, g, r * P:(r + 1) * P], taken,
                                           start=True, stop=True)
                    ins.then_inc(o_ready, 1)

                def onT_of(b):
                    pe.wait_ge(norm_done, b.idx + 1)
                    for r in range(RB):
                        ins = t.transpose(ps_out[:, r * P:(r + 1) * P], on[:, r].rearrange("p h d -> p (h d)"), ident[:, :])
                    ins.then_inc(onT_ready, 1)

                def attn(b):
                    pe.wait_ge(onT_copied, b.idx + 1)
                    for r in range(RB):
                        ins = t.matmul(ps_out[:, r * C:(r + 1) * C], onT[:, r * P:(r + 1) * P], wo[:, :], start=True, stop=True)
                    ins.then_inc(attn_ready, 1)

                def x1T_of(b, more):
                    pe.wait_ge(x1_made, b.idx * 2 + 2)
                    if more:
                        pe.wait_ge(oT_copied, b.idx * 2 + 3)
                    for r in range(RB):
                        ins = t.transpose(ps_out[:, r * P:(r + 1) * P], x1[:, b.slot, 0, r, 0:C], ident[:, :])
                    ins.then_inc(x1T_ready, 1)

                def logits_of(b):
                    pe.wait_ge(x1T_copied, b.idx + 1)
                    for r in range(RB):
                        ins = t.matmul(ps_out[:, r * 8:(r + 1) * 8], x1T[:, r * P:(r + 1) * P], gate_t[:, :],
                                       start=True, stop=True)
                    ins.then_inc(logits_ready, 1)

                def step(at):
                    for s in range(UNITS):
                        if b := at(1):
                            scores_max(b, s)
                        if b := at(-1 if s < 4 else 0):
                            scores_exp(b, (s - 4) % UNITS)
                        if s == 0 and (b := at(-2)):
                            attn(b)
                        if s == 0 and (b := at(3)):
                            rope(b, 0)
                        if s == 1 and (b := at(0)):
                            neg_maxT_of(b, at(3) is not None)
                        if s == 4 and (b := at(3)):
                            splitT_of(b)
                        if s == 3 and (b := at(-1)):
                            pv(b, 0)
                        if s == 3 and (b := at(3)):
                            rope(b, 1)
                        if s == 5 and (b := at(3)):
                            content(b)
                        if s == 5 and (b := at(-2)):
                            x1T_of(b, at(-1) is not None)
                        if s == 6 and (b := at(-2)):
                            logits_of(b)
                        if s == 6 and (b := at(3)):
                            rope(b, 2)
                        if s == 7 and (b := at(-1)):
                            pv(b, 1)
                        if s == 8 and (b := at(-1)):
                            o_of(b)
                        if s == 7 and (b := at(-3)):
                            counts_of(b, at)
                        if s == 9 and (b := at(2)):
                            v_of(b, at(3) is not None)
                        if s == 9 and (b := at(3)):
                            rope(b, 3)
                        if s == 10 and (b := at(4)):
                            xT_of(b)
                        if s == 10 and (b := at(-1)):
                            onT_of(b)
                        if s == 11 and (b := at(4)):
                            qkv_of(b)
                run_steps(pe, NB, step)


def experts(nc, logits, ranks, next_row, x1_all, xs_dram, y_dram, out, w1, b1T, w2, b2):
    N = out.shape[0] * out.shape[1]
    NT = N // P
    NR = route_tiles(N)
    NGRP = NT // GT

    with ExitStack() as ctx:
        def sb(name, shape, dt):
            return ctx.enter_context(nc.sbuf_tensor(name, shape, dt))

        def psum(name, shape, dt):
            return ctx.enter_context(nc.psum_tensor(name, shape, dt))

        def sem(name):
            return ctx.enter_context(nc.semaphore(name))

        def ring_sems(name, n):
            return [sem(f"{name}{i}") for i in range(n)]

        w1_raw = sb("w1_raw", [C, E, HID], F32)
        w1_split = sb("w1_split", [C, E, 2, HID], F16)
        w2_sb = sb("w2_sb", [P, E, HC, C], F32)
        b1_sb = sb("b1_sb", [P, E * HC], F32)
        b2_sb = sb("b2_sb", [P, E, C], F32)
        r_ident16 = sb("r_ident16", [P, P], F16)
        tile_row = sb("tile_row", [P, NR], F32)
        first_row = sb("first_row", [P, E], F32)
        filling = sb("filling", [P, 2 * E * RB, ROWLEN], F32)
        r_neghalf = sb("r_neghalf", [P, GT], F32)
        zeros = sb("zeros", [P, E], F32)
        prob = sb("prob", [P, NT, E], F32)
        second = sb("second", [P, NT, E], F32)
        largest = sb("largest", [P, NT], F32)
        total = sb("total", [P, NT], F32)
        best = sb("best", [P, 2, NT], F32)
        top_w = sb("top_w", [P, 2, NT], F32)
        fill_row = sb("fill_row", [P, E], I32)
        count_f = sb("count_f", [P, E], F32)
        count_i = sb("count_i", [P, E], I32)
        tiles_f = sb("tiles_f", [P, E], F32)
        tiles_end = sb("tiles_end", [P, E], F32)
        spare = sb("spare", [P, E], F32)
        passed = sb("passed", [P, NR, E], F32)
        row_f = sb("row_tile_f", [P, NR], F32)
        row_of = sb("row_of", [P, NR], I32)
        expert_f = sb("expert_f", [P, NR], F32)
        expert_of = sb("expert_of", [P, NR], I32)
        xs = sb("xs", [P, XRING, RB, ROWLEN], F32)
        xs_split = sb("xs_split", [P, 2, RB, C], F16)
        xsT = sb("xsT", [C, 2, 2, ROWS], F16)
        hid = sb("hid", [P, 2, HC, ROWS], F32)
        ys = sb("ys", [P, XRING, RB, C], F32)
        y0 = sb("y0", [P, CRING, GT, C], F32)
        y1 = sb("y1", [P, CRING, GT, C], F32)
        z = sb("z", [P, CRING, GT, C], F32)
        zst = sb("zst", [P, CRING, GT, 6], F32)
        zmv = sb("zmv", [P, CRING, GT, 2], F32)
        zve = sb("zve", [P, CRING, GT], F32)
        zr = sb("zr", [P, CRING, GT], F32)
        zb = sb("zb", [P, CRING, GT], F32)
        zo = sb("zo", [P, CRING, GT, C], F32)

        ps_t = psum("ps_t", [P, 512], F32)
        ps_h = psum("ps_h", [P, 2, 2, 512], F32)
        ps_y = psum("ps_y", [P, 2, 512], F32)
        t16 = ps_t[:, :].bitcast(F16)

        biases_in = sem("biases_in")
        made = sem("made")
        half_filling = sem("half_filling")
        step_done = sem("step_done")
        shifted = sem("shifted")
        exp_taken = sem("exp_taken")
        routed = sem("routed")
        fill_ready = sem("fill_ready")
        filled = sem("filled")
        spare_filled = sem("spare_filled")
        w1_in = sem("w1_in")
        w2_in = sem("w2_in")
        w1_hi = sem("w1_hi")
        w1_lo = sem("w1_lo")
        xs_in = ring_sems("xs_in", XRING)
        xs_hi_made = sem("xs_hi_made")
        xs_lo_made = sem("xs_lo_made")
        xsT_ready = sem("xsT_ready")
        xsT_copied = sem("xsT_copied")
        hid_ready = sem("hid_ready")
        gelu_done = sem("gelu_done")
        y_ready = sem("y_ready")
        y_made = sem("y_made")
        y_out = ring_sems("y_out", XRING)
        comb_in = ring_sems("comb_in", CRING)
        weighed = sem("weighed")
        summed = sem("summed")
        z_made = sem("z_made")
        zst_made = sem("zst_made")
        zmv_made = sem("zmv_made")
        zve_made = sem("zve_made")
        zr_made = sem("zr_made")
        zb_made = sem("zb_made")
        zo_made = sem("zo_made")
        stored = ring_sems("stored", CRING)

        out_rows = out.rearrange("b t c -> (b t) c")

        def tiles_at(a, first, n):
            return a[bass.ds(first * P, n * P), :].rearrange("(n p) c -> p n c", p=P)

        def rows_at(a, row):
            return a[bass.ds(row, ROWS), :].rearrange("(r p) c -> p r c", p=P)

        def fill(eng, parity):
            eng.wait_ge(made, 8)
            eng.wait_ge(fill_ready, 1)
            for e in range(parity, E, 2):
                row = eng.value_load(fill_row[0:1, e:e + 1], min_val=0, max_val=E * room(N))
                eng.dma_start(rows_at(xs_dram, row), filling[:, e * RB:(e + 1) * RB]).then_inc(filled, 16)

        with nc.Block() as block:
            @block.sync
            def _(sp):
                fill(sp, 0)

                def step(at):
                    if (b := at(3)) and isinstance(b.idx, int) and b.idx == 3:
                        sp.dma_start(w2_sb[:, :, :, :], w2.rearrange("e (c p) d -> p e c d", p=P)).then_inc(w2_in, 16)
                    if (b := at(3)) and isinstance(b.idx, int) and b.idx == 5:
                        sp.dma_start(xs_dram[E * room(N):].rearrange("(r p) c -> p r c", p=P),
                                     filling[:, E * RB:]).then_inc(spare_filled, 16)
                    if b := at(3):
                        if not (isinstance(b.idx, int) and b.idx <= 5):
                            sp.wait_ge(spare_filled, 16)
                        wait(sp, y_out[b.slot], 16 * RB * b.turn)
                        row = sp.value_load(row_of[0:1, bass.ds(b.idx, 1)], min_val=0, max_val=E * (room(N) + ROWS) - ROWS)
                        sp.dma_start(xs[:, b.slot], rows_at(xs_dram, row)).then_inc(xs_in[b.slot], 16)
                sp.wait_ge(filled, 16 * E)
                sp.wait_ge(routed, 2)
                run_steps(sp, NR, step, -1, 3, XRING)
                for s in range(XRING):
                    sp.wait_ge(y_out[s], 16 * RB * len(range(s, NR, XRING)))

                def step(at):
                    if b := at(2):
                        wait(sp, z_made, (b.idx - CRING + 1) * GT)
                        for dst, first in ((y0, 0), (y1, N)):
                            sp.dma_start(dst[:, b.slot], tiles_at(y_dram[first:first + N], b.idx * GT, GT)
                                         ).then_inc(comb_in[b.slot], 16)
                    if b := at(-2):
                        wait(sp, zo_made, b.idx * GT + GT)
                        sp.dma_start(tiles_at(out_rows, b.idx * GT, GT), zo[:, b.slot]).then_inc(stored[b.slot], 16)
                run_steps(sp, NGRP, step, -2, 2, CRING)
                for s in range(CRING):
                    wait(sp, stored[s], 16 * len(range(s, NGRP, CRING)))

            @block.gpsimd
            def _(pool):
                g = nc.gpsimd
                g.memset(r_ident16[:, :], 0.0).then_inc(made, 1)
                g.memset(r_neghalf[:, :], -0.5).then_inc(made, 1)
                g.memset(zeros[:, :], 0.0).then_inc(made, 1)
                g.memset(filling[:, E * RB:], 0.0).then_inc(made, 1)
                g.iota(first_row[:, :], pattern=[[room(N), E]], base=0, channel_multiplier=0,
                       allow_small_or_imprecise_dtypes=True).then_inc(made, 1)
                g.iota(tile_row[:, :], pattern=[[ROWS, NR]], base=0, channel_multiplier=0,
                       allow_small_or_imprecise_dtypes=True).then_inc(made, 1)
                pool.wait_ge(made, 6)
                pool.wait_ge(half_filling, 1)
                g.iota(filling[:, :, C:C + 1].bitcast(I32), pattern=[[P, 2 * E * RB], [0, 1]], base=2 * N,
                       channel_multiplier=1).then_inc(made, 1)
                g.affine_select(out=r_ident16[:, :], in_=r_ident16[:, :], compare_op=ALU.not_equal, fill=1.0, base=0,
                                pattern=[[-1, P]], channel_multiplier=1).then_inc(made, 1)

                def step(at):
                    if b := at(-1):
                        products, = counts(pool, b.idx + 1)
                        pool.wait_ge(made, 8)
                        pool.wait_ge(y_made, products)
                        for r in range(RB):
                            g.indirect_dma_start(
                                out=y_dram,
                                out_offset=bass.IndirectOffsetOnAxis(ap=xs[:, b.slot, r, C:C + 1].bitcast(I32), axis=0),
                                in_=ys[:, b.slot, r], in_offset=None).then_inc(y_out[b.slot], 16)
                run_steps(pool, NR, step, -1, 3, XRING)

                def step(at):
                    if b := at(1):
                        pool.wait_ge(weighed, b.idx * GT + GT)
                        g.tensor_tensor(z[:, b.slot], z[:, b.slot], x1_all[:, bass.ds(b.idx * GT, GT)],
                                        ALU.add).then_inc(summed, 1)
                    if b := at(0):
                        variances, used = counts(pool, b.idx * GT + GT, b.idx - CRING + 1)
                        pool.wait_ge(made, 8)
                        pool.wait_ge(zmv_made, variances)
                        wait(pool, zr_made, used)
                        g.tensor_scalar(zve[:, b.slot], zmv[:, b.slot, :, 1], 1e-5, None, ALU.add).then_inc(zve_made, 1)
                        pool.wait_ge(zve_made, b.idx + 1)
                        wait(pool, zo_made, (b.idx - CRING + 1) * GT)
                        g.tensor_tensor(zr[:, b.slot], zve[:, b.slot], r_neghalf[:, :], ALU.pow).then_inc(zr_made, 1)
                run_steps(pool, NGRP, step, -2, 2, CRING)

            @block.scalar
            def _(act):
                a = nc.scalar
                for e in range(0, E, 2):
                    act.dma_start(w1_raw[:, e:e + 2], w1[e:e + 2].rearrange("e d h -> d e h")).then_inc(w1_in, 16)
                fill(act, 1)
                for dst, src in ((b1_sb[:, :], b1T),
                                 (b2_sb[:, :, :].rearrange("p e c -> p (e c)"),
                                  b2.rearrange("e c -> (e c)").partition_broadcast(P))):
                    act.dma_start(dst, src).then_inc(biases_in, 16)
                act.wait_ge(w1_in, 16 * (E // 2))
                for e in range(0, E, 2):
                    a.activation(w1_split[:, e:e + 2, 0], w1_raw[:, e:e + 2], ACT.Copy).then_inc(w1_hi, 1)

                def xs_hi(b):
                    act.wait_ge(xs_in[b.slot], b.turn * 16 + 16)
                    wait(act, xsT_ready, b.idx)
                    a.activation(xs_split[:, 0], xs[:, b.slot, :, 0:C], ACT.Copy).then_inc(xs_hi_made, 1)

                def step(at):
                    if b := at(1):
                        act.wait_ge(xsT_ready, b.idx + 1)
                        a.activation(xsT[:, b.par].rearrange("p s t -> p (s t)"), t16[:, 0:2 * ROWS],
                                     ACT.Copy).then_inc(xsT_copied, 1)
                    if b := at(0):
                        if isinstance(b.idx, int) and b.idx == 0:
                            act.wait_ge(biases_in, 16 * 2)
                        e = act.value_load(expert_of[0:1, bass.ds(b.idx, 1)], min_val=0, max_val=E - 1)
                        for c in range(HC):
                            if c % 2 == 0:
                                act.wait_ge(hid_ready, b.idx * 2 + (c // 2 + 1))
                            if c == 0:
                                wait(act, y_ready, b.idx - 1)
                            a.activation(hid[:, b.par, c], ps_h[:, b.par, c // 2, (c % 2) * ROWS:(c % 2 + 1) * ROWS],
                                         ACT.Gelu, bias=b1_sb[:, bass.ds(e * HC + c, 1)]).then_inc(gelu_done, 1)
                    if b := at(2):
                        xs_hi(b)
                        if isinstance(b.idx, int) and b.idx == 2:
                            act.wait_ge(shifted, 1)
                            a.activation(prob[:, :, :], prob[:, :, :], ACT.Exp).then_inc(exp_taken, 1)
                act.wait_ge(routed, 2)
                run_steps(act, NR, step, -1, 3, XRING)

                def step(at):
                    if b := at(1):
                        act.wait_ge(comb_in[b.slot], b.turn * 32 + 32)
                        wait(act, zo_made, (b.idx - CRING + 1) * GT)
                        for k in range(GT):
                            a.activation(z[:, b.slot, k], y0[:, b.slot, k], ACT.Copy,
                                         scale=top_w[:, 0, bass.ds(b.idx * GT + k, 1)]).then_inc(weighed, 1)
                    if b := at(-2):
                        act.wait_ge(zb_made, b.idx + 1)
                        wait(act, stored[b.slot], b.turn * 16)
                        for k in range(GT):
                            a.activation(zo[:, b.slot, k], z[:, b.slot, k], ACT.Identity, bias=zb[:, b.slot, k:k + 1],
                                         scale=zr[:, b.slot, k:k + 1]).then_inc(zo_made, 1)
                run_steps(act, NGRP, step, -2, 2, CRING)

            @block.vector
            def _(dve):
                v = nc.vector
                n = [0]

                def link(ins):
                    n[0] += 1
                    ins.then_inc(step_done, 1)
                    dve.wait_ge(step_done, n[0])

                v.memset(filling[:, 0:E * RB], 0.0).then_inc(half_filling, 1)
                v.tensor_copy(fill_row[:, :], next_row[:, :]).then_inc(fill_ready, 1)
                dve.wait_ge(made, 8)
                link(v.tensor_tensor(count_f[:, :], next_row[:, :], first_row[:, :], ALU.subtract))
                link(v.tensor_scalar(count_i[:, :], count_f[:, :], float(ROWS - 1), None, ALU.add))
                link(v.tensor_scalar(count_i[:, :], count_i[:, :], ROWS.bit_length() - 1, None, ALU.logical_shift_right))
                link(v.tensor_copy(tiles_f[:, :], count_i[:, :]))
                link(v.tensor_tensor_scan(out=tiles_end[:, :], data0=tiles_f[:, :], data1=zeros[:, :], initial=0.0,
                                          op0=ALU.add, op1=ALU.add))
                link(v.tensor_scalar(tiles_end[:, :], tiles_end[:, :], float(ROWS), None, ALU.mult))
                link(v.tensor_scalar(spare[:, :], tiles_f[:, :], -float(ROWS), float(room(N)), ALU.mult, ALU.add))
                link(v.tensor_tensor(passed[:, :, :], tile_row[:, :].unsqueeze(2).broadcast_to([P, NR, E]),
                                     tiles_end[:, :].unsqueeze(1).broadcast_to([P, NR, E]), ALU.is_ge))
                link(v.tensor_reduce(expert_f[:, :], passed[:, :, :], AX.X, ALU.add))
                link(v.tensor_tensor(passed[:, :, :], passed[:, :, :],
                                     spare[:, :].unsqueeze(1).broadcast_to([P, NR, E]), ALU.mult))
                link(v.tensor_reduce(row_f[:, :], passed[:, :, :], AX.X, ALU.add))
                link(v.tensor_tensor(row_f[:, :], row_f[:, :], tile_row[:, :], ALU.add))
                v.tensor_copy(row_of[:, :], row_f[:, :]).then_inc(routed, 1)
                v.tensor_scalar(expert_of[:, :], expert_f[:, :], float(E - 1), None, ALU.min).then_inc(routed, 1)

                cell = [P, NT, E]

                def over_e(a):
                    return a.unsqueeze(2).broadcast_to(cell)

                def expert_weights(part):
                    if part == 0:
                        link(v.tensor_reduce(largest[:, :], logits[:, :, :], AX.X, ALU.max))
                        v.tensor_tensor(prob[:, :, :], logits[:, :, :], over_e(largest[:, :]), ALU.subtract).then_inc(shifted, 1)
                    if part == 1:
                        dve.wait_ge(exp_taken, 1)
                        link(v.tensor_reduce(total[:, :], prob[:, :, :], AX.X, ALU.add))
                        link(v.reciprocal(total[:, :], total[:, :]))
                    if part == 2:
                        link(v.tensor_tensor(prob[:, :, :], prob[:, :, :], over_e(total[:, :]), ALU.mult))
                        link(v.tensor_scalar(second[:, :, :], ranks[:, :, :], 1.0, None, ALU.is_equal))
                    if part == 3:
                        link(v.tensor_tensor(second[:, :, :], second[:, :, :], prob[:, :, :], ALU.mult))
                        link(v.tensor_reduce(best[:, 0], prob[:, :, :], AX.X, ALU.max))
                    if part == 4:
                        link(v.tensor_reduce(best[:, 1], second[:, :, :], AX.X, ALU.add))
                        link(v.tensor_tensor(total[:, :], best[:, 0], best[:, 1], ALU.add))
                    if part == 5:
                        link(v.tensor_scalar(total[:, :], total[:, :], 1e-9, None, ALU.add))
                        link(v.reciprocal(total[:, :], total[:, :]))
                        link(v.tensor_tensor(top_w[:, :, :], best[:, :, :],
                                             total[:, :].unsqueeze(1).broadcast_to([P, 2, NT]), ALU.mult))

                for e in range(E):
                    dve.wait_ge(w1_hi, e // 2 + 1)
                    v.tensor_tensor(w1_split[:, e, 1], w1_raw[:, e], w1_split[:, e, 0], ALU.subtract).then_inc(w1_lo, 1)

                def step(at):
                    if b := at(2):
                        dve.wait_ge(xs_hi_made, b.idx + 1)
                        v.tensor_tensor(xs_split[:, 1], xs[:, b.slot, :, 0:C], xs_split[:, 0],
                                        ALU.subtract).then_inc(xs_lo_made, 1)
                        if isinstance(b.idx, int) and 2 <= b.idx < 8:
                            expert_weights(b.idx - 2)
                    if b := at(-1):
                        if isinstance(b.idx, int) and b.idx == 0:
                            dve.wait_ge(biases_in, 16 * 2)
                        e = dve.value_load(expert_of[0:1, bass.ds(b.idx, 1)], min_val=0, max_val=E - 1)
                        dve.wait_ge(y_ready, b.idx + 1)
                        wait(dve, y_out[b.slot], b.turn * (16 * RB))
                        bias = b2_sb[:, bass.ds(e, 1), :].broadcast_to([P, RB, C])
                        v.tensor_tensor(ys[:, b.slot], ps_y[:, b.par, 0:RB * C].rearrange("p (r c) -> p r c", r=RB),
                                        bias, ALU.add).then_inc(y_made, 1)
                run_steps(dve, NR, step, -1, 3, XRING)

                def combine(b):
                    dve.wait_ge(summed, b.idx + 1)
                    for k in range(GT):
                        v.scalar_tensor_tensor(out=z[:, b.slot, k], in0=y1[:, b.slot, k],
                                               scalar=top_w[:, 1, bass.ds(b.idx * GT + k, 1)], in1=z[:, b.slot, k],
                                               op0=ALU.mult, op1=ALU.add).then_inc(z_made, 1)
                    dve.wait_ge(z_made, b.idx * GT + GT)
                    for k in range(GT):
                        v.bn_stats(zst[:, b.slot, k], z[:, b.slot, k]).then_inc(zst_made, 1)
                    blocks, = counts(dve, b.idx * GT + GT)
                    dve.wait_ge(made, 8)
                    dve.wait_ge(zst_made, blocks)
                    for k in range(GT):
                        v.bn_aggr(zmv[:, b.slot, k], zst[:, b.slot, k]).then_inc(zmv_made, 1)

                def shift(b):
                    dve.wait_ge(zr_made, b.idx + 1)
                    v.scalar_tensor_tensor(out=zb[:, b.slot], in0=zmv[:, b.slot, :, 0], scalar=-1.0, in1=zr[:, b.slot],
                                           op0=ALU.mult, op1=ALU.mult).then_inc(zb_made, 1)

                def step(at):
                    if b := at(0):
                        combine(b)
                    if b := at(-1):
                        shift(b)
                run_steps(dve, NGRP, step, -2, 2, CRING)

            @block.tensor
            def _(pe):
                t = nc.tensor
                pe.wait_ge(w1_hi, E // 2)
                pe.wait_ge(w1_lo, E)
                pe.wait_ge(routed, 2)

                def step(at):
                    now, last = (pe.value_load(expert_of[0:1, bass.ds(at(d).idx, 1)], min_val=0, max_val=E - 1)
                                 if at(d) else None for d in (0, -1))
                    if b := at(0):
                        e = now
                        pe.wait_ge(xsT_copied, b.idx + 1)
                        for half in range(2):
                            for c in (2 * half, 2 * half + 1):
                                hi, lo = (w1_split[:, bass.ds(e, 1), k, c * P:(c + 1) * P].rearrange("p a n -> p (a n)")
                                          for k in range(2))
                                xh, xl = xsT[:, b.par, 0], xsT[:, b.par, 1]
                                out_ = ps_h[:, b.par, half, (c % 2) * ROWS:(c % 2 + 1) * ROWS]
                                t.matmul(out_, hi, xh, start=True, stop=False)
                                t.matmul(out_, hi, xl, start=False, stop=False)
                                ins = t.matmul(out_, lo, xh, start=False, stop=True)
                            ins.then_inc(hid_ready, 1)
                    if b := at(1):
                        pe.wait_ge(xs_lo_made, b.idx + 1)
                        wait(pe, xsT_copied, b.idx)
                        for k in range(2):
                            for r in range(RB):
                                ins = t.transpose(t16[:, (k * RB + r) * P:(k * RB + r + 1) * P], xs_split[:, k, r],
                                                  r_ident16[:, :])
                        ins.then_inc(xsT_ready, 1)
                    if b := at(-1):
                        e = last
                        if isinstance(b.idx, int) and b.idx == 0:
                            pe.wait_ge(w2_in, 16)
                        pe.wait_ge(gelu_done, b.idx * HC + HC)
                        wait(pe, y_made, b.idx - 1)
                        for r in range(RB):
                            for c in range(HC):
                                w = w2_sb[:, bass.ds(e, 1), c].rearrange("p a n -> p (a n)")
                                ins = t.matmul(ps_y[:, b.par, r * C:(r + 1) * C], hid[:, b.par, c, r * P:(r + 1) * P], w,
                                               start=(c == 0), stop=(c == HC - 1))
                        ins.then_inc(y_ready, 1)
                run_steps(pe, NR, step, -1, 3, XRING)


def program(nc, x, weights, tables, w1, b1T, w2, b2, scratch, xs_dram, y_dram, out):
    NT = RB * x.shape[0]
    with (nc.sbuf_tensor("logits", [P, NT, E], F32) as logits, nc.sbuf_tensor("ranks", [P, NT, E], F32) as ranks,
          nc.sbuf_tensor("next_row", [P, E], F32) as next_row, nc.sbuf_tensor("x1_all", [P, NT, C], F32) as x1_all):
        attention(nc, logits, ranks, next_row, x1_all, x, weights, tables, xs_dram, scratch)
        experts(nc, logits, ranks, next_row, x1_all, xs_dram, y_dram, out, w1, b1T, w2, b2)


def rope_tables():
    inv_freq = 1.0 / 10000.0 ** (np.arange(0, DR, 2, dtype=np.float32) / DR)
    freqs = np.outer(np.arange(T, dtype=np.float32), inv_freq)
    angle = np.concatenate([freqs, freqs], -1)
    sign = np.where(np.arange(DR) < DR // 2, -1, 1).astype(np.float32)
    return [np.ascontiguousarray(np.repeat(a.T, 4, 0)).astype(np.float32)
            for a in (np.cos(angle), np.sin(angle) * sign)]


def kernel(**inputs):
    import concourse.bacc as bacc
    from concourse.bass_utils import run_bass_kernel_spmd

    nc = bacc.Bacc("TRN2", target_bir_lowering=False, num_devices=1)
    given = {name.split("_", 2)[2]: np.ascontiguousarray(a) for name, a in inputs.items()}
    arrays = {"x": given["x"]}
    tall = [np.tile(given[name].reshape(given[name].shape[0], -1), (P // given[name].shape[0], 1))
            for name in ("W_q", "W_kv", "W_qdec", "W_kdec", "W_vdec", "W_krope", "W_qrope", "g_kv")]
    gap = np.zeros((P, P - QR - KR), np.float32)
    arrays["weights"] = np.concatenate(tall[:2] + [gap] + tall[2:], axis=1)
    arrays["tables"] = np.concatenate(rope_tables() + [given["W_o"], given["gate_w"].T], axis=1)
    arrays["w1"] = given["w1"]
    arrays["b1T"] = np.ascontiguousarray(given["b1"].reshape(E, HC, P).transpose(2, 0, 1)).reshape(P, E * HC)
    arrays["w2"], arrays["b2"] = given["w2"], given["b2"]
    args = [nc.dram_tensor(name, a.shape, F32, kind="ExternalInput").ap() for name, a in arrays.items()]
    n = given["x"].shape[0] * T
    for name, shape, dtype in (("scratch", (RING, 2, 2, P, (NG + 1) * T), F16),
                               ("xs_dram", (E * (room(n) + ROWS), ROWLEN), F32),
                               ("y_dram", (2 * n + 2 * E * ROWS, C), F32)):
        args.append(nc.dram_tensor(name, shape, dtype, kind="Internal").ap())
    args.append(nc.dram_tensor("out", given["x"].shape, F32, kind="ExternalOutput").ap())
    program(nc, *args)
    return run_bass_kernel_spmd(nc, [arrays], core_ids=[0]).results[0]["out"]
```
